# Optimizing a Trainium2 kernel written in Bass

```python
import numpy as np
import jax
import jax.numpy as jnp

def _softmax(x, axis=-1):
    return jax.nn.softmax(x, axis=axis)

def _gelu(x):
    return jax.nn.gelu(x, approximate=True)

def _silu(x):
    return jax.nn.silu(x)

def _sigmoid(x):
    return jax.nn.sigmoid(x)

def _layernorm(x, axis=-1, eps=1e-05):
    m = jnp.mean(x, axis=axis, keepdims=True)
    v = jnp.var(x, axis=axis, keepdims=True)
    return (x - m) / jnp.sqrt(v + eps)

def _scatter_add(tgt, idx, src, axis=0):
    return tgt.at[idx].add(src)

def _segment_sum(src, seg, n):
    return jax.ops.segment_sum(src, seg, n)
kernel_name = 'mk_flamingo_gated_d4_seqx_r8_c74a87'

def setup_inputs(seed: int=0):
    np.random.seed(seed)
    _w = jnp.asarray

    def _rec_inputs():
        import jax
        import jax.numpy as jnp
        _rk = jax.random.key(seed)
        x = -0.000929 + 1 * jax.random.normal(jax.random.fold_in(_rk, 1), (16, 128, 256), jnp.float32)
        _lenS = 128 - jax.random.randint(jax.random.fold_in(_rk, 7), (16,), 0, max(1, 128 // 4) + 1, jnp.int32)
        _lenS2 = 128 - jax.random.randint(jax.random.fold_in(_rk, 8), (16,), 0, max(1, 128 // 4) + 1, jnp.int32)
        _ctx_2048P = jax.random.normal(jax.random.fold_in(_rk, 11), (16, 16, 256), jnp.float32)
        _ctx_2048c = jax.random.dirichlet(jax.random.fold_in(_rk, 511), 0.3 * jnp.ones((16,), jnp.float32), (16, 128))
        _ctx_2048t = jnp.einsum('bsk,bkd->bsd', _ctx_2048c, _ctx_2048P)
        _ctx_2048t = _ctx_2048t * jax.lax.rsqrt(jnp.mean(jnp.square(_ctx_2048t)) + 1e-12) * 0.953939
        ctx_2048 = 2.81802e-05 + 1.00001 * (_ctx_2048t + 0.3 * jax.random.normal(jax.random.fold_in(_rk, 611), (16, 128, 256), jnp.float32))
        _validS = jnp.arange(128)[None, :] < _lenS[:, None]
        _validS2 = jnp.arange(128)[None, :] < _lenS2[:, None]
        _causal = jnp.tril(jnp.ones((128, 128), dtype=bool))
        mask_BxS2_bk0 = jnp.logical_not(jnp.broadcast_to(_validS2[:, :], (16, 128)))
        _g = jax.random.normal(jax.random.fold_in(_rk, 9001), (2, 4), jnp.float32)
        _g = jnp.sign(_g) * jnp.maximum(jnp.abs(_g), 1.0) + (_g == 0) * 1.0
        g_xattn = _g[0]
        g_ffn = _g[1]
        return (x, ctx_2048, mask_BxS2_bk0, g_xattn, g_ffn)
    x, ctx_2048, mask_BxS2_bk0, g_xattn, g_ffn = _rec_inputs()

    def _L0_xattn_setup():
        import jax, jax.numpy as jnp
        import numpy as np
        from jax import lax
        LN_EPS = 1e-05
        key = jax.random.key(seed)
        ks = jax.random.split(key, 8)
        B, S, T, D = (4, 128, 256, 256)
        scale = 0.02
        return {'Z': jax.random.normal(ks[0], (B, S, D), dtype=jnp.float32), 'kv': jax.random.normal(ks[1], (B, T, D), dtype=jnp.float32), 'decay': jnp.float32(0.9), 'W_in': jax.random.normal(ks[2], (D, D), dtype=jnp.float32) * scale, 'b_in': jnp.zeros((D,), dtype=jnp.float32), 'W_out': jax.random.normal(ks[3], (D, D), dtype=jnp.float32) * scale, 'b_out': jnp.zeros((D,), dtype=jnp.float32), 'gamma': jnp.ones((D,), dtype=jnp.float32), 'beta': jnp.zeros((D,), dtype=jnp.float32)}
    _L0_xattn_all = _L0_xattn_setup()
    _L0_xattn_in = {k: v for k, v in _L0_xattn_all.items() if k in ('decay', 'W_in', 'b_in', 'W_out', 'b_out', 'gamma', 'beta')}
    del _L0_xattn_all

    def _L0_ffn_setup():
        import jax, jax.numpy as jnp
        import numpy as np
        key = jax.random.key(seed)
        k1, k2, k3, k4 = jax.random.split(key, 4)
        B, S, D_IN, D_OUT = (4, 512, 256, 256)
        x = jax.random.normal(k1, (B, S, D_IN), dtype=jnp.float32)
        weight = jax.random.normal(k2, (D_OUT, D_IN), dtype=jnp.float32) * 0.02
        scale_weight = jax.random.uniform(k3, (D_OUT,), dtype=jnp.float32, minval=0.5, maxval=1.5)
        bias = jax.random.normal(k4, (D_OUT,), dtype=jnp.float32) * 0.02
        return {'x': x, 'weight': weight, 'scale_weight': scale_weight, 'bias': bias}
    _L0_ffn_all = _L0_ffn_setup()
    _L0_ffn_in = {k: v for k, v in _L0_ffn_all.items() if k in ('weight', 'scale_weight', 'bias')}
    del _L0_ffn_all

    def _L1_xattn_setup():
        import jax, jax.numpy as jnp
        import numpy as np
        key = jax.random.key(seed)
        k1, k2, k3 = jax.random.split(key, 3)
        B, S, D, M = (8, 256, 256, 128)
        hidden_states = jax.random.normal(k1, (B, S, D), dtype=jnp.float32)
        memory_tokens = jax.random.normal(k2, (B, M, D), dtype=jnp.float32)
        memory_mask = jax.random.randint(k3, (B, M), 0, 2).astype(jnp.bool_)
        return {'hidden_states': hidden_states, 'memory_tokens': memory_tokens, 'memory_mask': memory_mask}
    _L1_xattn_all = _L1_xattn_setup()
    _L1_xattn_in = {k: v for k, v in _L1_xattn_all.items() if k in ()}
    del _L1_xattn_all

    def _L1_ffn_setup():
        import jax, jax.numpy as jnp
        import numpy as np
        B, S, H = (2, 256, 256)
        E, K = (16, 4)
        I_MOE, I_SH = (176, 704)
        key = jax.random.key(seed)
        ks = jax.random.split(key, 9)

        def w(k, shape, fan_in):
            return jax.random.normal(k, shape, jnp.float32) * fan_in ** (-0.5)
        return {'hidden_states': jax.random.normal(ks[0], (B, S, H), jnp.float32), 'router_w': w(ks[1], (E, H), H), 'w_gate': w(ks[2], (E, H, I_MOE), H), 'w_up': w(ks[3], (E, H, I_MOE), H), 'w_down': w(ks[4], (E, I_MOE, H), I_MOE), 'sh_gate': w(ks[5], (H, I_SH), H), 'sh_up': w(ks[6], (H, I_SH), H), 'sh_down': w(ks[7], (I_SH, H), I_SH), 'sh_gate_w': w(ks[8], (H, 1), H)}
    _L1_ffn_all = _L1_ffn_setup()
    _L1_ffn_in = {k: v for k, v in _L1_ffn_all.items() if k in ('router_w', 'w_gate', 'w_up', 'w_down', 'sh_gate', 'sh_up', 'sh_down', 'sh_gate_w')}
    del _L1_ffn_all

    def _L2_xattn_setup():
        import jax, jax.numpy as jnp
        import numpy as np
        DIM = 256
        NHEADS = 32
        HEAD_DIM = DIM // NHEADS
        EPS = 1e-06

        def _rmsnorm(t):
            return t * jax.lax.rsqrt(jnp.mean(t * t, axis=-1, keepdims=True) + EPS)
        key = jax.random.key(seed)
        kx, kc, kq, kk, kv = jax.random.split(key, 5)
        x = jax.random.normal(kx, (2, 512, DIM), dtype=jnp.float32)
        context = jax.random.normal(kc, (2, 64, DIM), dtype=jnp.float32)
        std = 0.02
        Wq = jax.random.normal(kq, (DIM, DIM), dtype=jnp.float32) * std
        Wk = jax.random.normal(kk, (DIM, DIM), dtype=jnp.float32) * std
        Wv = jax.random.normal(kv, (DIM, DIM), dtype=jnp.float32) * std
        return {'x': x, 'context': context, 'Wq': Wq, 'Wk': Wk, 'Wv': Wv}
    _L2_xattn_all = _L2_xattn_setup()
    _L2_xattn_in = {k: v for k, v in _L2_xattn_all.items() if k in ('Wq', 'Wk', 'Wv')}
    del _L2_xattn_all

    def _L2_ffn_setup():
        import jax, jax.numpy as jnp
        import numpy as np
        B, S, D, F, E, SH, K = (2, 256, 256, 128, 16, 2, 2)

        def _experts_all(x, g, gb, w1, b1, w2, b2):
            y = jax.nn.gelu(jnp.einsum('bsd,edf->bsef', x, g) + gb, approximate=False)
            y = y * (jnp.einsum('bsd,edf->bsef', x, w1) + b1)
            return jnp.einsum('bsef,efd->bsed', y, w2) + b2
        key = jax.random.key(seed)
        ks = jax.random.split(key, 8)
        std = 0.02
        mk = lambda k, sh: jax.random.normal(k, sh, jnp.float32) * std
        return {'x': jax.random.normal(ks[0], (B, S, D), jnp.float32), 'wa': mk(ks[1], (D, E)), 'rg': mk(ks[2], (E, D, F)), 'rgb': jnp.zeros((E, F), jnp.float32), 'rw1': mk(ks[3], (E, D, F)), 'rb1': jnp.zeros((E, F), jnp.float32), 'rw2': mk(ks[4], (E, F, D)), 'rb2': jnp.zeros((E, D), jnp.float32), 'sg': mk(ks[5], (SH, D, F)), 'sgb': jnp.zeros((SH, F), jnp.float32), 'sw1': mk(ks[6], (SH, D, F)), 'sb1': jnp.zeros((SH, F), jnp.float32), 'sw2': mk(ks[7], (SH, F, D)), 'sb2': jnp.zeros((SH, D), jnp.float32)}
    _L2_ffn_all = _L2_ffn_setup()
    _L2_ffn_in = {k: v for k, v in _L2_ffn_all.items() if k in ('wa', 'rg', 'rgb', 'rw1', 'rb1', 'rw2', 'rb2', 'sg', 'sgb', 'sw1', 'sb1', 'sw2', 'sb2')}
    del _L2_ffn_all

    def _L3_xattn_setup():
        import jax, jax.numpy as jnp
        import numpy as np
        N_HEAD = 8
        key = jax.random.key(seed)
        k1, k2, k3 = jax.random.split(key, 3)
        B, D, L = (4, 128, 256)
        q = jax.random.normal(k1, (B, D, L), dtype=jnp.float32)
        k = jax.random.normal(k2, (B, D, L), dtype=jnp.float32)
        v = jax.random.normal(k3, (B, D, L), dtype=jnp.float32)
        gamma = jnp.ones((), dtype=jnp.float32)
        return {'q': q, 'k': k, 'v': v, 'gamma': gamma}
    _L3_xattn_all = _L3_xattn_setup()
    _L3_xattn_in = {k: v for k, v in _L3_xattn_all.items() if k in ('gamma',)}
    del _L3_xattn_all

    def _L3_ffn_setup():
        import jax, jax.numpy as jnp
        import numpy as np
        NUM_EXPERTS = 16
        TOP_K = 4
        N_GROUP = 4
        TOPK_GROUP = 2
        SCALING = 2.5

        def _route(x, gate_weight, expert_bias):
            logits = x @ gate_weight.T
            scores = jax.nn.sigmoid(logits)
            biased = scores + expert_bias[None, :]
            T = x.shape[0]
            gsz = NUM_EXPERTS // N_GROUP
            grp = biased.reshape(T, N_GROUP, gsz)
            top2, _ = jax.lax.top_k(grp, 2)
            group_scores = top2.sum(-1)
            _, gidx = jax.lax.top_k(group_scores, TOPK_GROUP)
            gmask = jax.nn.one_hot(gidx, N_GROUP, dtype=scores.dtype).sum(1)
            emask = jnp.repeat(gmask, gsz, axis=1)
            masked = jnp.where(emask > 0, biased, -jnp.inf)
            _, sel = jax.lax.top_k(masked, TOP_K)
            w = jnp.take_along_axis(scores, sel, axis=1)
            w = w / (w.sum(-1, keepdims=True) + 1e-20)
            return (w * SCALING, sel)

        def _moe(x, w, sel, gate_proj, up_proj, down_proj):
            cw = (jax.nn.one_hot(sel, NUM_EXPERTS, dtype=x.dtype) * w[..., None]).sum(1)

            def body(acc, inp):
                g, u, d, we = inp
                y = jax.nn.silu(x @ g.T) * (x @ u.T) @ d.T
                return (acc + we[:, None] * y, None)
            out, _ = jax.lax.scan(body, jnp.zeros_like(x), (gate_proj, up_proj, down_proj, cw.T))
            return out
        key = jax.random.key(seed)
        ks = jax.random.split(key, 9)
        B, S, H, I = (2, 128, 256, 128)
        w = lambda k, shape: jax.random.normal(k, shape, jnp.float32) * 0.02
        return {'hidden_states': jax.random.normal(ks[0], (B, S, H), jnp.float32), 'gate_weight': w(ks[1], (NUM_EXPERTS, H)), 'expert_bias': jnp.zeros((NUM_EXPERTS,), jnp.float32), 'gate_proj': w(ks[2], (NUM_EXPERTS, I, H)), 'up_proj': w(ks[3], (NUM_EXPERTS, I, H)), 'down_proj': w(ks[4], (NUM_EXPERTS, H, I)), 'shared_gate': w(ks[5], (I, H)), 'shared_up': w(ks[6], (I, H)), 'shared_down': w(ks[7], (H, I))}
    _L3_ffn_all = _L3_ffn_setup()
    _L3_ffn_in = {k: v for k, v in _L3_ffn_all.items() if k in ('gate_weight', 'expert_bias', 'gate_proj', 'up_proj', 'down_proj', 'shared_gate', 'shared_up', 'shared_down')}
    del _L3_ffn_all
    return {'x': x, 'ctx_2048': ctx_2048, 'mask_BxS2_bk0': mask_BxS2_bk0, 'g_xattn': g_xattn, 'g_ffn': g_ffn, 'L0_xattn_decay': _L0_xattn_in['decay'], 'L0_xattn_W_in': _L0_xattn_in['W_in'], 'L0_xattn_b_in': _L0_xattn_in['b_in'], 'L0_xattn_W_out': _L0_xattn_in['W_out'], 'L0_xattn_b_out': _L0_xattn_in['b_out'], 'L0_xattn_gamma': _L0_xattn_in['gamma'], 'L0_xattn_beta': _L0_xattn_in['beta'], 'L0_ffn_weight': _L0_ffn_in['weight'], 'L0_ffn_scale_weight': _L0_ffn_in['scale_weight'], 'L0_ffn_bias': _L0_ffn_in['bias'], 'L1_ffn_router_w': _L1_ffn_in['router_w'], 'L1_ffn_w_gate': _L1_ffn_in['w_gate'], 'L1_ffn_w_up': _L1_ffn_in['w_up'], 'L1_ffn_w_down': _L1_ffn_in['w_down'], 'L1_ffn_sh_gate': _L1_ffn_in['sh_gate'], 'L1_ffn_sh_up': _L1_ffn_in['sh_up'], 'L1_ffn_sh_down': _L1_ffn_in['sh_down'], 'L1_ffn_sh_gate_w': _L1_ffn_in['sh_gate_w'], 'L2_xattn_Wq': _L2_xattn_in['Wq'], 'L2_xattn_Wk': _L2_xattn_in['Wk'], 'L2_xattn_Wv': _L2_xattn_in['Wv'], 'L2_ffn_wa': _L2_ffn_in['wa'], 'L2_ffn_rg': _L2_ffn_in['rg'], 'L2_ffn_rgb': _L2_ffn_in['rgb'], 'L2_ffn_rw1': _L2_ffn_in['rw1'], 'L2_ffn_rb1': _L2_ffn_in['rb1'], 'L2_ffn_rw2': _L2_ffn_in['rw2'], 'L2_ffn_rb2': _L2_ffn_in['rb2'], 'L2_ffn_sg': _L2_ffn_in['sg'], 'L2_ffn_sgb': _L2_ffn_in['sgb'], 'L2_ffn_sw1': _L2_ffn_in['sw1'], 'L2_ffn_sb1': _L2_ffn_in['sb1'], 'L2_ffn_sw2': _L2_ffn_in['sw2'], 'L2_ffn_sb2': _L2_ffn_in['sb2'], 'L3_xattn_gamma': _L3_xattn_in['gamma'], 'L3_ffn_gate_weight': _L3_ffn_in['gate_weight'], 'L3_ffn_expert_bias': _L3_ffn_in['expert_bias'], 'L3_ffn_gate_proj': _L3_ffn_in['gate_proj'], 'L3_ffn_up_proj': _L3_ffn_in['up_proj'], 'L3_ffn_down_proj': _L3_ffn_in['down_proj'], 'L3_ffn_shared_gate': _L3_ffn_in['shared_gate'], 'L3_ffn_shared_up': _L3_ffn_in['shared_up'], 'L3_ffn_shared_down': _L3_ffn_in['shared_down']}

def reference(x, ctx_2048, mask_BxS2_bk0, g_xattn, g_ffn, L0_xattn_decay, L0_xattn_W_in, L0_xattn_b_in, L0_xattn_W_out, L0_xattn_b_out, L0_xattn_gamma, L0_xattn_beta, L0_ffn_weight, L0_ffn_scale_weight, L0_ffn_bias, L1_ffn_router_w, L1_ffn_w_gate, L1_ffn_w_up, L1_ffn_w_down, L1_ffn_sh_gate, L1_ffn_sh_up, L1_ffn_sh_down, L1_ffn_sh_gate_w, L2_xattn_Wq, L2_xattn_Wk, L2_xattn_Wv, L2_ffn_wa, L2_ffn_rg, L2_ffn_rgb, L2_ffn_rw1, L2_ffn_rb1, L2_ffn_rw2, L2_ffn_rb2, L2_ffn_sg, L2_ffn_sgb, L2_ffn_sw1, L2_ffn_sb1, L2_ffn_sw2, L2_ffn_sb2, L3_xattn_gamma, L3_ffn_gate_weight, L3_ffn_expert_bias, L3_ffn_gate_proj, L3_ffn_up_proj, L3_ffn_down_proj, L3_ffn_shared_gate, L3_ffn_shared_up, L3_ffn_shared_down):
    import jax
    import jax.numpy as jnp

    def _L0_xattn_ref(Z, kv, decay, W_in, b_in, W_out, b_out, gamma, beta):
        import jax, jax.numpy as jnp
        import numpy as np
        from jax import lax
        LN_EPS = 1e-05
        B, T, D = kv.shape
        K = jax.nn.sigmoid(decay)
        x = jnp.einsum('btd,ed->bte', kv, W_in) + b_in

        def scan_fn(s, xt):
            s = K * s + xt
            return (s, s)
        s0 = jnp.zeros((B, D), dtype=kv.dtype)
        _, states = lax.scan(scan_fn, s0, jnp.swapaxes(x, 0, 1))
        states = jnp.swapaxes(states, 0, 1)
        proj = jnp.einsum('btd,ed->bte', states, W_out) + b_out
        summary = jnp.mean(proj, axis=1, keepdims=True)
        y = Z + summary
        mu = jnp.mean(y, axis=-1, keepdims=True)
        var = jnp.mean((y - mu) ** 2, axis=-1, keepdims=True)
        return (y - mu) / jnp.sqrt(var + LN_EPS) * gamma + beta

    def _L0_ffn_ref(x, weight, scale_weight, bias):
        import jax, jax.numpy as jnp
        import numpy as np
        w = weight * scale_weight[:, None]
        out = jnp.einsum('bsi,oi->bso', x, w) + bias
        return out

    def _L1_xattn_ref(hidden_states, memory_tokens, memory_mask):
        import jax, jax.numpy as jnp
        import numpy as np
        B, S, D = hidden_states.shape
        scale = 1.0 / jnp.sqrt(jnp.asarray(D, hidden_states.dtype))
        scores = jnp.einsum('bsd,bmd->bsm', hidden_states, memory_tokens) * scale
        neg_inf = jnp.asarray(-1e+30, scores.dtype)
        scores = jnp.where(memory_mask[:, None, :], scores, neg_inf)
        attn = jax.nn.softmax(scores, axis=-1)
        readout = jnp.einsum('bsm,bmd->bsd', attn, memory_tokens)
        valid_b = jnp.any(memory_mask, axis=-1)
        out = jnp.where(valid_b[:, None, None], readout, jnp.zeros_like(readout))
        return out

    def _L1_ffn_ref(hidden_states, router_w, w_gate, w_up, w_down, sh_gate, sh_up, sh_down, sh_gate_w):
        import jax, jax.numpy as jnp
        import numpy as np
        B, S, H = (2, 256, 256)
        E, K = (16, 4)
        I_MOE, I_SH = (176, 704)
        orig = hidden_states.shape
        h = hidden_states.reshape(-1, orig[-1])
        N = h.shape[0]
        logits = h @ router_w.T
        probs = jax.nn.softmax(logits.astype(jnp.float32), axis=-1)
        top_vals, top_idx = jax.lax.top_k(probs, K)
        top_vals = top_vals / jnp.maximum(top_vals.sum(-1, keepdims=True), 1e-09)
        top_vals = top_vals.astype(h.dtype)
        comb = jnp.zeros((N, E), h.dtype).at[jnp.arange(N)[:, None], top_idx].add(top_vals)
        g = jnp.einsum('nh,ehi->eni', h, w_gate)
        u = jnp.einsum('nh,ehi->eni', h, w_up)
        y = jnp.einsum('eni,eih->enh', jax.nn.silu(g) * u, w_down)
        routed = jnp.einsum('enh,ne->nh', y, comb)
        shared = jax.nn.silu(h @ sh_gate) * (h @ sh_up) @ sh_down
        sg = jax.nn.sigmoid(h @ sh_gate_w)
        return (routed + sg * shared).reshape(orig)

    def _L2_xattn_ref(x, context, Wq, Wk, Wv):
        import jax, jax.numpy as jnp
        import numpy as np
        DIM = 256
        NHEADS = 32
        HEAD_DIM = DIM // NHEADS
        EPS = 1e-06

        def _rmsnorm(t):
            return t * jax.lax.rsqrt(jnp.mean(t * t, axis=-1, keepdims=True) + EPS)
        b, n, _ = x.shape
        m = context.shape[1]
        q = x @ Wq.T
        k_raw = context @ Wk.T
        v_raw = context @ Wv.T
        q = q.reshape(b, n, NHEADS, HEAD_DIM).transpose(0, 2, 1, 3)
        kv = jnp.concatenate([k_raw, v_raw], axis=-1)
        kv = kv.reshape(b, m, NHEADS, HEAD_DIM, 2)
        k = kv[..., 0].transpose(0, 2, 1, 3)
        v = kv[..., 1].transpose(0, 2, 1, 3)
        q = _rmsnorm(q)
        k = _rmsnorm(k)
        scale = HEAD_DIM ** (-0.5)
        scores = jnp.einsum('bhnd,bhmd->bhnm', q, k) * scale
        attn = jax.nn.softmax(scores, axis=-1)
        out = jnp.einsum('bhnm,bhmd->bhnd', attn, v)
        return out.transpose(0, 2, 1, 3).reshape(b, n, NHEADS * HEAD_DIM)

    def _L2_ffn_ref(x, wa, rg, rgb, rw1, rb1, rw2, rb2, sg, sgb, sw1, sb1, sw2, sb2):
        import jax, jax.numpy as jnp
        import numpy as np
        B, S, D, F, E, SH, K = (2, 256, 256, 128, 16, 2, 2)

        def _experts_all(x, g, gb, w1, b1, w2, b2):
            y = jax.nn.gelu(jnp.einsum('bsd,edf->bsef', x, g) + gb, approximate=False)
            y = y * (jnp.einsum('bsd,edf->bsef', x, w1) + b1)
            return jnp.einsum('bsef,efd->bsed', y, w2) + b2
        aff = jax.nn.sigmoid(jnp.einsum('bsd,de->bse', x, wa))
        topk_p, topk_i = jax.lax.top_k(aff, K)
        topk_p = topk_p / jnp.sum(topk_p, axis=-1, keepdims=True)
        combine = jnp.sum(jax.nn.one_hot(topk_i, E, dtype=x.dtype) * topk_p[..., None], axis=2)
        routed = jnp.einsum('bsed,bse->bsd', _experts_all(x, rg, rgb, rw1, rb1, rw2, rb2), combine)
        shared = jnp.sum(_experts_all(x, sg, sgb, sw1, sb1, sw2, sb2), axis=2)
        return x + shared + routed

    def _L3_xattn_ref(q, k, v, gamma):
        import jax, jax.numpy as jnp
        import numpy as np
        N_HEAD = 8
        B, Dq, Lq = q.shape
        Dv, Lk = (v.shape[-2], v.shape[-1])
        h = N_HEAD
        dq = Dq // h
        dv = Dv // h
        qh = q.reshape(B, h, dq, Lq)
        kh = k.reshape(B, h, dq, Lk)
        vh = v.reshape(B, h, dv, Lk)
        scale = 1.0 / jnp.sqrt(jnp.asarray(dq, dtype=q.dtype))
        qk = jnp.einsum('bhdq,bhdl->bhql', qh, kh) * scale
        sm = jax.nn.softmax(qk, axis=-1)
        ret = jnp.einsum('bhql,bhdl->bhdq', sm, vh)
        ret = ret.reshape(B, Dv, Lq)
        return gamma * ret

    def _L3_ffn_ref(hidden_states, gate_weight, expert_bias, gate_proj, up_proj, down_proj, shared_gate, shared_up, shared_down):
        import jax, jax.numpy as jnp
        import numpy as np
        NUM_EXPERTS = 16
        TOP_K = 4
        N_GROUP = 4
        TOPK_GROUP = 2
        SCALING = 2.5

        def _route(x, gate_weight, expert_bias):
            logits = x @ gate_weight.T
            scores = jax.nn.sigmoid(logits)
            biased = scores + expert_bias[None, :]
            T = x.shape[0]
            gsz = NUM_EXPERTS // N_GROUP
            grp = biased.reshape(T, N_GROUP, gsz)
            top2, _ = jax.lax.top_k(grp, 2)
            group_scores = top2.sum(-1)
            _, gidx = jax.lax.top_k(group_scores, TOPK_GROUP)
            gmask = jax.nn.one_hot(gidx, N_GROUP, dtype=scores.dtype).sum(1)
            emask = jnp.repeat(gmask, gsz, axis=1)
            masked = jnp.where(emask > 0, biased, -jnp.inf)
            _, sel = jax.lax.top_k(masked, TOP_K)
            w = jnp.take_along_axis(scores, sel, axis=1)
            w = w / (w.sum(-1, keepdims=True) + 1e-20)
            return (w * SCALING, sel)

        def _moe(x, w, sel, gate_proj, up_proj, down_proj):
            cw = (jax.nn.one_hot(sel, NUM_EXPERTS, dtype=x.dtype) * w[..., None]).sum(1)

            def body(acc, inp):
                g, u, d, we = inp
                y = jax.nn.silu(x @ g.T) * (x @ u.T) @ d.T
                return (acc + we[:, None] * y, None)
            out, _ = jax.lax.scan(body, jnp.zeros_like(x), (gate_proj, up_proj, down_proj, cw.T))
            return out
        B, S, H = hidden_states.shape
        x = hidden_states.reshape(-1, H)
        w, sel = _route(x, gate_weight, expert_bias)
        out = _moe(x, w, sel, gate_proj, up_proj, down_proj)
        shared = jax.nn.silu(x @ shared_gate.T) * (x @ shared_up.T) @ shared_down.T
        return (out + shared).reshape(B, S, H)
    x = x + jnp.tanh(g_xattn[0]) * _L0_xattn_ref(_layernorm(x, axis=-1), ctx_2048, L0_xattn_decay, L0_xattn_W_in, L0_xattn_b_in, L0_xattn_W_out, L0_xattn_b_out, L0_xattn_gamma, L0_xattn_beta)
    x = x + jnp.tanh(g_ffn[0]) * _L0_ffn_ref(_layernorm(x, axis=-1), L0_ffn_weight, L0_ffn_scale_weight, L0_ffn_bias)
    x = x + jnp.tanh(g_xattn[1]) * _L1_xattn_ref(_layernorm(x, axis=-1), ctx_2048, mask_BxS2_bk0)
    x = x + jnp.tanh(g_ffn[1]) * _L1_ffn_ref(_layernorm(x, axis=-1), L1_ffn_router_w, L1_ffn_w_gate, L1_ffn_w_up, L1_ffn_w_down, L1_ffn_sh_gate, L1_ffn_sh_up, L1_ffn_sh_down, L1_ffn_sh_gate_w)
    x = x + jnp.tanh(g_xattn[2]) * _L2_xattn_ref(_layernorm(x, axis=-1), ctx_2048, L2_xattn_Wq, L2_xattn_Wk, L2_xattn_Wv)
    x = x + jnp.tanh(g_ffn[2]) * _L2_ffn_ref(_layernorm(x, axis=-1), L2_ffn_wa, L2_ffn_rg, L2_ffn_rgb, L2_ffn_rw1, L2_ffn_rb1, L2_ffn_rw2, L2_ffn_rb2, L2_ffn_sg, L2_ffn_sgb, L2_ffn_sw1, L2_ffn_sb1, L2_ffn_sw2, L2_ffn_sb2)
    x = x + jnp.tanh(g_xattn[3]) * _L3_xattn_ref(_layernorm(x, axis=-1), ctx_2048, ctx_2048, L3_xattn_gamma)
    x = x + jnp.tanh(g_ffn[3]) * _L3_ffn_ref(_layernorm(x, axis=-1), L3_ffn_gate_weight, L3_ffn_expert_bias, L3_ffn_gate_proj, L3_ffn_up_proj, L3_ffn_down_proj, L3_ffn_shared_gate, L3_ffn_shared_up, L3_ffn_shared_down)
    return x

_drawn_inputs = setup_inputs


def setup_inputs(seed=0):
    import zlib

    import numpy as np

    out = dict(_drawn_inputs(seed))
    spreads = {'L0_xattn_b_in': (0.0, 0.1),
     'L0_xattn_b_out': (0.0, 0.1),
     'L0_xattn_gamma': (1.0, 0.2),
     'L0_xattn_beta': (0.0, 0.1),
     'L2_ffn_rgb': (0.0, 0.8),
     'L2_ffn_rb1': (0.0, 0.8),
     'L2_ffn_rb2': (0.0, 0.316),
     'L2_ffn_sgb': (0.0, 0.8),
     'L2_ffn_sb1': (0.0, 0.8),
     'L2_ffn_sb2': (0.0, 0.1),
     'L3_ffn_expert_bias': (0.0, 0.603)}
    factors = {'g_ffn': 39.544,
     'L0_ffn_bias': 5.552,
     'L2_ffn_rg': 8.0,
     'L2_ffn_rw1': 8.0,
     'L2_ffn_rw2': 8.0,
     'L2_ffn_sg': 4.551,
     'L2_ffn_sw1': 4.466,
     'L2_ffn_sw2': 4.308,
     'L3_ffn_gate_weight': 6.295,
     'L3_ffn_gate_proj': 4.189,
     'L3_ffn_up_proj': 4.15,
     'L3_ffn_down_proj': 4.141,
     'L3_ffn_shared_gate': 5.351,
     'L3_ffn_shared_up': 5.24,
     'L3_ffn_shared_down': 5.251}
    for name, (base, spread) in spreads.items():
        noise = np.random.default_rng([zlib.crc32(name.encode()), seed]).standard_normal(out[name].shape)
        drawn = base * np.exp(spread * noise) if base else spread * noise
        out[name] = jnp.asarray(drawn.astype(out[name].dtype))
    for name, factor in factors.items():
        out[name] = (out[name] * factor).astype(out[name].dtype)
    return out
```

```python
from contextlib import ExitStack

import concourse.bass as bass
from concourse import mybir

F32 = mybir.dt.float32
BF16 = mybir.dt.bfloat16
U8 = mybir.dt.uint8
ALU = mybir.AluOpType
ACT = mybir.ActivationFunctionType
AX = mybir.AxisListType
ds = bass.ds

P = 128
NB = 16
D = 256
C = D // P
NE = 16
PAD = 24
FILL = -3.0e38
BARRED = -2.9e38
TAKEN = -3.2e38
LN_EPS = 1e-5
STOP = 99


class Chain:

    def __init__(self, eng, sem, base=0):
        self.eng, self.sem, self.base, self.n = eng, sem, base, 0

    def __call__(self, ins):
        ins.then_inc(self.sem, 1)
        self.n += 1
        self.eng.wait_ge(self.sem, self.base + self.n)
        return ins


def flat(ap):
    return ap.rearrange("p a b -> p (a b)")


def build(nc, io):
    with ExitStack() as top:
        _build(nc, io, top)


def _build(nc, io, top):
    def sb(name, shape, dt=F32, at=None):
        return (at or top).enter_context(nc.sbuf_tensor(name, shape, dt))

    bank = [top.enter_context(nc.psum_tensor(f"bank{i}", [P, 512], F32)) for i in range(8)]
    x = sb("x", [P, NB, D])
    xn = sb("xn", [P, NB, D])
    ctx = sb("ctx", [P, NB, D])
    ctxT = sb("ctxT", [P, NB, C, P])
    weights = sb("weights", [P, 24320])
    ident = sb("ident", [P, P])
    ones = sb("ones", [P, P])
    neg_half = sb("neg_half", [P, 64])
    mean = sb("mean", [P, NB])
    rstd = sb("rstd", [P, NB])
    comb = sb("comb", [P, NB, 20])
    xs = sb("xs", [P, 2, D])
    xT = sb("xT", [P, 2, C, P])
    small = {k: sb(k, list(io[k].shape), U8 if k == "mask" else F32)
             for k in ("mask", "g_xattn", "g_ffn", "decay", "l0_win", "l0_bin", "l0_wout", "l0_bout", "l0_gamma",
                       "l0_beta", "l0_w", "l0_scale", "l0_bias", "l1_router", "l2_router", "l3_router",
                       "l2_wq", "l2_wk", "l2_wv", "l2_b2", "l3_gamma", "l3_ebias")}
    gbias = sb("gbias", [3, 18 * 256], BF16)
    tg_x = sb("tg_x", [P, 4])
    tg_f = sb("tg_f", [P, 4])

    inputs_loaded = top.enter_context(nc.semaphore("inputs_loaded"))
    moe_loaded = [top.enter_context(nc.semaphore(f"moe_loaded{i}")) for i in range(3)]
    out_stored = top.enter_context(nc.semaphore("out_stored"))

    MOE = {1: dict(E=20, I=176, parts=2, k=4), 2: dict(E=18, I=128, parts=1, k=2), 3: dict(E=17, I=128, parts=1, k=4)}

    def moe_views(layer):
        m = MOE[layer]
        n = m["E"] * C * 2 * m["I"]
        kp = m["I"] // m["parts"]
        gu = weights[:, 0:n].rearrange("p (e c i) -> p e c i", e=m["E"], c=C)
        dn = weights[0:kp, n:n + m["E"] * m["parts"] * D].rearrange("p (e k d) -> p e k d", e=m["E"], k=m["parts"])
        return gu, dn, kp

    def load_experts(eng, layer):
        gu, dn, _ = moe_views(layer)
        eng.dma_start(gu, io[f"l{layer}_gu"]).then_inc(moe_loaded[layer - 1], 16)
        eng.dma_start(dn, io[f"l{layer}_dn"]).then_inc(moe_loaded[layer - 1], 16)

    def carver():
        at = [18 * (2 * D + D)]

        def carve(shape):
            n = 1
            for k in shape[1:]:
                n *= k
            view = weights[0:shape[0], at[0]:at[0] + n]
            at[0] += n
            assert at[0] <= 24320
            if len(shape) > 2:
                names = "abcd"[:len(shape) - 1]
                view = view.rearrange(f"p ({' '.join(names)}) -> p {' '.join(names)}",
                                      **{k: v for k, v in zip(names, shape[1:])})
            return view
        return carve

    def setup():
        with ExitStack() as st:
            sem = lambda n: st.enter_context(nc.semaphore(n))
            cleared = sem("su_cleared")
            own = sem("su_own")
            b_raw = sb("b_raw", [3, 18 * 256 // 9], F32, st)
            b_one = sb("b_one", [3, 512], F32, st)
            parts = [sb(f"b_part{i}", [3, 512], BF16, st) for i in range(3)]
            b_in = sem("su_b_in")
            b_done = sem("su_b_done")
            block = st.enter_context(nc.Block())

            @block.sync
            def _(sp):
                sp.dma_start(x[:], io["x"]).then_inc(inputs_loaded, 16)
                for k in small:
                    sp.dma_start(small[k][:], io[k]).then_inc(inputs_loaded, 16)
                sp.dma_start(ctx[:], io["ctx"]).then_inc(inputs_loaded, 16)
                sp.dma_start(ctxT[:], io["ctxT"]).then_inc(inputs_loaded, 16)
                load_experts(sp, 1)

            @block.scalar
            def _(act):
                for i in range(9):
                    if i:
                        act.wait_ge(b_done, i)
                    act.dma_start(b_raw[:], io["l2_gub"][:, i * 512:(i + 1) * 512]).then_inc(b_in, 16)
                act.wait_ge(inputs_loaded, 16 * (len(small) + 3))
                nc.scalar.activation(tg_x[:], small["g_xattn"][:], ACT.Tanh)
                nc.scalar.activation(tg_f[:], small["g_ffn"][:], ACT.Tanh)

            @block.gpsimd
            def _(pool):
                nc.gpsimd.memset(ident[:], 0.0).then_inc(cleared, 1)
                nc.gpsimd.memset(ones[:], 1.0)
                nc.gpsimd.memset(neg_half[:], -0.5)
                pool.wait_ge(cleared, 1)
                nc.gpsimd.affine_select(out=ident[:], in_=ident[:], compare_op=ALU.not_equal, fill=1.0, base=0,
                                        pattern=[[-1, P]], channel_multiplier=1)

            @block.vector
            def _(dve):
                step = Chain(dve, own)
                for i in range(9):
                    dve.wait_ge(b_in, 16 * (i + 1))
                    cols = slice(i * 512, (i + 1) * 512)
                    step(nc.vector.tensor_copy(parts[0][:], b_raw[:]))
                    step(nc.vector.tensor_tensor(b_one[:], b_raw[:], parts[0][:], ALU.subtract))
                    step(nc.vector.tensor_copy(parts[1][:], b_one[:]))
                    step(nc.vector.tensor_tensor(b_one[:], b_one[:], parts[1][:], ALU.subtract))
                    step(nc.vector.tensor_copy(gbias[0:3, cols], b_one[:]))
                    step(nc.vector.tensor_copy(gbias[0:2, cols], parts[1][0:2, :]))
                    nc.vector.tensor_copy(gbias[0:1, cols], parts[0][0:1, :]).then_inc(b_done, 1)
                    dve.wait_ge(b_done, i + 1)

    def normalize(name, affine=None):
        src = x if affine is None else xn
        with ExitStack() as st:
            sem = lambda n: st.enter_context(nc.semaphore(f"{name}_{n}"))
            stats = sb(f"{name}_stats", [P, NB, 6], F32, st)
            tmp = sb(f"{name}_tmp", [P, 2, NB], F32, st)
            own, var_ready, rstd_ready = sem("own"), sem("var"), sem("rstd")
            block = st.enter_context(nc.Block())

            @block.vector
            def _(dve):
                with dve.Fori(0, NB) as t:
                    nc.vector.bn_stats(flat(stats[:, ds(t, 1), :]), flat(src[:, ds(t, 1), :])).then_inc(own, 1)
                dve.wait_ge(own, NB)
                step = Chain(dve, own, NB)
                nc.vector.tensor_tensor(mean[:], stats[:, :, 1], stats[:, :, 4], ALU.add).then_inc(own, 1)
                nc.vector.tensor_tensor(tmp[:, 0, :], stats[:, :, 1], stats[:, :, 4], ALU.subtract).then_inc(own, 1)
                nc.vector.tensor_tensor(tmp[:, 1, :], stats[:, :, 2], stats[:, :, 5], ALU.add).then_inc(own, 1)
                step.n = 3
                dve.wait_ge(own, NB + 3)
                step(nc.vector.tensor_tensor(tmp[:, 0, :], tmp[:, 0, :], tmp[:, 0, :], ALU.mult))
                step(nc.vector.tensor_scalar(tmp[:, 1, :], tmp[:, 1, :], 1.0 / D, LN_EPS, ALU.mult, ALU.add))
                step(nc.vector.tensor_scalar(mean[:], mean[:], 0.5, None, ALU.mult))
                nc.vector.scalar_tensor_tensor(tmp[:, 1, :], tmp[:, 0, :], 0.25, tmp[:, 1, :], ALU.mult,
                                               ALU.add).then_inc(var_ready, 1)
                dve.wait_ge(rstd_ready, 1)
                with dve.Fori(0, NB) as t:
                    nc.vector.tensor_scalar(xn[:, ds(t, 1), :], src[:, ds(t, 1), :], mean[:, ds(t, 1)],
                                            rstd[:, ds(t, 1)], ALU.subtract, ALU.mult)

            @block.gpsimd
            def _(pool):
                pool.wait_ge(var_ready, 1)
                nc.gpsimd.tensor_tensor(rstd[:], tmp[:, 1, :], neg_half[:, 0:NB], ALU.pow).then_inc(rstd_ready, 1)

    def decay_summary():
        with ExitStack() as st:
            sem = lambda n: st.enter_context(nc.semaphore(f"l0a_{n}"))
            own, pe_done, act_done = sem("own"), sem("pe"), sem("act")
            e_ready = sem("e")
            K = sb("K", [P, 1], F32, st)
            powers = sb("powers", [P, P], F32, st)
            kbc = sb("kbc", [P, P], F32, st)
            cw = sb("cw", [P, 2], F32, st)
            sumT = sb("sumT", [P, C, NB], F32, st)
            inT = sb("inT", [P, C, NB], F32, st)
            block = st.enter_context(nc.Block())

            @block.scalar
            def _(act):
                nc.scalar.activation(K[:], small["decay"][:], ACT.Exp, scale=-1.0).then_inc(e_ready, 1)

            @block.vector
            def _(dve):
                step = Chain(dve, own)
                dve.wait_ge(e_ready, 1)
                step(nc.vector.tensor_scalar(K[:], K[:], 1.0, None, ALU.add))
                step(nc.vector.reciprocal(K[:], K[:]))
                step(nc.vector.tensor_scalar(kbc[:], ones[:], K[:], None, ALU.mult))
                step(nc.vector.tensor_tensor_scan(powers[:], kbc[:], ident[:], 0.0, ALU.mult, ALU.add))
                step(nc.vector.tensor_reduce(cw[:, 0:1], powers[:], AX.X, ALU.add))
                step(nc.vector.tensor_scalar(cw[:, 0:1], cw[:, 0:1], 1.0 / P, None, ALU.mult))
                dve.wait_ge(pe_done, 1)
                step(nc.vector.tensor_copy(cw[:, 1:2], bank[0][:, 32:33]))
                step(nc.vector.tensor_copy(sumT[:], bank[0][:, 0:32].rearrange("p (b c) -> p c b", c=C)))
                dve.wait_ge(pe_done, 2)
                bb = sb("bb", [P, C], F32, st)
                step(nc.vector.tensor_scalar(bb[:], small["l0_bin"][:], cw[:, 1:2], None, ALU.mult))
                for c in range(C):
                    step(nc.vector.tensor_scalar(inT[:, c, :], bank[1][:, c * NB:(c + 1) * NB], bb[:, c:c + 1], None,
                                                 ALU.add))
                for b in range(NB):
                    dve.wait_ge(pe_done, 3 + b)
                    step(nc.vector.tensor_tensor(xn[:, b, :], xn[:, b, :], bank[2 + b % 4][:, 0:D], ALU.add))
                    step(nc.vector.tensor_tensor(xn[:, b, :], xn[:, b, :], small["l0_bout"][:], ALU.add))

            @block.tensor
            def _(pe):
                pe.wait_ge(own, 6)
                nc.tensor.matmul(bank[0][:, 32:33], ones[:], cw[:, 0:1], start=True, stop=True)
                for b in range(NB):
                    for c in range(C):
                        last = nc.tensor.matmul(bank[0][:, b * C + c:b * C + c + 1], ctx[:, b, c * P:(c + 1) * P],
                                                cw[:, 0:1], start=True, stop=True)
                last.then_inc(pe_done, 1)
                pe.wait_ge(own, 8)
                for e in range(C):
                    for c in range(C):
                        last = nc.tensor.matmul(bank[1][:, e * NB:(e + 1) * NB],
                                                small["l0_win"][:, c, e * P:(e + 1) * P], sumT[:, c, :],
                                                start=(c == 0), stop=(c == C - 1))
                last.then_inc(pe_done, 1)
                pe.wait_ge(own, 11)
                for b in range(NB):
                    if b >= 4:
                        pe.wait_ge(own, 11 + 2 * (b - 4) + 1)
                    for c in range(C):
                        last = nc.tensor.matmul(bank[2 + b % 4][:, 0:D], inT[:, c, b:b + 1].broadcast_to([P, P]),
                                                small["l0_wout"][:, c, :], start=(c == 0), stop=(c == C - 1))
                    last.then_inc(pe_done, 1)

    def decay_add():
        with ExitStack() as st:
            own = st.enter_context(nc.semaphore("l0b_own"))
            tmp = sb("l0b_tmp", [P, 2, 1, D], F32, st)
            gg = sb("l0b_gg", [P, 2, 1, D], F32, st)
            block = st.enter_context(nc.Block())

            @block.vector
            def _(dve):
                step = Chain(dve, own)
                step(nc.vector.tensor_scalar(gg[:, 0, 0, :], small["l0_gamma"][:], tg_x[:, 0:1], None, ALU.mult))
                step(nc.vector.tensor_scalar(gg[:, 1, 0, :], small["l0_beta"][:], tg_x[:, 0:1], None, ALU.mult))
                with dve.Fori(0, NB) as t:
                    step = Chain(dve, own, t * 3 + 2)
                    xt = x[:, ds(t, 1), :]
                    step(nc.vector.tensor_tensor(tmp[:, 0], xn[:, ds(t, 1), :], gg[:, 0], ALU.mult))
                    step(nc.vector.tensor_tensor(tmp[:, 0], tmp[:, 0], gg[:, 1], ALU.add))
                    step(nc.vector.tensor_tensor(xt, xt, tmp[:, 0], ALU.add))

    def linear():
        with ExitStack() as st:
            sem = lambda n: st.enter_context(nc.semaphore(f"l0f_{n}"))
            staged, turned, xT_ready, y_ready, own, used = (sem(n) for n in
                                                           ("staged", "turned", "xT", "y", "own", "used"))
            w_ready = sem("w")
            block = st.enter_context(nc.Block())
            w = small["l0_w"]

            @block.gpsimd
            def _(pool):
                with pool.Fori(0, NB) as t:
                    pool.wait_ge(turned, t + 1)
                    nc.gpsimd.tensor_copy(xs[:, 0:1, :], xn[:, ds(t, 1), :]).then_inc(staged, 1)

            @block.tensor
            def _(pe):
                pe.sem_inc(turned, 1)
                pe.wait_ge(w_ready, 4)
                with pe.Fori(0, NB) as t:
                    pe.wait_ge(staged, t + 1)
                    for c in range(C):
                        last = nc.tensor.transpose(bank[0][:, c * P:(c + 1) * P], xs[:, 0, c * P:(c + 1) * P], ident[:])
                    last.then_inc(turned, 1)
                    pe.wait_ge(xT_ready, t + 1)
                    pe.wait_ge(used, t + 1)
                    for c in range(C):
                        last = nc.tensor.matmul(bank[1][:, 0:D], xT[:, 0, c, :], w[:, c, :], start=(c == 0),
                                                stop=(c == C - 1))
                    last.then_inc(y_ready, 1)

            @block.scalar
            def _(act):
                with act.Fori(0, NB) as t:
                    act.wait_ge(turned, t + 2)
                    nc.scalar.copy(flat(xT[:, 0]), bank[0][:, 0:D]).then_inc(xT_ready, 1)

            @block.vector
            def _(dve):
                step = Chain(dve, w_ready)
                for c in range(C):
                    step(nc.vector.tensor_tensor(w[:, c, :], w[:, c, :], small["l0_scale"][:], ALU.mult))
                step(nc.vector.tensor_scalar(flat(w[:]), flat(w[:]), tg_f[:, 0:1], None, ALU.mult))
                step(nc.vector.tensor_scalar(small["l0_bias"][:], small["l0_bias"][:], tg_f[:, 0:1], None, ALU.mult))
                dve.sem_inc(used, 1)
                with dve.Fori(0, NB) as t:
                    step = Chain(dve, own, t)
                    xt = x[:, ds(t, 1), :]
                    dve.wait_ge(y_ready, t + 1)
                    nc.vector.tensor_tensor(xt, xt, bank[1][:, 0:D].rearrange("p (a d) -> p a d", a=1),
                                            ALU.add).then_inc(used, 1)
                    dve.wait_ge(used, t + 2)
                    step(nc.vector.tensor_tensor(xt, xt, small["l0_bias"][:].rearrange("p (a d) -> p a d", a=1),
                                                 ALU.add))

    def masked_attention():
        with ExitStack() as st:
            sem = lambda n: st.enter_context(nc.semaphore(f"l1a_{n}"))
            staged, turned, xT_ready, s_ready, exp_ready, e_turned, eT_ready, y_ready, own = (
                sem(n) for n in ("staged", "turned", "xT", "s", "exp", "et", "eT", "y", "own"))
            bias_ready = sem("bias")
            score = sb("score", [P, P], F32, st)
            neg = sb("neg", [P, P], F32, st)
            top1 = sb("top1", [P, 4], F32, st)
            kept = sb("kept", [P, NB], F32, st)
            e = sb("e", [P, P], F32, st)
            eT = sb("eT", [P, P], F32, st)
            block = st.enter_context(nc.Block())
            mask = small["mask"]

            @block.gpsimd
            def _(pool):
                with pool.Fori(0, NB) as b:
                    pool.wait_ge(turned, b + 1)
                    nc.gpsimd.tensor_copy(xs[:, 0:1, :], xn[:, ds(b, 1), :]).then_inc(staged, 1)

            @block.tensor
            def _(pe):
                pe.sem_inc(turned, 1)
                with pe.Fori(0, NB) as b:
                    pe.wait_ge(staged, b + 1)
                    for c in range(C):
                        last = nc.tensor.transpose(bank[0][:, c * P:(c + 1) * P], xs[:, 0, c * P:(c + 1) * P], ident[:])
                    last.then_inc(turned, 1)
                    pe.wait_ge(xT_ready, b + 1)
                    for c in range(C):
                        last = nc.tensor.matmul(bank[1][:, 0:P], xT[:, 0, c, :], flat(ctxT[:, ds(b, 1), c, :]),
                                                start=(c == 0), stop=(c == C - 1))
                    last.then_inc(s_ready, 1)
                    pe.wait_ge(exp_ready, b + 1)
                    nc.tensor.transpose(bank[2][:, 0:P], e[:], ident[:]).then_inc(e_turned, 1)
                    pe.wait_ge(eT_ready, b + 1)
                    nc.tensor.matmul(bank[3][:, 0:D], eT[:], flat(ctx[:, ds(b, 1), :]), start=True,
                                     stop=True).then_inc(y_ready, 1)

            @block.scalar
            def _(act):
                with act.Fori(0, NB) as b:
                    act.wait_ge(turned, b + 2)
                    nc.scalar.copy(flat(xT[:, 0]), bank[0][:, 0:D]).then_inc(xT_ready, 1)
                    act.wait_ge(bias_ready, b + 1)
                    nc.scalar.activation(e[:], score[:], ACT.Exp, bias=top1[:, 0:1],
                                         accum_out=top1[:, 1:2]).then_inc(exp_ready, 1)

            @block.vector
            def _(dve):
                step = Chain(dve, own)
                step(nc.vector.tensor_reduce(kept[:], mask[:], AX.X, ALU.max))
                step(nc.vector.tensor_scalar(kept[:], kept[:], tg_x[:, 1:2], None, ALU.mult))
                with dve.Fori(0, NB) as b:
                    step = Chain(dve, own, b * 7 + 2)
                    mk = flat(mask[:, ds(b, 1), :])
                    step(nc.vector.tensor_scalar(neg[:], mk, -1.0, 1e30, ALU.add, ALU.mult))
                    dve.wait_ge(s_ready, b + 1)
                    step(nc.vector.scalar_tensor_tensor(score[:], bank[1][:, 0:P], D ** -0.5, mk, ALU.mult, ALU.mult))
                    step(nc.vector.tensor_tensor(score[:], score[:], neg[:], ALU.add))
                    step(nc.vector.tensor_reduce(top1[:, 0:1], score[:], AX.X, ALU.max))
                    nc.vector.tensor_scalar(top1[:, 0:1], top1[:, 0:1], -1.0, None, ALU.mult).then_inc(bias_ready, 1)
                    dve.wait_ge(e_turned, b + 1)
                    nc.vector.tensor_copy(eT[:], bank[2][:, 0:P]).then_inc(eT_ready, 1)
                    step(nc.vector.reciprocal(top1[:, 2:3], top1[:, 1:2]))
                    step(nc.vector.tensor_scalar(top1[:, 2:3], top1[:, 2:3], kept[:, ds(b, 1)], None, ALU.mult))
                    dve.wait_ge(y_ready, b + 1)
                    step(nc.vector.scalar_tensor_tensor(flat(x[:, ds(b, 1), :]), bank[3][:, 0:D], top1[:, 2:3],
                                                        flat(x[:, ds(b, 1), :]), ALU.mult, ALU.add))

    def many_heads():
        H, HD = 32, 8
        carve = carver()
        with ExitStack() as st:
            sem = lambda n: st.enter_context(nc.semaphore(f"l2a_{n}"))
            (staged, turned, xT_ready, p_ready, sq_ready, pow_done, qk_ready, qk_turned, qkT_ready, s_ready, e_ready,
             pv_done, y_ready, own, q_spread, own_act, mask_ready) = (sem(n) for n in (
                "staged", "turned", "xT", "p", "sq", "pow", "qk", "qkt", "qkT", "s", "e", "pv", "y", "own", "qs",
                "oa", "mk"))
            cT = carve([P, C, P])
            sq = carve([P, D])
            ss = carve([P, 2, H])
            rn = carve([P, 2, H])
            qk = carve([P, 2, D])
            qT = carve([P, C, P])
            kT = carve([P, C, P])
            qm = carve([P, C, 4, P])
            rowmask = carve([P, 4, P])
            v = carve([P, H, HD + 1])
            e = carve([P, 3, 4, P])
            inv = carve([P, H])
            o = carve([P, H, HD])
            block = st.enter_context(nc.Block())

            @block.sync
            def _(sp):
                load_experts(sp, 2)

            @block.gpsimd
            def _(pool):
                nc.gpsimd.memset(rowmask[:], 1.0).then_inc(mask_ready, 1)
                nc.gpsimd.memset(v[:], 1.0).then_inc(mask_ready, 1)
                pool.wait_ge(mask_ready, 2)
                for g in range(4):
                    rm = rowmask[32 * g:32 * g + 32]
                    nc.gpsimd.affine_select(out=rm, in_=rm, compare_op=ALU.is_ge, fill=0.0, base=0,
                                            pattern=[[-HD, 4], [0, P]], channel_multiplier=1).then_inc(mask_ready, 1)
                pool.wait_ge(mask_ready, 6)
                for g in range(4):
                    rm = rowmask[32 * g:32 * g + 32]
                    nc.gpsimd.affine_select(out=rm, in_=rm, compare_op=ALU.is_ge, fill=0.0, base=HD - 1,
                                            pattern=[[HD, 4], [0, P]], channel_multiplier=-1).then_inc(mask_ready, 1)
                pool.wait_ge(mask_ready, 10)
                with pool.Fori(0, NB) as b:
                    pool.wait_ge(turned, b + 1)
                    nc.gpsimd.tensor_copy(xs[:, 0:1, :], xn[:, ds(b, 1), :]).then_inc(staged, 1)
                    pool.wait_ge(p_ready, b + 1)
                    nc.gpsimd.tensor_copy(flat(cT[:]), ctxT[:, ds(b, 1), :, :].rearrange("p a c m -> p (a c m)")).then_inc(staged, 1)
                    pool.wait_ge(sq_ready, b + 1)
                    nc.gpsimd.tensor_tensor(flat(rn[:]), flat(ss[:]), neg_half[:], ALU.pow).then_inc(pow_done, 1)

            @block.tensor
            def _(pe):
                pe.sem_inc(turned, 1)
                pe.sem_inc(p_ready, 1)
                with pe.Fori(0, NB) as b:
                    pe.wait_ge(staged, b * 2 + 1)
                    for c in range(C):
                        last = nc.tensor.transpose(bank[0][:, c * P:(c + 1) * P], xs[:, 0, c * P:(c + 1) * P], ident[:])
                    last.then_inc(turned, 1)
                    pe.wait_ge(staged, b * 2 + 2)
                    pe.wait_ge(xT_ready, b + 1)
                    for i, (lhs, w) in enumerate(((xT[:, 0], "l2_wq"), (cT, "l2_wk"))):
                        for c in range(C):
                            nc.tensor.matmul(bank[1][:, i * D:(i + 1) * D], lhs[:, c, :], small[w][:, c, :],
                                             start=(c == 0), stop=(c == C - 1))
                    for c in range(C):
                        last = nc.tensor.matmul(bank[2][:, 0:D], cT[:, c, :], small["l2_wv"][:, c, :],
                                                start=(c == 0), stop=(c == C - 1))
                    last.then_inc(p_ready, 1)
                    pe.wait_ge(qk_ready, b + 1)
                    for i in range(2):
                        for c in range(C):
                            last = nc.tensor.transpose(bank[7 * i][:, c * P:(c + 1) * P],
                                                       qk[:, i, c * P:(c + 1) * P], ident[:])
                    last.then_inc(qk_turned, 1)
                    pe.wait_ge(q_spread, b * 2 + 2)
                    for n in range(8 + 1):
                        if n < 8:
                            c, g = divmod(n, 4)
                            rows = slice(32 * g, 32 * g + 32)
                            pe.wait_ge(e_ready, b * 8 + n)
                            nc.tensor.matmul(bank[3 + n % 3][:], kT[rows, c, :],
                                             qm[rows, c].rearrange("p j q -> p (j q)"), start=True, stop=True,
                                             tile_position=(32 * g, 0)).then_inc(s_ready, 1)
                        if n >= 1:
                            m = n - 1
                            pe.wait_ge(e_ready, b * 8 + m + 2)
                            for j in range(4):
                                h = 4 * m + j
                                last = nc.tensor.matmul(bank[6][:, h * (HD + 1):(h + 1) * (HD + 1)],
                                                        e[:, m % 3, j, :], v[:, h, :], start=True, stop=True)
                            last.then_inc(pv_done, 1)

            @block.scalar
            def _(act):
                act.sem_inc(e_ready, 1)
                with act.Fori(0, NB) as b:
                    act.wait_ge(turned, b + 2)
                    nc.scalar.copy(flat(xT[:, 0]), bank[0][:, 0:D]).then_inc(xT_ready, 1)
                    act.wait_ge(qk_turned, b + 1)
                    nc.scalar.copy(flat(kT[:]), bank[7][:, 0:D]).then_inc(q_spread, 1)
                    for n in range(8):
                        act.wait_ge(s_ready, b * 8 + n + 1)
                        if n >= 3:
                            act.wait_ge(pv_done, b * 8 + n - 2)
                        nc.scalar.activation(flat(e[:, n % 3]), bank[3 + n % 3][:], ACT.Exp,
                                             scale=HD ** -0.5).then_inc(e_ready, 1)

            @block.vector
            def _(dve):
                dve.wait_ge(mask_ready, 10)
                with dve.Fori(0, NB) as b:
                    step = Chain(dve, own, b * 8)
                    dve.wait_ge(p_ready, b + 2)
                    for i in range(2):
                        src = bank[1][:, i * D:(i + 1) * D]
                        step(nc.vector.tensor_copy(qk[:, i, :], src))
                        step(nc.vector.tensor_tensor(sq[:], qk[:, i, :], qk[:, i, :], ALU.mult))
                        ins = nc.vector.tensor_reduce(ss[:, i, :], sq[:].rearrange("p (h d) -> p h d", h=H), AX.X,
                                                      ALU.add)
                        if i == 0:
                            step(ins)
                        else:
                            step(ins)
                    nc.vector.tensor_scalar(flat(ss[:]), flat(ss[:]), 1.0 / HD, 1e-6, ALU.mult,
                                            ALU.add).then_inc(sq_ready, 1)
                    nc.vector.tensor_copy(v[:, :, 0:HD], bank[2][:, 0:D].rearrange("p (h d) -> p h d", h=H)).then_inc(y_ready, 1)
                    dve.wait_ge(pow_done, b + 1)
                    nc.vector.tensor_tensor(qk[:].rearrange("p i (h d) -> p (i h) d", h=H),
                                            qk[:].rearrange("p i (h d) -> p (i h) d", h=H),
                                            flat(rn[:]).unsqueeze(2).broadcast_to([P, 2 * H, HD]),
                                            ALU.mult).then_inc(qk_ready, 1)
                    dve.wait_ge(qk_turned, b + 1)
                    nc.vector.tensor_copy(flat(qT[:]), bank[0][:, 0:D]).then_inc(qkT_ready, 1)
                    dve.wait_ge(qkT_ready, b * 3 + 1)
                    for c in range(C):
                        ins = nc.vector.tensor_tensor(qm[:, c], qT[:, c, :].unsqueeze(1).broadcast_to([P, 4, P]),
                                                      rowmask[:], ALU.mult).then_inc(qkT_ready, 1)
                    dve.wait_ge(qkT_ready, b * 3 + 3)
                    dve.sem_inc(q_spread, 1)
                    dve.wait_ge(pv_done, b * 8 + 8)
                    pv = bank[6][:, 0:H * (HD + 1)].rearrange("p (h d) -> p h d", h=H)
                    step(nc.vector.reciprocal(inv[:], pv[:, :, HD]))
                    nc.vector.tensor_tensor(o[:], pv[:, :, 0:HD], inv[:].unsqueeze(2).broadcast_to([P, H, HD]),
                                            ALU.mult).then_inc(y_ready, 1)
                    dve.wait_ge(y_ready, b * 2 + 2)
                    step(nc.vector.scalar_tensor_tensor(flat(x[:, ds(b, 1), :]), flat(o[:]), tg_x[:, 2:3],
                                                        flat(x[:, ds(b, 1), :]), ALU.mult, ALU.add))

    def channel_heads():
        H, HD, L = 8, 16, D
        scale = HD ** -0.5
        carve = carver()
        with ExitStack() as st:
            sem = lambda n: st.enter_context(nc.semaphore(f"l3a_{n}"))
            (staged, k_spread, s_ready, m_ready, e_ready, e_turned, eT_ready, pv_done, o_ready, o_turned, own,
             v_ready, mask_ready, x_done) = (sem(n) for n in (
                "staged", "ks", "s", "m", "e", "et", "eT", "pv", "o", "ot", "own", "v", "mk", "x"))
            km = carve([P, 2, L])
            rowmask = carve([P, 2, L])
            mx = carve([P, 2, 2])
            e = carve([P, 2, 2, L])
            eT = carve([P, 2, 4, P])
            v = carve([P, C, H, HD + 1])
            inv = carve([P, H])
            o = carve([P, 2, H, HD])
            gf = carve([P, 1])
            block = st.enter_context(nc.Block())
            G = 4

            @block.sync
            def _(sp):
                load_experts(sp, 3)

            @block.gpsimd
            def _(pool):
                nc.gpsimd.memset(rowmask[:], 1.0).then_inc(mask_ready, 1)
                nc.gpsimd.memset(v[:], 1.0).then_inc(mask_ready, 1)
                pool.wait_ge(mask_ready, 2)
                for g in range(G):
                    rm = rowmask[32 * g:32 * g + 32]
                    nc.gpsimd.affine_select(out=rm, in_=rm, compare_op=ALU.is_ge, fill=0.0, base=0,
                                            pattern=[[-HD, 2], [0, L]], channel_multiplier=1).then_inc(mask_ready, 1)
                pool.wait_ge(mask_ready, 6)
                for g in range(G):
                    rm = rowmask[32 * g:32 * g + 32]
                    nc.gpsimd.affine_select(out=rm, in_=rm, compare_op=ALU.is_ge, fill=0.0, base=HD - 1,
                                            pattern=[[HD, 2], [0, L]], channel_multiplier=-1).then_inc(mask_ready, 1)
                pool.wait_ge(mask_ready, 10)
                with pool.Fori(0, NB) as b:
                    pool.wait_ge(x_done, b + 1)
                    nc.gpsimd.tensor_copy(xs[:, 0:1, :], xn[:, ds(b, 1), :]).then_inc(staged, 1)
                    for c in range(C):
                        nc.gpsimd.tensor_copy(v[:, c, :, 0:HD],
                                              flat(ctxT[:, ds(b, 1), c, :]).rearrange("p (h d) -> p h d", h=H)
                                              ).then_inc(v_ready, 1)

            @block.tensor
            def _(pe):
                with pe.Fori(0, NB) as b:
                    pe.wait_ge(staged, b + 1)
                    pe.wait_ge(k_spread, b + 1)
                    pe.wait_ge(v_ready, b * 2 + 2)
                    for n in range(8 + 2):
                        if n < 8:
                            qh, g = divmod(n, G)
                            rows = slice(32 * g, 32 * g + 32)
                            if n >= 2:
                                pe.wait_ge(e_ready, b * 16 + 2 * (n - 2) + 2)
                            nc.tensor.matmul(bank[n % 2][:], xs[rows, 0, qh * P:(qh + 1) * P],
                                             km[rows].rearrange("p j l -> p (j l)"), start=True, stop=True,
                                             tile_position=(32 * g, 0)).then_inc(s_ready, 1)
                        if 1 <= n < 9:
                            m = n - 1
                            pe.wait_ge(e_ready, b * 16 + 2 * m + 2)
                            if m >= 2:
                                pe.wait_ge(eT_ready, b * 8 + m - 1)
                            for j in range(2):
                                for c in range(C):
                                    k = j * C + c
                                    last = nc.tensor.transpose(bank[2 + m % 2][:, k * P:(k + 1) * P],
                                                               e[:, m % 2, j, c * P:(c + 1) * P], ident[:])
                            last.then_inc(e_turned, 1)
                        if n >= 2:
                            m = n - 2
                            qh, g = divmod(m, G)
                            pe.wait_ge(eT_ready, b * 8 + m + 1)
                            for j in range(2):
                                h = 2 * g + j
                                for c in range(C):
                                    last = nc.tensor.matmul(bank[4 + qh][:, h * (HD + 1):(h + 1) * (HD + 1)],
                                                            eT[:, m % 2, j * C + c, :], v[:, c, h, :],
                                                            start=(c == 0), stop=(c == C - 1))
                            last.then_inc(pv_done, 1)
                    pe.wait_ge(o_ready, b * 2 + 2)
                    for qh in range(2):
                        last = nc.tensor.transpose(bank[6][:, qh * P:(qh + 1) * P],
                                                   o[:, qh].rearrange("p h d -> p (h d)"), ident[:])
                    last.then_inc(o_turned, 1)

            @block.scalar
            def _(act):
                with act.Fori(0, NB) as b:
                    for n in range(8):
                        act.wait_ge(m_ready, b * 8 + n + 1)
                        if n >= 2:
                            act.wait_ge(e_turned, b * 8 + n - 1)
                        for j in range(2):
                            nc.scalar.activation(e[:, n % 2, j, :], bank[n % 2][:, j * L:(j + 1) * L], ACT.Exp,
                                                 bias=mx[:, n % 2, j:j + 1], scale=scale).then_inc(e_ready, 1)

            @block.vector
            def _(dve):
                nc.vector.tensor_tensor(gf[:], small["l3_gamma"][:], tg_x[:, 3:4], ALU.mult).then_inc(own, 1)
                dve.wait_ge(mask_ready, 10)
                dve.sem_inc(x_done, 1)
                with dve.Fori(0, NB) as b:
                    step = Chain(dve, own, b * 11 + 1)
                    nc.vector.tensor_tensor(km[:], ctx[:, ds(b, 1), :].broadcast_to([P, 2, L]), rowmask[:],
                                            ALU.mult).then_inc(k_spread, 1)
                    for n in range(8 + 1):
                        if n < 8:
                            dve.wait_ge(s_ready, b * 8 + n + 1)
                            step(nc.vector.tensor_reduce(mx[:, n % 2, :],
                                                         bank[n % 2][:].rearrange("p (j l) -> p j l", j=2), AX.X,
                                                         ALU.max))
                            nc.vector.tensor_scalar(mx[:, n % 2, :], mx[:, n % 2, :], -scale, None,
                                                    ALU.mult).then_inc(m_ready, 1)
                        if n >= 1:
                            m = n - 1
                            dve.wait_ge(e_turned, b * 8 + m + 1)
                            if m >= 2:
                                dve.wait_ge(pv_done, b * 8 + m - 1)
                            nc.vector.tensor_copy(flat(eT[:, m % 2]), bank[2 + m % 2][:]).then_inc(eT_ready, 1)
                    for qh in range(2):
                        dve.wait_ge(pv_done, b * 8 + 4 * (qh + 1))
                        pv = bank[4 + qh][:, 0:H * (HD + 1)].rearrange("p (h d) -> p h d", h=H)
                        step(nc.vector.reciprocal(inv[:], pv[:, :, HD]))
                        nc.vector.tensor_tensor(o[:, qh], pv[:, :, 0:HD], inv[:].unsqueeze(2).broadcast_to([P, H, HD]),
                                                ALU.mult).then_inc(o_ready, 1)
                        dve.wait_ge(o_ready, b * 2 + qh + 1)
                    dve.wait_ge(o_turned, b + 1)
                    step(nc.vector.scalar_tensor_tensor(flat(x[:, ds(b, 1), :]), bank[6][:, 0:D], gf[:, 0:1],
                                                        flat(x[:, ds(b, 1), :]), ALU.mult, ALU.add))
                    dve.sem_inc(x_done, 1)

    def route(layer):
        m = MOE[layer]
        R = 17 if layer == 1 else 16
        router = small[f"l{layer}_router"]
        with ExitStack() as st:
            sem = lambda n: nc.alloc_semaphore(f"r{layer}_{n}")
            staged, turned, xT_ready, l_ready, own, act_done, to_act, taken = (
                sem(n) for n in ("staged", "turned", "xT", "l", "own", "act", "ta", "taken"))
            carve = carver()
            t = lambda n, s: sb(f"r{layer}_{n}", s, F32, st) if layer == 1 else carve(s)
            lg = t("lg", [P, NB, R])
            prob = t("prob", [P, NB, PAD])
            rep = t("rep", [P, NB, PAD])
            best = t("best", [P, NB, 8])
            row = t("row", [P, 3, NB])
            block = st.enter_context(nc.Block())

            @block.gpsimd
            def _(pool):
                with pool.Fori(0, NB) as i:
                    pool.wait_ge(turned, i + 1)
                    nc.gpsimd.tensor_copy(xs[:, 0:1, :], xn[:, ds(i, 1), :]).then_inc(staged, 1)

            @block.tensor
            def _(pe):
                pe.sem_inc(turned, 1)
                with pe.Fori(0, NB) as i:
                    pe.wait_ge(staged, i + 1)
                    for c in range(C):
                        last = nc.tensor.transpose(bank[0][:, c * P:(c + 1) * P], xs[:, 0, c * P:(c + 1) * P], ident[:])
                    last.then_inc(turned, 1)
                    pe.wait_ge(xT_ready, i + 1)
                    pe.wait_ge(taken, i + 1)
                    for c in range(C):
                        last = nc.tensor.matmul(bank[1][:, 0:R], xT[:, 0, c, :], router[:, c, :], start=(c == 0),
                                                stop=(c == C - 1))
                    last.then_inc(l_ready, 1)

            @block.scalar
            def _(act):
                with act.Fori(0, NB) as i:
                    act.wait_ge(turned, i + 2)
                    nc.scalar.copy(flat(xT[:, 0]), bank[0][:, 0:D]).then_inc(xT_ready, 1)
                act.wait_ge(to_act, 1)
                if layer == 1:
                    nc.scalar.activation(prob[:, :, 0:NE], prob[:, :, 0:NE], ACT.Exp).then_inc(act_done, 1)
                    nc.scalar.activation(row[:, 2, :], lg[:, :, NE], ACT.Sigmoid).then_inc(act_done, 1)
                else:
                    nc.scalar.activation(lg[:], lg[:], ACT.Sigmoid).then_inc(act_done, 1)

            @block.vector
            def _(dve):
                bc = lambda a, n=NE: a.unsqueeze(2).broadcast_to([P, NB, n])
                nc.vector.memset(prob[:], FILL).then_inc(own, 1)
                nc.vector.memset(best[:], FILL).then_inc(own, 1)
                dve.sem_inc(taken, 1)
                with dve.Fori(0, NB) as i:
                    dve.wait_ge(l_ready, i + 1)
                    nc.vector.tensor_copy(flat(lg[:, ds(i, 1), :]), bank[1][:, 0:R]).then_inc(taken, 1)
                dve.wait_ge(taken, NB + 1)
                dve.wait_ge(own, 2)
                step = Chain(dve, own, 2)
                if layer == 1:
                    step(nc.vector.tensor_reduce(row[:, 0, :], lg[:, :, 0:NE], AX.X, ALU.max))
                    nc.vector.tensor_tensor(prob[:, :, 0:NE], lg[:, :, 0:NE], bc(row[:, 0, :]),
                                            ALU.subtract).then_inc(to_act, 1)
                    dve.wait_ge(act_done, 2)
                    step(nc.vector.tensor_reduce(row[:, 0, :], prob[:, :, 0:NE], AX.X, ALU.add))
                    step(nc.vector.reciprocal(row[:, 0, :], row[:, 0, :]))
                    step(nc.vector.tensor_tensor(prob[:, :, 0:NE], prob[:, :, 0:NE], bc(row[:, 0, :]), ALU.mult))
                    score = prob[:, :, 0:NE]
                else:
                    dve.sem_inc(to_act, 1)
                    dve.wait_ge(act_done, 1)
                    score = lg[:]
                    if layer == 2:
                        step(nc.vector.tensor_copy(prob[:, :, 0:NE], score))
                    else:
                        g4 = prob[:, :, 0:NE].rearrange("p t (g i) -> p t g i", g=4)
                        step(nc.vector.tensor_tensor(prob[:, :, 0:NE], score,
                                                     small["l3_ebias"][:].unsqueeze(1).broadcast_to([P, NB, NE]),
                                                     ALU.add))
                        hi = t("hi", [P, NB, 4, 2])
                        lo = t("lo", [P, NB, 4, 2])
                        f = lambda a: a.rearrange("p t g -> p (t g)")
                        for k in range(2):
                            step(nc.vector.tensor_tensor(hi[:, :, :, k], g4[:, :, :, 2 * k], g4[:, :, :, 2 * k + 1],
                                                         ALU.max))
                            step(nc.vector.tensor_tensor(lo[:, :, :, k], g4[:, :, :, 2 * k], g4[:, :, :, 2 * k + 1],
                                                         ALU.min))
                        g1 = t("g1", [P, NB, 4])
                        g2 = t("g2", [P, NB, 4])
                        step(nc.vector.tensor_tensor(g1[:], hi[:, :, :, 0], hi[:, :, :, 1], ALU.max))
                        step(nc.vector.tensor_tensor(g2[:], hi[:, :, :, 0], hi[:, :, :, 1], ALU.min))
                        step(nc.vector.tensor_tensor(lo[:, :, :, 0], lo[:, :, :, 0], lo[:, :, :, 1], ALU.max))
                        step(nc.vector.tensor_tensor(g2[:], g2[:], lo[:, :, :, 0], ALU.max))
                        step(nc.vector.tensor_tensor(g1[:], g1[:], g2[:], ALU.add))
                        rank = t("rank", [P, NB, 4])
                        cmp = t("cmp", [P, NB])
                        step(nc.vector.memset(rank[:], 0.0))
                        for j in range(4):
                            for g in range(j + 1, 4):
                                step(nc.vector.tensor_tensor(cmp[:], g1[:, :, j], g1[:, :, g], ALU.is_ge))
                                step(nc.vector.tensor_tensor(rank[:, :, g], rank[:, :, g], cmp[:], ALU.add))
                                step(nc.vector.tensor_tensor(cmp[:], g1[:, :, g], g1[:, :, j], ALU.is_gt))
                                step(nc.vector.tensor_tensor(rank[:, :, j], rank[:, :, j], cmp[:], ALU.add))
                        step(nc.vector.tensor_scalar(rank[:], rank[:], 1.5, None, ALU.is_lt))
                        r4 = rank[:].unsqueeze(3).broadcast_to([P, NB, 4, 4])
                        step(nc.vector.tensor_scalar(g2[:], rank[:], -1.0, -BARRED, ALU.add, ALU.mult))
                        step(nc.vector.tensor_tensor(g4, g4, r4, ALU.mult))
                        step(nc.vector.tensor_tensor(g4, g4, g2[:].unsqueeze(3).broadcast_to([P, NB, 4, 4]), ALU.add))
                for i in range(NB):
                    nc.vector.max(best[:, i, :], prob[:, i, 0:NE]).then_inc(own, 1)
                step.n += NB
                dve.wait_ge(own, 2 + step.n)
                step(nc.vector.memset(best[:, :, m["k"]:8], FILL))
                for i in range(NB):
                    nc.vector.match_replace(rep[:, i, :], best[:, i, :], prob[:, i, :], TAKEN).then_inc(own, 1)
                step.n += NB
                dve.wait_ge(own, 2 + step.n)
                w = comb[:, :, 0:NE]
                step(nc.vector.tensor_scalar(rep[:, :, 0:NE], rep[:, :, 0:NE], TAKEN, None, ALU.is_equal))
                step(nc.vector.tensor_tensor(w, rep[:, :, 0:NE], score, ALU.mult))
                step(nc.vector.tensor_reduce(row[:, 0, :], w, AX.X, ALU.add))
                if layer == 1:
                    step(nc.vector.tensor_scalar(row[:, 0, :], row[:, 0, :], 1e-9, None, ALU.max))
                if layer == 3:
                    step(nc.vector.tensor_scalar(row[:, 0, :], row[:, 0, :], 1e-20, None, ALU.add))
                step(nc.vector.reciprocal(row[:, 0, :], row[:, 0, :]))
                if layer == 3:
                    step(nc.vector.tensor_scalar(row[:, 0, :], row[:, 0, :], 2.5, None, ALU.mult))
                step(nc.vector.tensor_scalar(row[:, 0, :], row[:, 0, :], tg_f[:, layer:layer + 1], None, ALU.mult))
                step(nc.vector.tensor_tensor(w, w, bc(row[:, 0, :]), ALU.mult))
                n = m["E"] - NE
                if layer == 1:
                    step(nc.vector.tensor_scalar(row[:, 2, :], row[:, 2, :], tg_f[:, 1:2], None, ALU.mult))
                    step(nc.vector.tensor_copy(comb[:, :, NE:NE + n], bc(row[:, 2, :], n)))
                else:
                    step(nc.vector.memset(comb[:, :, NE:NE + n], 1.0))
                    step(nc.vector.tensor_scalar(comb[:, :, NE:NE + n], comb[:, :, NE:NE + n],
                                                 tg_f[:, layer:layer + 1], None, ALU.mult))

    def experts(layer):
        m = MOE[layer]
        E, I, parts = m["E"], m["I"], m["parts"]
        gu_w, dn_w, kp = moe_views(layer)
        func = ACT.Gelu if layer == 2 else ACT.Silu
        with ExitStack() as st:
            sem = lambda n: nc.alloc_semaphore(f"m{layer}_{n}")
            (staged, turned, xT_ready, gu_ready, sg_ready, h_ready, h_turned, hT_ready, y_ready, acc_done, own,
             c_turned, cT_ready, b_ready, ones_ready) = (sem(n) for n in (
                "staged", "turned", "xT", "gu", "sg", "h", "ht", "hT", "y", "acc", "own", "ct", "cT", "b", "one"))
            sg = sb(f"sg{layer}", [P, 2, I], F32, st)
            h = sb(f"h{layer}", [P, 2, I], F32, st)
            hT = sb(f"hT{layer}", [kp, 2, parts, P], F32, st)
            ones3 = sb(f"ones3{layer}", [3, P], BF16, st)
            cs = sb(f"cs{layer}", [P, 20], F32, st)
            cT = sb(f"cT{layer}", [20, P], F32, st)
            block = st.enter_context(nc.Block())
            GU, HT, Y = bank[0:2], bank[2:4], bank[4:6]
            XT = bank[6]
            if layer == 2:
                gb = gbias[:].rearrange("p (e n) -> p e n", e=E)

            @block.gpsimd
            def _(pool):
                with pool.Fori(0, NB) as t:
                    pool.wait_ge(turned, t + 1)
                    if layer == 2:
                        nc.gpsimd.tensor_copy(cs[:, 0:E], flat(comb[:, ds(t, 1), 0:E]))
                    nc.gpsimd.tensor_copy(xs[:, 0:1, :], xn[:, ds(t, 1), :]).then_inc(staged, 1)

            @block.tensor
            def _(pe):
                pe.sem_inc(turned, 1)
                pe.wait_ge(moe_loaded[layer - 1], 32)
                pe.wait_ge(ones_ready, 1)

                def gate_up(b, w, bias):
                    for c in range(C):
                        last = nc.tensor.matmul(GU[b][:, 0:2 * I], xT[:, 0, c, :], w[c], start=(c == 0),
                                                stop=(c == C - 1 and bias is None))
                    if bias is not None:
                        last = nc.tensor.matmul(GU[b][:, 0:2 * I], ones3[:], bias, start=False, stop=True)
                    last.then_inc(gu_ready, 1)

                def turn(b, at_count):
                    pe.wait_ge(h_ready, at_count)
                    for k in range(parts):
                        last = nc.tensor.transpose(HT[b][0:kp, k * P:(k + 1) * P], h[:, b, k * kp:(k + 1) * kp],
                                                   ident[:])
                    last.then_inc(h_turned, 1)

                def down(b, w, at_count):
                    pe.wait_ge(hT_ready, at_count)
                    pe.wait_ge(acc_done, at_count)
                    for k in range(parts):
                        last = nc.tensor.matmul(Y[b][:, 0:D], hT[:, b, k, :], w[k], start=(k == 0),
                                                stop=(k == parts - 1))
                    last.then_inc(y_ready, 1)

                with pe.Fori(0, NB) as t:
                    pe.wait_ge(staged, t + 1)
                    for c in range(C):
                        last = nc.tensor.transpose(XT[:, c * P:(c + 1) * P], xs[:, 0, c * P:(c + 1) * P], ident[:])
                    if layer == 2:
                        last = nc.tensor.transpose(XT[0:E, D:D + P], cs[:, 0:E], ident[:])
                    last.then_inc(turned, 1)
                    pe.wait_ge(xT_ready, t + 1)
                    if layer == 2:
                        nc.tensor.matmul(bank[7][:, 0:D], cT[0:E, :], small["l2_b2"][:], start=True,
                                         stop=True).then_inc(c_turned, 1)
                    st_w = lambda e: [gu_w[:, e, c, :] for c in range(C)]
                    st_d = lambda e: [dn_w[:, e, k, :] for k in range(parts)]
                    gate_up(0, st_w(0), gb[:, 0, :] if layer == 2 else None)
                    gate_up(1, st_w(1), gb[:, 1, :] if layer == 2 else None)
                    turn(0, t * E + 1)

                    n = (E - 2) // 2
                    with pe.Fori(0, n) as j:
                        for u in range(2):
                            gu_e = gu_w[:, 2:2 + 2 * n].rearrange("p (j u) c i -> p j u c i", u=2)
                            dn_e = dn_w[:, 0:2 * n].rearrange("p (j u) k d -> p j u k d", u=2)
                            bias = None
                            if layer == 2:
                                bias = flat(gb[:, 2:2 + 2 * n, :].rearrange("p (j u) n -> p j u n", u=2)[:, ds(j, 1), u, :])
                            gate_up(u, [flat(gu_e[:, ds(j, 1), u, c, :]) for c in range(C)], bias)
                            turn(1 - u, t * E + j * 2 + (u + 2))
                            down(u, [flat(dn_e[:, ds(j, 1), u, k, :]) for k in range(parts)], t * E + j * 2 + (u + 1))
                    if E % 2:
                        gate_up(0, st_w(E - 1), None)
                        turn(1, t * E + (E - 1))
                        down((E - 3) % 2, st_d(E - 3), t * E + (E - 2))
                    turn((E - 1) % 2, t * E + E)
                    down((E - 2) % 2, st_d(E - 2), t * E + (E - 1))
                    down((E - 1) % 2, st_d(E - 1), t * E + E)

            @block.scalar
            def _(act):
                def gate(b, at_count):
                    act.wait_ge(gu_ready, at_count)
                    nc.scalar.activation(sg[:, b, :], GU[b][:, 0:I], func).then_inc(sg_ready, 1)

                def move(b, at_count):
                    act.wait_ge(h_turned, at_count)
                    nc.scalar.copy(hT[:, b].rearrange("p k t -> p (k t)"), HT[b][0:kp, 0:parts * P]).then_inc(hT_ready, 1)

                with act.Fori(0, NB) as t:
                    act.wait_ge(turned, t + 2)
                    if layer == 2:
                        nc.scalar.copy(cT[0:E, :], XT[0:E, D:D + P])
                    nc.scalar.copy(flat(xT[:, 0]), XT[:, 0:D]).then_inc(xT_ready, 1)
                    gate(0, t * E + 1)
                    gate(1, t * E + 2)
                    move(0, t * E + 1)
                    with act.Fori(0, (E - 2) // 2) as j:
                        for u in range(2):
                            gate(u, t * E + j * 2 + (u + 3))
                            move(1 - u, t * E + j * 2 + (u + 2))
                    if E % 2:
                        gate(0, t * E + E)
                        move(1, t * E + (E - 1))
                    move((E - 1) % 2, t * E + E)

            @block.vector
            def _(dve):
                nc.vector.memset(ones3[:], 1.0).then_inc(ones_ready, 1)
                dve.sem_inc(acc_done, 2)

                def hidden(b, at_count):
                    dve.wait_ge(sg_ready, at_count)
                    nc.vector.tensor_tensor(h[:, b, :], sg[:, b, :], GU[b][:, I:2 * I], ALU.mult).then_inc(h_ready, 1)

                with dve.Fori(0, NB) as t:
                    xt = flat(x[:, ds(t, 1), :])

                    def add(b, scalar, at_count):
                        dve.wait_ge(y_ready, at_count)
                        dve.wait_ge(acc_done, at_count + 1)
                        nc.vector.scalar_tensor_tensor(xt, Y[b][:, 0:D], scalar, xt, ALU.mult,
                                                       ALU.add).then_inc(acc_done, 1)

                    if layer == 2:
                        dve.wait_ge(c_turned, t + 1)
                        nc.vector.tensor_tensor(xt, xt, bank[7][:, 0:D], ALU.add).then_inc(own, 1)
                        dve.wait_ge(own, t * 2 + 1)
                        nc.vector.scalar_tensor_tensor(xt, flat(xn[:, ds(t, 1), :]), tg_f[:, 2:3], xt, ALU.mult,
                                                       ALU.add).then_inc(own, 1)
                        dve.wait_ge(own, t * 2 + 2)
                    ct = comb[:, ds(t, 1), :].rearrange("p a e -> p (a e)")
                    hidden(0, t * E + 1)
                    hidden(1, t * E + 2)
                    n = (E - 2) // 2
                    with dve.Fori(0, n) as j:
                        for u in range(2):
                            hidden(u, t * E + j * 2 + (u + 3))
                            cu = comb[:, :, 0:2 * n].rearrange("p t (j u) -> p t j u", u=2)[:, ds(t, 1), ds(j, 1), u]
                            add(u, cu.rearrange("p a b -> p (a b)"), t * E + j * 2 + (u + 1))
                    if E % 2:
                        hidden(0, t * E + E)
                        add((E - 3) % 2, ct[:, E - 3:E - 2], t * E + (E - 2))
                    add((E - 2) % 2, ct[:, E - 2:E - 1], t * E + (E - 1))
                    add((E - 1) % 2, ct[:, E - 1:E], t * E + E)

    def store():
        with ExitStack() as st:
            block = st.enter_context(nc.Block())

            @block.sync
            def _(sp):
                sp.dma_start(io["out"], x[:]).then_inc(out_stored, 16)
                for k in range(3):
                    if STOP > (0, 4, 6)[k]:
                        sp.wait_ge(moe_loaded[k], 32)
                sp.wait_ge(out_stored, 16)

    def l0_attn():
        normalize("n0")
        decay_summary()
        normalize("n1", affine=True)
        decay_add()

    def mixture(layer):
        normalize(f"nf{layer}")
        with nc.cleanup_on_exit():
            route(layer)
            experts(layer)

    stages = [l0_attn, lambda: (normalize("n2"), linear()), lambda: (normalize("n3"), masked_attention()),
              lambda: mixture(1), lambda: (normalize("n4"), many_heads()), lambda: mixture(2),
              lambda: (normalize("n5"), channel_heads()), lambda: mixture(3)]
    setup()
    for stage in stages[:STOP]:
        stage()
    store()


def kernel(**inputs):
    import numpy as np
    import concourse.bacc as bacc
    from concourse.bass_utils import run_bass_kernel_spmd as run

    i = {k: np.asarray(v) for k, v in inputs.items()}

    def rows(a):
        return np.broadcast_to(a.reshape(1, -1), (P, a.size))

    def chunks(a):
        return a.reshape(C, P, -1).transpose(1, 0, 2)

    def gate_up(gate, up):
        gu = np.concatenate([gate, up], axis=2)
        return gu.reshape(gu.shape[0], C, P, -1).transpose(2, 0, 1, 3)

    def down(d, parts):
        return d.reshape(d.shape[0], parts, -1, D).transpose(2, 0, 1, 3)

    def join(*a):
        return np.concatenate(a, axis=0)

    tr = lambda a: a.transpose(0, 2, 1)
    cut = lambda a: a.reshape(D, 4, 176).transpose(1, 0, 2)
    Wkv = np.concatenate([i["L2_xattn_Wk"], i["L2_xattn_Wv"]], axis=0)
    arrays = {
        "x": i["x"].transpose(1, 0, 2), "ctx": i["ctx_2048"].transpose(1, 0, 2),
        "ctxT": i["ctx_2048"].reshape(NB, P, C, P).transpose(3, 0, 2, 1),
        "mask": np.broadcast_to(i["mask_BxS2_bk0"][None], (P, NB, P)),
        "g_xattn": rows(i["g_xattn"]), "g_ffn": rows(i["g_ffn"]), "decay": rows(i["L0_xattn_decay"]),
        "l0_win": chunks(i["L0_xattn_W_in"].T), "l0_bin": i["L0_xattn_b_in"].reshape(C, P).T,
        "l0_wout": chunks(i["L0_xattn_W_out"].T), "l0_bout": rows(i["L0_xattn_b_out"]),
        "l0_gamma": rows(i["L0_xattn_gamma"]), "l0_beta": rows(i["L0_xattn_beta"]),
        "l0_w": chunks(i["L0_ffn_weight"].T), "l0_scale": rows(i["L0_ffn_scale_weight"]),
        "l0_bias": rows(i["L0_ffn_bias"]),
        "l1_router": chunks(np.concatenate([i["L1_ffn_router_w"].T, i["L1_ffn_sh_gate_w"]], axis=1)),
        "l2_router": chunks(i["L2_ffn_wa"]), "l3_router": chunks(i["L3_ffn_gate_weight"].T),
        "l2_wq": chunks(i["L2_xattn_Wq"].T), "l2_wk": chunks(Wkv[0::2].T), "l2_wv": chunks(Wkv[1::2].T),
        "l2_b2": join(i["L2_ffn_rb2"], i["L2_ffn_sb2"]), "l3_gamma": rows(i["L3_xattn_gamma"]),
        "l3_ebias": rows(i["L3_ffn_expert_bias"]),
        "l2_gub": np.broadcast_to(np.concatenate([join(i["L2_ffn_rgb"], i["L2_ffn_sgb"]),
                                                  join(i["L2_ffn_rb1"], i["L2_ffn_sb1"])], axis=1).reshape(1, -1),
                                  (3, 18 * 256)),
        "l1_gu": gate_up(join(i["L1_ffn_w_gate"], cut(i["L1_ffn_sh_gate"])),
                         join(i["L1_ffn_w_up"], cut(i["L1_ffn_sh_up"]))),
        "l1_dn": down(join(i["L1_ffn_w_down"], i["L1_ffn_sh_down"].reshape(4, 176, D)), 2),
        "l2_gu": gate_up(join(i["L2_ffn_rg"], i["L2_ffn_sg"]), join(i["L2_ffn_rw1"], i["L2_ffn_sw1"])),
        "l2_dn": down(join(i["L2_ffn_rw2"], i["L2_ffn_sw2"]), 1),
        "l3_gu": gate_up(tr(join(i["L3_ffn_gate_proj"], i["L3_ffn_shared_gate"][None])),
                         tr(join(i["L3_ffn_up_proj"], i["L3_ffn_shared_up"][None]))),
        "l3_dn": down(tr(join(i["L3_ffn_down_proj"], i["L3_ffn_shared_down"][None])), 1),
    }
    nc = bacc.Bacc("TRN2", target_bir_lowering=False, num_devices=1)
    io, sent = {}, {}
    for name, a in arrays.items():
        a = np.ascontiguousarray(a)
        sent[f"in_{name}"] = a
        io[name] = nc.dram_tensor(f"in_{name}", a.shape, mybir.dt.from_np(a.dtype), kind="ExternalInput").ap()
    io["out"] = nc.dram_tensor("out_x", [P, NB, D], F32, kind="ExternalOutput").ap()
    build(nc, io)
    got = run(nc, [sent], core_ids=[0]).results[0]["out_x"]
    return got.transpose(1, 0, 2)
```

```python
from contextlib import ExitStack

import concourse.bass as bass
from concourse import mybir

F32 = mybir.dt.float32
BF16 = mybir.dt.bfloat16
U8 = mybir.dt.uint8
ALU = mybir.AluOpType
ACT = mybir.ActivationFunctionType
AX = mybir.AxisListType
ds = bass.ds

P = 128
NB = 16
D = 256
C = D // P
NE = 16
PAD = 24
FILL = -3.0e38
BARRED = -2.9e38
TAKEN = -3.2e38
LN_EPS = 1e-5
STOP = 99


PACKED = (("g_xattn", 4), ("g_ffn", 4), ("decay", 1), ("l0_bin", C), ("l0_gamma", D), ("l0_beta", D),
          ("l0_bout", D), ("l0_win", C * D), ("l0_wout", C * D), ("l0_scale", D), ("l0_bias", D), ("l0_w", C * D),
          ("l1_router", C * 17), ("l2_router", C * 16), ("l3_router", C * 16), ("l3_gamma", 1), ("l3_ebias", 16),
          ("l2_wq", C * D), ("l2_wk", C * D), ("l2_wv", C * D))
CHUNKED = ("l0_win", "l0_wout", "l0_w", "l1_router", "l2_router", "l3_router", "l2_wq", "l2_wk", "l2_wv")


class Chain:

    def __init__(self, eng, sem, base=0):
        self.eng, self.sem, self.base, self.n = eng, sem, base, 0

    def __call__(self, ins):
        ins.then_inc(self.sem, 1)
        self.n += 1
        self.eng.wait_ge(self.sem, self.base + self.n)
        return ins


def flat(ap):
    return ap.rearrange("p a b -> p (a b)")


class At:

    def __init__(self, k, j=None, steps=NB // 2 - 1):
        self.k, self.j, self.steps = k, j, steps
        self.u = k % 2

    def count(self, each, plus=0):
        if self.j is None:
            return self.k * each + plus
        return self.j * (2 * each) + (self.k * each + plus)

    def of(self, view):
        view = view[:]
        if self.j is None:
            return view[:, self.k:self.k + 1]
        lo = self.k - self.k % 2
        dims = "abcd"[:len(view.shape) - 2]
        pairs = view[:, lo:lo + 2 * self.steps].rearrange(f"p (j u) {' '.join(dims)} -> p j u {' '.join(dims)}", u=2)
        return pairs[:, ds(self.j, 1), self.k % 2]


def each_batch(eng, body):
    body(None, At(0), At(1))
    with eng.Fori(0, NB // 2 - 1) as j:
        body(At(0, j), At(1, j), At(2, j))
        body(At(1, j), At(2, j), At(3, j))
    body(At(NB - 2), At(NB - 1), None)


def each_batch_far(eng, body):
    steps = NB // 2 - 2
    body(None, At(0), At(1), At(2))
    with eng.Fori(0, steps) as j:
        body(*(At(k, j, steps) for k in range(4)))
        body(*(At(k, j, steps) for k in range(1, 5)))
    body(*(At(k) for k in range(NB - 4, NB)))
    body(At(NB - 3), At(NB - 2), At(NB - 1), None)
    body(At(NB - 2), At(NB - 1), None, None)


def build(nc, io):
    with ExitStack() as top:
        _build(nc, io, top)


def _build(nc, io, top):
    def sb(name, shape, dt=F32, at=None):
        return (at or top).enter_context(nc.sbuf_tensor(name, shape, dt))

    bank = [top.enter_context(nc.psum_tensor(f"bank{i}", [P, 512], F32)) for i in range(8)]
    x = sb("x", [P, NB, D])
    xn = sb("xn", [P, NB, D])
    ctx = sb("ctx", [P, NB, D])
    ctxT = sb("ctxT", [P, NB, C, P])
    weights = sb("weights", [P, 24320])
    ident = sb("ident", [P, P])
    ones = sb("ones", [P, P])
    neg_half = sb("neg_half", [P, 64])
    stats = sb("stats", [P, NB, 6])
    var = sb("var", [P, 2, NB])
    nmean = sb("nmean", [P, NB])
    rstd = sb("rstd", [P, NB])
    comb = sb("comb", [P, NB, 20])
    xs = sb("xs", [P, 2, D])
    xT = sb("xT", [P, 2, C, P])
    pack = sb("pack", [P, sum(n for _, n in PACKED)])
    small, at = {"mask": sb("mask", [P, NB, P], U8), "l2_b2": sb("l2_b2", [18, D])}, 0
    for k, n in PACKED:
        view = pack[:, at:at + n]
        small[k] = view.rearrange("p (c n) -> p c n", c=C) if k in CHUNKED else view
        at += n
    gbias = sb("gbias", [3, 18 * 256], BF16)
    tg_x = sb("tg_x", [P, 4])
    tg_f = sb("tg_f", [P, 4])

    NCH, CH = 6, 18 * 256 // 6
    bias_raw = sb("bias_raw", [3, CH])
    x_loaded, ctx_loaded, ctxT_loaded, pack_loaded, rest_loaded = (
        top.enter_context(nc.semaphore(n)) for n in ("x_loaded", "ctx_loaded", "ctxT_loaded", "pack_loaded",
                                                     "rest_loaded"))
    moe_loaded = [top.enter_context(nc.semaphore(f"moe_loaded{i}")) for i in range(3)]
    out_stored = top.enter_context(nc.semaphore("out_stored"))

    MOE = {1: dict(E=20, I=176, parts=2, k=4), 2: dict(E=18, I=128, parts=1, k=2), 3: dict(E=17, I=128, parts=1, k=4)}

    def moe_views(layer):
        m = MOE[layer]
        n = m["E"] * C * 2 * m["I"]
        kp = m["I"] // m["parts"]
        gu = weights[:, 0:n].rearrange("p (e c i) -> p e c i", e=m["E"], c=C)
        dn = weights[0:kp, n:n + m["E"] * m["parts"] * D].rearrange("p (e k d) -> p e k d", e=m["E"], k=m["parts"])
        return gu, dn, kp

    def load_experts(eng, layer):
        gu, dn, _ = moe_views(layer)
        eng.dma_start(gu, io[f"l{layer}_gu"]).then_inc(moe_loaded[layer - 1], 16)
        eng.dma_start(dn, io[f"l{layer}_dn"]).then_inc(moe_loaded[layer - 1], 16)

    def carver():
        at = [18 * (2 * D + D)]

        def carve(shape):
            n = 1
            for k in shape[1:]:
                n *= k
            view = weights[0:shape[0], at[0]:at[0] + n]
            at[0] += n
            assert at[0] <= 24320
            if len(shape) > 2:
                names = "abcd"[:len(shape) - 1]
                view = view.rearrange(f"p ({' '.join(names)}) -> p {' '.join(names)}",
                                      **{k: v for k, v in zip(names, shape[1:])})
            return view
        return carve

    def setup():
        with ExitStack() as st:
            sem = lambda n: st.enter_context(nc.semaphore(n))
            cleared = sem("su_cleared")
            block = st.enter_context(nc.Block())

            @block.sync
            def _(sp):
                sp.dma_start(x[:], io["x"]).then_inc(x_loaded, 16)
                sp.dma_start(ctx[:], io["ctx"]).then_inc(ctx_loaded, 16)
                sp.dma_start(ctxT[:], io["ctxT"]).then_inc(ctxT_loaded, 16)
                load_experts(sp, 1)

            @block.scalar
            def _(act):
                act.dma_start(pack[:], io["pack"]).then_inc(pack_loaded, 16)
                act.dma_start(small["mask"][:], io["mask"]).then_inc(rest_loaded, 16)
                act.dma_start(small["l2_b2"][:], io["l2_b2"]).then_inc(rest_loaded, 16)
                act.wait_ge(pack_loaded, 16)
                nc.scalar.activation(tg_x[:], small["g_xattn"], ACT.Tanh)
                nc.scalar.activation(tg_f[:], small["g_ffn"], ACT.Tanh)

            @block.gpsimd
            def _(pool):
                nc.gpsimd.memset(ident[:], 0.0).then_inc(cleared, 1)
                nc.gpsimd.memset(ones[:], 1.0)
                nc.gpsimd.memset(neg_half[:], -0.5)
                pool.wait_ge(cleared, 1)
                nc.gpsimd.affine_select(out=ident[:], in_=ident[:], compare_op=ALU.not_equal, fill=1.0, base=0,
                                        pattern=[[-1, P]], channel_multiplier=1)

            @block.vector
            def _(dve):
                dve.wait_ge(x_loaded, 16)
                with dve.Fori(0, NB) as t:
                    nc.vector.bn_stats(flat(stats[:, ds(t, 1), :]), flat(x[:, ds(t, 1), :]))

    def finish_vector(dve, own, var_ready, rstd_ready):
        nc.vector.tensor_tensor(nmean[:], stats[:, :, 1], stats[:, :, 4], ALU.add).then_inc(own, 1)
        nc.vector.tensor_tensor(var[:, 0, :], stats[:, :, 1], stats[:, :, 4], ALU.subtract).then_inc(own, 1)
        nc.vector.tensor_tensor(var[:, 1, :], stats[:, :, 2], stats[:, :, 5], ALU.add).then_inc(own, 1)
        dve.wait_ge(own, 3)
        nc.vector.tensor_tensor(var[:, 0, :], var[:, 0, :], var[:, 0, :], ALU.mult).then_inc(own, 1)
        nc.vector.tensor_scalar(var[:, 1, :], var[:, 1, :], 1.0 / D, LN_EPS, ALU.mult, ALU.add).then_inc(own, 1)
        nc.vector.tensor_scalar(nmean[:], nmean[:], -0.5, None, ALU.mult).then_inc(own, 1)
        dve.wait_ge(own, 6)
        nc.vector.scalar_tensor_tensor(var[:, 1, :], var[:, 0, :], 0.25, var[:, 1, :], ALU.mult,
                                       ALU.add).then_inc(var_ready, 1)
        dve.wait_ge(rstd_ready, 1)

    def finish_pool(pool, var_ready, rstd_ready):
        pool.wait_ge(var_ready, 1)
        nc.gpsimd.tensor_tensor(rstd[:], var[:, 1, :], neg_half[:, 0:NB], ALU.pow).then_inc(rstd_ready, 1)

    def norm_tile(out, src, t):
        return nc.vector.tensor_scalar(out, t.of(src).rearrange("p a d -> p (a d)"),
                                       t.of(nmean[:]), t.of(rstd[:]), ALU.add, ALU.mult)

    def normalize(name):
        with ExitStack() as st:
            own, var_ready, rstd_ready = (st.enter_context(nc.semaphore(f"{name}_{n}")) for n in ("own", "var", "rs"))
            block = st.enter_context(nc.Block())

            @block.vector
            def _(dve):
                finish_vector(dve, own, var_ready, rstd_ready)
                with dve.Fori(0, NB) as t:
                    nc.vector.tensor_scalar(xn[:, ds(t, 1), :], x[:, ds(t, 1), :], nmean[:, ds(t, 1)],
                                            rstd[:, ds(t, 1)], ALU.add, ALU.mult)

            @block.gpsimd
            def _(pool):
                finish_pool(pool, var_ready, rstd_ready)

    def decay_attention():
        with ExitStack() as st:
            sem = lambda n: st.enter_context(nc.semaphore(f"l0a_{n}"))
            own, pe_done, e_ready, summed, cw_ready, sumT_ready, inT_ready = (
                sem(n) for n in ("own", "pe", "e", "summed", "cw", "sumT", "inT"))
            fin = [[sem(f"{n}{i}") for n in ("fin", "var", "rstd")] for i in range(2)]
            based = sem("based")
            K = sb("K", [P, 1], F32, st)
            powers = sb("powers", [P, P], F32, st)
            kbc = sb("kbc", [P, P], F32, st)
            cw = sb("cw", [P, 2], F32, st)
            bb = sb("bb", [P, C], F32, st)
            sumT = sb("sumT", [P, C, NB], F32, st)
            inT = sb("inT", [P, C, NB], F32, st)
            gg = sb("l0b_gg", [P, 2, D], F32, st)
            tmp = sb("l0b_tmp", [P, 2, D], F32, st)
            block = st.enter_context(nc.Block())

            @block.scalar
            def _(act):
                act.wait_ge(pack_loaded, 16)
                nc.scalar.activation(K[:], small["decay"], ACT.Exp, scale=-1.0).then_inc(e_ready, 1)

            @block.vector
            def _(dve):
                step = Chain(dve, own)
                dve.wait_ge(e_ready, 1)
                step(nc.vector.tensor_scalar(K[:], K[:], 1.0, None, ALU.add))
                step(nc.vector.reciprocal(K[:], K[:]))
                step(nc.vector.tensor_scalar(kbc[:], ones[:], K[:], None, ALU.mult))
                step(nc.vector.tensor_tensor_scan(powers[:], kbc[:], ident[:], 0.0, ALU.mult, ALU.add))
                step(nc.vector.tensor_reduce(cw[:, 0:1], powers[:], AX.X, ALU.add))
                nc.vector.tensor_scalar(cw[:, 0:1], cw[:, 0:1], 1.0 / P, None, ALU.mult).then_inc(cw_ready, 1)
                finish_vector(dve, *fin[0])
                with dve.Fori(0, NB) as t:
                    nc.vector.tensor_scalar(xn[:, ds(t, 1), :], x[:, ds(t, 1), :], nmean[:, ds(t, 1)],
                                            rstd[:, ds(t, 1)], ALU.add, ALU.mult).then_inc(based, 1)
                step(nc.vector.tensor_scalar(gg[:, 0, :], small["l0_gamma"], tg_x[:, 0:1], None, ALU.mult))
                nc.vector.tensor_scalar(gg[:, 1, :], small["l0_beta"], tg_x[:, 0:1], None, ALU.mult).then_inc(based, 1)
                dve.wait_ge(pe_done, 1)
                step(nc.vector.tensor_copy(cw[:, 1:2], bank[0][:, 32:33]))
                nc.vector.tensor_copy(sumT[:], bank[0][:, 0:32].rearrange("p (b c) -> p c b", c=C)).then_inc(sumT_ready, 1)
                dve.wait_ge(pe_done, 2)
                step(nc.vector.tensor_scalar(bb[:], small["l0_bin"], cw[:, 1:2], None, ALU.mult))
                for c in range(C):
                    nc.vector.tensor_scalar(inT[:, c, :], bank[1][:, c * NB:(c + 1) * NB], bb[:, c:c + 1], None,
                                            ALU.add).then_inc(inT_ready, 1)
                dve.wait_ge(based, NB)
                for b in range(NB):
                    dve.wait_ge(pe_done, 3 + b)
                    nc.vector.tensor_tensor(xn[:, b, :], xn[:, b, :], bank[2 + b % 4][:, 0:D], ALU.add).then_inc(summed, 1)
                    if b:
                        dve.wait_ge(summed, b)
                        nc.vector.bn_stats(stats[:, b - 1, :], xn[:, b - 1, :])
                dve.wait_ge(summed, NB)
                step(nc.vector.bn_stats(stats[:, NB - 1, :], xn[:, NB - 1, :]))
                finish_vector(dve, *fin[1])
                dve.wait_ge(based, 2 * NB + 1)
                base = step.n
                with dve.Fori(0, NB) as t:
                    step = Chain(dve, own, t * 3 + base)
                    xt = flat(x[:, ds(t, 1), :])
                    step(nc.vector.tensor_scalar(tmp[:, 0, :], flat(xn[:, ds(t, 1), :]), nmean[:, ds(t, 1)],
                                                 rstd[:, ds(t, 1)], ALU.add, ALU.mult))
                    step(nc.vector.tensor_tensor(tmp[:, 0, :], tmp[:, 0, :], gg[:, 0, :], ALU.mult))
                    step(nc.vector.tensor_tensor(xt, xt, tmp[:, 0, :], ALU.add))
                    nc.vector.bn_stats(flat(stats[:, ds(t, 1), :]), xt)

            @block.gpsimd
            def _(pool):
                finish_pool(pool, *fin[0][1:])
                pool.wait_ge(based, NB + 1)
                with pool.Fori(0, NB) as t:
                    nc.gpsimd.tensor_tensor(flat(x[:, ds(t, 1), :]), flat(x[:, ds(t, 1), :]), gg[:, 1, :],
                                            ALU.add).then_inc(based, 1)
                finish_pool(pool, *fin[1][1:])

            @block.tensor
            def _(pe):
                pe.wait_ge(cw_ready, 1)
                pe.wait_ge(ctx_loaded, 16)
                nc.tensor.matmul(bank[0][:, 32:33], ones[:], cw[:, 0:1], start=True, stop=True)
                for b in range(NB):
                    for c in range(C):
                        last = nc.tensor.matmul(bank[0][:, b * C + c:b * C + c + 1], ctx[:, b, c * P:(c + 1) * P],
                                                cw[:, 0:1], start=True, stop=True)
                last.then_inc(pe_done, 1)
                pe.wait_ge(sumT_ready, 1)
                for e in range(C):
                    for c in range(C):
                        last = nc.tensor.matmul(bank[1][:, e * NB:(e + 1) * NB],
                                                small["l0_win"][:, c, e * P:(e + 1) * P], sumT[:, c, :],
                                                start=(c == 0), stop=(c == C - 1))
                last.then_inc(pe_done, 1)
                pe.wait_ge(inT_ready, 2)
                for b in range(NB):
                    if b >= 4:
                        pe.wait_ge(summed, b - 3)
                    for c in range(C):
                        nc.tensor.matmul(bank[2 + b % 4][:, 0:D], inT[:, c, b:b + 1].broadcast_to([P, P]),
                                         small["l0_wout"][:, c, :], start=(c == 0), stop=False)
                    nc.tensor.matmul(bank[2 + b % 4][:, 0:D], ones[0:1, :], small["l0_bout"][0:1, :], start=False,
                                     stop=True).then_inc(pe_done, 1)

    def linear():
        with ExitStack() as st:
            sem = lambda n: st.enter_context(nc.semaphore(f"l0f_{n}"))
            normed, turned, xT_ready, y_ready, own, added, w_ready, *fin = (
                sem(n) for n in ("normed", "turned", "xT", "y", "own", "added", "w", "fin", "var", "rstd"))
            block = st.enter_context(nc.Block())
            w = small["l0_w"]

            @block.gpsimd
            def _(pool):
                finish_pool(pool, *fin[1:])

            @block.tensor
            def _(pe):
                def turn(t):
                    pe.wait_ge(normed, t.count(1, 1))
                    for c in range(C):
                        last = nc.tensor.transpose(bank[t.u][:, c * P:(c + 1) * P], xs[:, t.u, c * P:(c + 1) * P],
                                                   ident[:])
                    last.then_inc(turned, 1)

                def body(prev, t, nxt):
                    if prev is None:
                        turn(t)
                        pe.wait_ge(w_ready, 4)
                    if nxt:
                        turn(nxt)
                    pe.wait_ge(xT_ready, t.count(1, 1))
                    if prev:
                        pe.wait_ge(added, t.count(1, 0))
                    for c in range(C):
                        nc.tensor.matmul(bank[2 + t.u][:, 0:D], xT[:, t.u, c, :], w[:, c, :], start=(c == 0),
                                         stop=False)
                    nc.tensor.matmul(bank[2 + t.u][:, 0:D], ones[0:1, :], small["l0_bias"][0:1, :], start=False,
                                     stop=True).then_inc(y_ready, 1)
                each_batch(pe, body)

            @block.scalar
            def _(act):
                def body(prev, t, nxt):
                    act.wait_ge(turned, t.count(1, 1))
                    nc.scalar.copy(flat(xT[:, t.u]), bank[t.u][:, 0:D]).then_inc(xT_ready, 1)
                each_batch(act, body)

            @block.vector
            def _(dve):
                finish_vector(dve, *fin)
                step = Chain(dve, w_ready)
                for c in range(C):
                    step(nc.vector.tensor_tensor(w[:, c, :], w[:, c, :], small["l0_scale"], ALU.mult))
                step(nc.vector.tensor_scalar(flat(w), flat(w), tg_f[:, 0:1], None, ALU.mult))
                step(nc.vector.tensor_scalar(small["l0_bias"], small["l0_bias"], tg_f[:, 0:1], None, ALU.mult))

                dve.sem_inc(added, 1)

                def body(prev, t, nxt):
                    if prev is None:
                        norm_tile(xs[:, 0, :], x, t).then_inc(normed, 1)
                    if nxt:
                        if prev:
                            dve.wait_ge(turned, t.count(1, 0))
                        norm_tile(xs[:, nxt.u, :], x, nxt).then_inc(normed, 1)
                    xt = flat(t.of(x))
                    dve.wait_ge(y_ready, t.count(1, 1))
                    nc.vector.tensor_tensor(xt, xt, bank[2 + t.u][:, 0:D], ALU.add).then_inc(added, 1)
                    dve.wait_ge(added, t.count(1, 2))
                    nc.vector.bn_stats(flat(t.of(stats)), xt)
                each_batch(dve, body)

    def masked_attention():
        with ExitStack() as st:
            sem = lambda n: st.enter_context(nc.semaphore(f"l1a_{n}"))
            (normed, turned, xT_ready, s_ready, shift_ready, exp_ready, e_turned, eT_ready, y_ready, own,
             added, *fin) = (sem(n) for n in ("normed", "turned", "xT", "s", "shift", "exp", "et", "eT", "y", "own",
                                              "added", "fin", "var", "rstd"))
            score = sb("score", [P, 2, P], F32, st)
            neg = sb("neg", [P, P], F32, st)
            shift = sb("shift", [P, 2], F32, st)
            total = sb("total", [P, 2], F32, st)
            factor = sb("factor", [P, 2], F32, st)
            kept = sb("kept", [P, NB], F32, st)
            e = sb("e", [P, 2, P], F32, st)
            eT = sb("eT", [P, 2, P], F32, st)
            block = st.enter_context(nc.Block())
            mask = small["mask"]
            part = [sb(f"bias_part{i}", [3, CH], BF16, st) for i in range(2)]
            b_in, b_own = sem("bin"), sem("bown")

            @block.sync
            def _(sp):
                for i in range(NCH):
                    if i:
                        sp.wait_ge(b_own, 7 * i)
                    sp.dma_start(bias_raw[:], io["l2_gub"][:, i * CH:(i + 1) * CH]).then_inc(b_in, 16)

            @block.gpsimd
            def _(pool):
                finish_pool(pool, *fin[1:])
                step = Chain(pool, b_own)
                for i in range(NCH):
                    pool.wait_ge(b_in, 16 * (i + 1))
                    cols = slice(i * CH, (i + 1) * CH)
                    step(nc.gpsimd.tensor_copy(part[0][:], bias_raw[:]))
                    step(nc.gpsimd.tensor_tensor(bias_raw[:], bias_raw[:], part[0][:], ALU.subtract))
                    step(nc.gpsimd.tensor_copy(part[1][:], bias_raw[:]))
                    step(nc.gpsimd.tensor_tensor(bias_raw[:], bias_raw[:], part[1][:], ALU.subtract))
                    step(nc.gpsimd.tensor_copy(gbias[0:3, cols], bias_raw[:]))
                    step(nc.gpsimd.tensor_copy(gbias[0:2, cols], part[1][0:2, :]))
                    step(nc.gpsimd.tensor_copy(gbias[0:1, cols], part[0][0:1, :]))

            @block.tensor
            def _(pe):
                pe.wait_ge(ctxT_loaded, 16)

                def scores(b):
                    pe.wait_ge(normed, b.count(1, 1))
                    for c in range(C):
                        last = nc.tensor.transpose(bank[b.u][:, c * P:(c + 1) * P], xs[:, b.u, c * P:(c + 1) * P],
                                                   ident[:])
                    last.then_inc(turned, 1)
                    pe.wait_ge(xT_ready, b.count(1, 1))
                    for c in range(C):
                        last = nc.tensor.matmul(bank[2 + b.u][:, 0:P], xT[:, b.u, c, :], flat(b.of(ctxT)[:, :, c, :]),
                                                start=(c == 0), stop=(c == C - 1))
                    last.then_inc(s_ready, 1)

                def body(prev, b, nxt):
                    if prev is None:
                        scores(b)
                    if nxt:
                        scores(nxt)
                    pe.wait_ge(exp_ready, b.count(1, 1))
                    nc.tensor.transpose(bank[4 + b.u][:, 0:P], e[:, b.u, :], ident[:]).then_inc(e_turned, 1)
                    pe.wait_ge(eT_ready, b.count(1, 1))
                    nc.tensor.matmul(bank[6 + b.u][:, 0:D], eT[:, b.u, :], flat(b.of(ctx)), start=True,
                                     stop=True).then_inc(y_ready, 1)
                each_batch(pe, body)

            @block.scalar
            def _(act):
                def copy(b):
                    act.wait_ge(turned, b.count(1, 1))
                    nc.scalar.copy(flat(xT[:, b.u]), bank[b.u][:, 0:D]).then_inc(xT_ready, 1)

                def body(prev, b, nxt):
                    if prev is None:
                        copy(b)
                    if nxt:
                        copy(nxt)
                    act.wait_ge(shift_ready, b.count(1, 1))
                    nc.scalar.activation(e[:, b.u, :], score[:, b.u, :], ACT.Exp, bias=shift[:, b.u:b.u + 1],
                                         accum_out=total[:, b.u:b.u + 1]).then_inc(exp_ready, 1)
                each_batch(act, body)

            @block.vector
            def _(dve):
                finish_vector(dve, *fin)
                dve.wait_ge(rest_loaded, 32)
                step = Chain(dve, own)
                step(nc.vector.tensor_reduce(kept[:], mask[:], AX.X, ALU.max))
                step(nc.vector.tensor_scalar(kept[:], kept[:], tg_x[:, 1:2], None, ALU.mult))

                def masked(b, base):
                    step = Chain(dve, own, base)
                    mk = flat(b.of(mask))
                    step(nc.vector.tensor_scalar(neg[:], mk, -1.0, 1e30, ALU.add, ALU.mult))
                    dve.wait_ge(s_ready, b.count(1, 1))
                    step(nc.vector.scalar_tensor_tensor(score[:, b.u, :], bank[2 + b.u][:, 0:P], D ** -0.5, mk,
                                                        ALU.mult, ALU.mult))
                    step(nc.vector.tensor_tensor(score[:, b.u, :], score[:, b.u, :], neg[:], ALU.add))
                    step(nc.vector.tensor_reduce(shift[:, b.u:b.u + 1], score[:, b.u, :], AX.X, ALU.max))
                    nc.vector.tensor_scalar(shift[:, b.u:b.u + 1], shift[:, b.u:b.u + 1], -1.0, None,
                                            ALU.mult).then_inc(shift_ready, 1)

                def body(prev, b, nxt):
                    if prev is None:
                        norm_tile(xs[:, b.u, :], x, b).then_inc(normed, 1)
                        norm_tile(xs[:, nxt.u, :], x, nxt).then_inc(normed, 1)
                        masked(b, 2)
                    elif nxt:
                        norm_tile(xs[:, nxt.u, :], x, nxt).then_inc(normed, 1)
                    dve.wait_ge(e_turned, b.count(1, 1))
                    nc.vector.tensor_copy(eT[:, b.u, :], bank[4 + b.u][:, 0:P]).then_inc(eT_ready, 1)
                    if nxt:
                        masked(nxt, nxt.count(6))
                    at = 10 if nxt else 6
                    nc.vector.reciprocal(factor[:, b.u:b.u + 1], total[:, b.u:b.u + 1]).then_inc(own, 1)
                    dve.wait_ge(own, b.count(6, at + 1))
                    nc.vector.tensor_scalar(factor[:, b.u:b.u + 1], factor[:, b.u:b.u + 1],
                                            b.of(kept), None, ALU.mult).then_inc(own, 1)
                    dve.wait_ge(own, b.count(6, at + 2))
                    dve.wait_ge(y_ready, b.count(1, 1))
                    nc.vector.scalar_tensor_tensor(flat(b.of(x)), bank[6 + b.u][:, 0:D], factor[:, b.u:b.u + 1],
                                                   flat(b.of(x)), ALU.mult, ALU.add).then_inc(added, 1)
                    dve.wait_ge(added, b.count(1, 1))
                    nc.vector.bn_stats(flat(b.of(stats)), flat(b.of(x)))
                each_batch(dve, body)

    def many_heads():
        H, HD, W = 32, 8, 8 * 9
        carve = carver()
        with ExitStack() as st:
            sem = lambda n: st.enter_context(nc.semaphore(f"l2a_{n}"))
            (normed, c_staged, turned, xT_ready, p_ready, squared, sum_ready, pow_done, v_ready, qk_ready, qk_turned,
             k_ready, q_spread, s_ready, e_ready, pv_done, pvT_ready, turned_back, o_ready, added, own, mask_ready,
             *fin) = (
                sem(n) for n in ("normed", "cs", "turned", "xT", "p", "sq", "sum", "pow", "v", "qk", "qkt", "k",
                                 "q", "s", "e", "pv", "pvT", "back", "o", "added", "own", "mk", "fin", "var", "rstd"))
            sq = flat(small["l0_win"])
            qk = small["l0_wout"]
            pvT = flat(small["l0_w"])
            cT = carve([P, 2, C, P])
            ss = carve([P, 2 * H])
            rn = carve([P, 2 * H])
            kT = carve([P, 2, C, P])
            qm = [carve([P, C, 4, P]) for _ in range(2)]
            rowmask = carve([P, 4])
            v = [carve([P, H * (W + HD + 1)]) for _ in range(2)]
            e = carve([P, 2, 4, P])
            inv = carve([P, H])
            o = carve([P, H, HD])
            block = st.enter_context(nc.Block())
            PROJ, Q_T, S, PV = (bank[1], bank[5]), bank[2], bank[3:5], bank[6:8]
            own_columns = [v[i][:].rearrange("p (h w) -> p h w", h=H) for i in range(2)]

            @block.sync
            def _(sp):
                load_experts(sp, 2)

            @block.gpsimd
            def _(pool):
                nc.gpsimd.memset(rowmask[:], 1.0).then_inc(mask_ready, 1)
                for i in range(2):
                    nc.gpsimd.memset(v[i][:], 0.0).then_inc(mask_ready, 1)
                pool.wait_ge(mask_ready, 3)
                for i in range(2):
                    nc.gpsimd.memset(own_columns[i][:, :, HD], 1.0).then_inc(mask_ready, 1)
                pool.wait_ge(mask_ready, 5)
                for g in range(4):
                    rm = rowmask[32 * g:32 * g + 32]
                    nc.gpsimd.affine_select(out=rm, in_=rm, compare_op=ALU.is_ge, fill=0.0, base=0,
                                            pattern=[[-HD, 4]], channel_multiplier=1).then_inc(mask_ready, 1)
                pool.wait_ge(mask_ready, 9)
                for g in range(4):
                    rm = rowmask[32 * g:32 * g + 32]
                    nc.gpsimd.affine_select(out=rm, in_=rm, compare_op=ALU.is_ge, fill=0.0, base=HD - 1,
                                            pattern=[[HD, 4]], channel_multiplier=-1).then_inc(mask_ready, 1)
                pool.wait_ge(mask_ready, 13)
                finish_pool(pool, *fin[1:])

                def roots(b, free):
                    if free is not None:
                        pool.wait_ge(qk_turned, free)
                    nc.gpsimd.tensor_copy(cT[:, b.u].rearrange("p c m -> p (c m)"),
                                          b.of(ctxT).rearrange("p a c m -> p (a c m)")).then_inc(c_staged, 1)
                    pool.wait_ge(sum_ready, b.count(1, 1))
                    nc.gpsimd.tensor_tensor(rn[:], ss[:], neg_half[:], ALU.pow).then_inc(pow_done, 1)

                def body(prev, b, nxt, far):
                    if prev is None:
                        roots(b, None)
                        roots(nxt, None)
                    if far:
                        roots(far, b.count(1, 1))
                each_batch_far(pool, body)

            @block.tensor
            def _(pe):
                def turn(b):
                    pe.wait_ge(normed, b.count(1, 1))
                    for c in range(C):
                        last = nc.tensor.transpose(bank[0][:, c * P:(c + 1) * P], xs[:, b.u, c * P:(c + 1) * P],
                                                   ident[:])
                    last.then_inc(turned, 1)

                def product(out, lhs, w):
                    for c in range(C):
                        last = nc.tensor.matmul(out, lhs[:, c, :], small[w][:, c, :], start=(c == 0),
                                                stop=(c == C - 1))
                    return last

                def project(b):
                    pe.wait_ge(c_staged, b.count(1, 1))
                    pe.wait_ge(xT_ready, b.count(1, 1))
                    product(PROJ[b.u][:, 0:D], xT[:, 0], "l2_wq")
                    product(PROJ[b.u][:, D:2 * D], cT[:, b.u], "l2_wk").then_inc(p_ready, 1)

                def turn_qk(b):
                    product(bank[0][:, D:2 * D], cT[:, b.u], "l2_wv")
                    pe.wait_ge(qk_ready, b.count(1, 1))
                    for i, out in enumerate((Q_T, bank[0])):
                        for c in range(C):
                            last = nc.tensor.transpose(out[:, c * P:(c + 1) * P], qk[:, i, c * P:(c + 1) * P], ident[:])
                    last.then_inc(qk_turned, 1)

                def turn_back(b):
                    pe.wait_ge(pvT_ready, b.count(1, 1))
                    for t in range(4):
                        last = nc.tensor.transpose(PV[b.u][:, t * W:(t + 1) * W], pvT[0:W, t * P:(t + 1) * P],
                                                   ident[0:W, 0:W])
                    last.then_inc(turned_back, 1)

                def body(prev, b, nxt, far):
                    if prev is None:
                        turn(b)
                        project(b)
                        turn(nxt)
                        project(nxt)
                        turn_qk(b)
                    for n in range(8 + 1):
                        if n < 8:
                            c, g = divmod(n, 4)
                            rows = slice(32 * g, 32 * g + 32)
                            if n == 0:
                                pe.wait_ge(q_spread, b.count(2, 2))
                                pe.wait_ge(k_ready, b.count(1, 1))
                            nc.tensor.matmul(S[n % 2][:], kT[rows, b.u, c, :],
                                             qm[b.u][rows, c].rearrange("p j q -> p (j q)"), start=True, stop=True,
                                             tile_position=(32 * g, 0)).then_inc(s_ready, 1)
                        if n >= 1:
                            m = n - 1
                            pe.wait_ge(e_ready, b.count(8, m + 1))
                            if m == 0:
                                pe.wait_ge(v_ready, b.count(1, 1))
                            for j in range(4):
                                t, i = divmod(4 * m + j, 8)
                                at = t * 8 * (W + HD + 1) + i * W
                                last = nc.tensor.matmul(PV[b.u][0:W, t * P:(t + 1) * P], v[b.u][:, at:at + W],
                                                        e[:, m % 2, j, :], start=(i == 0), stop=(i == 7))
                            last.then_inc(pv_done, 1)
                        if n == 1 and far:
                            turn(far)
                        if n == 2 and far:
                            project(far)
                        if n == 2 and prev:
                            turn_back(prev)
                        if n == 5 and nxt:
                            turn_qk(nxt)
                    if nxt is None:
                        turn_back(b)
                each_batch_far(pe, body)

            @block.scalar
            def _(act):
                def copy_x(b):
                    act.wait_ge(turned, b.count(1, 1))
                    nc.scalar.copy(flat(xT[:, 0]), bank[0][:, 0:D]).then_inc(xT_ready, 1)

                def square(b):
                    act.wait_ge(p_ready, b.count(1, 1))
                    nc.scalar.activation(sq, PROJ[b.u][:], ACT.Square).then_inc(squared, 1)

                def copy_v_k(b):
                    act.wait_ge(qk_turned, b.count(1, 1))
                    nc.scalar.copy(own_columns[b.u][:, :, 0:HD],
                                   bank[0][:, D:2 * D].rearrange("p (h d) -> p h d", h=H)).then_inc(v_ready, 1)
                    nc.scalar.copy(flat(kT[:, b.u]), bank[0][:, 0:D]).then_inc(k_ready, 1)

                def copy_sums(b):
                    act.wait_ge(pv_done, b.count(8, 8))
                    nc.scalar.copy(pvT[0:W, :], PV[b.u][0:W, :]).then_inc(pvT_ready, 1)

                act.wait_ge(mask_ready, 5)

                def body(prev, b, nxt, far):
                    if prev is None:
                        copy_x(b)
                        square(b)
                        copy_x(nxt)
                        act.wait_ge(sum_ready, 1)
                        square(nxt)
                        copy_v_k(b)
                    for n in range(8):
                        act.wait_ge(s_ready, b.count(8, n + 1))
                        nc.scalar.activation(e[:, n % 2].rearrange("p j q -> p (j q)"), S[n % 2][:], ACT.Exp,
                                             scale=HD ** -0.5).then_inc(e_ready, 1)
                        if n == 0 and prev:
                            copy_sums(prev)
                        if n == 1 and far:
                            copy_x(far)
                        if n == 3 and far:
                            square(far)
                        if n == 5 and nxt:
                            copy_v_k(nxt)
                    if nxt is None:
                        copy_sums(b)
                each_batch_far(act, body)

            @block.vector
            def _(dve):
                finish_vector(dve, *fin)
                dve.wait_ge(mask_ready, 13)

                def norm(b):
                    norm_tile(xs[:, b.u, :], x, b).then_inc(normed, 1)

                def sums(b):
                    dve.wait_ge(squared, b.count(1, 1))
                    nc.vector.tensor_reduce(ss[:], sq.rearrange("p (h d) -> p h d", d=HD), AX.X,
                                            ALU.add).then_inc(own, 1)
                    dve.wait_ge(own, b.count(1, 1))
                    nc.vector.tensor_scalar(ss[:], ss[:], 1.0 / HD, 1e-6, ALU.mult, ALU.add).then_inc(sum_ready, 1)

                def scale(b):
                    dve.wait_ge(pow_done, b.count(1, 1))
                    nc.vector.tensor_tensor(qk.rearrange("p i (h d) -> p (i h) d", h=H),
                                            PROJ[b.u][:].rearrange("p (h d) -> p h d", d=HD),
                                            rn[:].unsqueeze(2).broadcast_to([P, 2 * H, HD]),
                                            ALU.mult).then_inc(qk_ready, 1)

                def spread(b):
                    dve.wait_ge(qk_turned, b.count(1, 1))
                    for c in range(C):
                        nc.vector.tensor_tensor(qm[b.u][:, c],
                                                Q_T[:, c * P:(c + 1) * P].unsqueeze(1).broadcast_to([P, 4, P]),
                                                rowmask[:].unsqueeze(2).broadcast_to([P, 4, P]),
                                                ALU.mult).then_inc(q_spread, 1)

                def finish(b):
                    dve.wait_ge(turned_back, b.count(1, 1))
                    pv = PV[b.u][:, 0:H * (HD + 1)].rearrange("p (h d) -> p h d", h=H)
                    nc.vector.reciprocal(inv[:], pv[:, :, HD]).then_inc(o_ready, 1)
                    dve.wait_ge(o_ready, b.count(2, 1))
                    nc.vector.tensor_tensor(o[:], pv[:, :, 0:HD], inv[:].unsqueeze(2).broadcast_to([P, H, HD]),
                                            ALU.mult).then_inc(o_ready, 1)
                    dve.wait_ge(o_ready, b.count(2, 2))
                    nc.vector.scalar_tensor_tensor(flat(b.of(x)), flat(o[:]), tg_x[:, 2:3], flat(b.of(x)), ALU.mult,
                                                   ALU.add).then_inc(added, 1)
                    dve.wait_ge(added, b.count(1, 1))
                    nc.vector.bn_stats(flat(b.of(stats)), flat(b.of(x)))

                def body(prev, b, nxt, far):
                    if prev is None:
                        norm(b)
                        norm(nxt)
                        sums(b)
                        scale(b)
                        sums(nxt)
                        spread(b)
                    if far:
                        dve.wait_ge(turned, b.count(1, 1))
                        norm(far)
                    if nxt:
                        scale(nxt)
                    if prev:
                        finish(prev)
                    if far:
                        sums(far)
                    if nxt:
                        spread(nxt)
                    if nxt is None:
                        finish(b)
                each_batch_far(dve, body)

    def channel_heads():
        H, HD, L = 8, 16, D
        scale = HD ** -0.5
        G, N = 4, 8
        carve = carver()
        with ExitStack() as st:
            sem = lambda n: st.enter_context(nc.semaphore(f"l3a_{n}"))
            (normed, k_spread, v_ready, s_ready, m_ready, e_ready, e_turned, eT_ready, pv_done, i_ready, o_ready,
             o_turned, out_ready, added, mask_ready, *fin) = (
                sem(n) for n in ("normed", "ks", "v", "s", "m", "e", "et", "eT", "pv", "i", "o", "ot", "out", "added",
                                 "mk", "fin", "var", "rstd"))
            km = [carve([P, 2, L]) for _ in range(2)]
            rowmask = carve([P, 2, L])
            mx = carve([P, 4, 2])
            e = [carve([P, 2, L]) for _ in range(4)]
            eT = carve([P, 2, 4, P])
            v = [carve([P, C, H * (P + HD)]) for _ in range(2)]
            total = carve([P, 2, 2, H])
            o = carve([P, 2, H, HD])
            out = carve([P, L])
            gf = carve([P, 1])
            block = st.enter_context(nc.Block())
            S = (bank[0], bank[1], bank[5], bank[7])
            PV, E_T, O_T = bank[3:5], bank[2], bank[6]

            @block.sync
            def _(sp):
                load_experts(sp, 3)

            @block.gpsimd
            def _(pool):
                nc.gpsimd.memset(rowmask[:], -scale).then_inc(mask_ready, 1)
                for i in range(2):
                    nc.gpsimd.memset(v[i][:], 0.0).then_inc(mask_ready, 1)
                pool.wait_ge(mask_ready, 3)
                for g in range(G):
                    rm = rowmask[32 * g:32 * g + 32]
                    nc.gpsimd.affine_select(out=rm, in_=rm, compare_op=ALU.is_ge, fill=0.0, base=0,
                                            pattern=[[-HD, 2], [0, L]], channel_multiplier=1).then_inc(mask_ready, 1)
                pool.wait_ge(mask_ready, 3 + G)
                for g in range(G):
                    rm = rowmask[32 * g:32 * g + 32]
                    nc.gpsimd.affine_select(out=rm, in_=rm, compare_op=ALU.is_ge, fill=0.0, base=HD - 1,
                                            pattern=[[HD, 2], [0, L]], channel_multiplier=-1).then_inc(mask_ready, 1)
                pool.wait_ge(mask_ready, 3 + 2 * G)
                finish_pool(pool, *fin[1:])

                def prep(b, free):
                    if free is not None:
                        pool.wait_ge(pv_done, free)
                    for j in range(2):
                        nc.gpsimd.tensor_tensor(km[b.u][:, j, :], flat(b.of(ctx)), rowmask[:, j, :],
                                                ALU.mult).then_inc(k_spread, 1)
                    for c in range(C):
                        nc.gpsimd.tensor_copy(v[b.u][:, c, :].rearrange("p (h w) -> p h w", h=H)[:, :, 0:HD],
                                              flat(b.of(ctxT)[:, :, c, :]).rearrange("p (h d) -> p h d", h=H)
                                              ).then_inc(v_ready, 1)

                def body(prev, b, nxt):
                    if prev is None:
                        prep(b, None)
                    if nxt:
                        prep(nxt, prev and prev.count(N, N))
                each_batch(pool, body)

            @block.tensor
            def _(pe):
                def scores(b, n):
                    qh, g = divmod(n, G)
                    rows = slice(32 * g, 32 * g + 32)
                    if n == 0:
                        pe.wait_ge(normed, b.count(1, 1))
                        pe.wait_ge(k_spread, b.count(2, 2))
                        pe.wait_ge(v_ready, b.count(2, 2))
                    nc.tensor.matmul(S[n % 4][:], xs[rows, b.u, qh * P:(qh + 1) * P],
                                     km[b.u][rows].rearrange("p j l -> p (j l)"), start=True, stop=True,
                                     tile_position=(32 * g, 0)).then_inc(s_ready, 1)

                def turn(b, n):
                    pe.wait_ge(e_ready, b.count(2 * N, 2 * n + 2))
                    if not (b.j is None and b.k == 0 and n == 0):
                        pe.wait_ge(eT_ready, b.count(N, n))
                    for j in range(2):
                        for c in range(C):
                            k = j * C + c
                            last = nc.tensor.transpose(E_T[:, k * P:(k + 1) * P],
                                                       e[n % 4][:, j, c * P:(c + 1) * P], ident[:])
                    last.then_inc(e_turned, 1)

                def values(b, n):
                    qh, g = divmod(n, G)
                    pe.wait_ge(eT_ready, b.count(N, n + 1))
                    for j in range(2):
                        h = 2 * g + j
                        for c in range(C):
                            last = nc.tensor.matmul(PV[b.u][:, qh * P:(qh + 1) * P], v[b.u][:, c, h * P:(h + 1) * P],
                                                    eT[:, n % 2, j * C + c, :], start=(h == 0 and c == 0),
                                                    stop=(h == H - 1 and c == C - 1))
                    last.then_inc(pv_done, 1)

                def turn_back(b):
                    pe.wait_ge(o_ready, b.count(1, 1))
                    for qh in range(2):
                        last = nc.tensor.transpose(O_T[:, qh * P:(qh + 1) * P],
                                                   o[:, qh].rearrange("p h d -> p (h d)"), ident[:])
                    last.then_inc(o_turned, 1)

                def body(prev, b, nxt):
                    for n in range(N):
                        scores(b, n)
                        if n >= 2:
                            turn(b, n - 2)
                        elif prev:
                            turn(prev, N - 2 + n)
                        if n >= 3:
                            values(b, n - 3)
                        elif prev:
                            values(prev, N - 3 + n)
                        if n == 5 and prev:
                            turn_back(prev)
                    if nxt is None:
                        turn(b, N - 2)
                        values(b, N - 3)
                        turn(b, N - 1)
                        values(b, N - 2)
                        values(b, N - 1)
                        turn_back(b)
                each_batch(pe, body)

            @block.scalar
            def _(act):
                def body(prev, b, nxt):
                    for n in range(N):
                        qh, g = divmod(n, G)
                        act.wait_ge(m_ready, b.count(N, n + 1))
                        for j in range(2):
                            nc.scalar.activation(e[n % 4][:, j, :], S[n % 4][:, j * L:(j + 1) * L], ACT.Exp,
                                                 bias=mx[:, n % 4, j:j + 1], scale=-1.0,
                                                 accum_out=total[:, b.u, qh, 2 * g + j:2 * g + j + 1]
                                                 ).then_inc(e_ready, 1)
                each_batch(act, body)

            @block.vector
            def _(dve):
                nc.vector.tensor_tensor(gf[:], small["l3_gamma"], tg_x[:, 3:4], ALU.mult)
                finish_vector(dve, *fin)

                def extremes(b, n):
                    dve.wait_ge(s_ready, b.count(N, n + 1))
                    nc.vector.tensor_reduce(mx[:, n % 4, :], S[n % 4][:].rearrange("p (j l) -> p j l", j=2), AX.X,
                                            ALU.min).then_inc(m_ready, 1)

                def copy(b, n):
                    dve.wait_ge(e_turned, b.count(N, n + 1))
                    nc.vector.tensor_copy(eT[:, n % 2].rearrange("p a q -> p (a q)"),
                                          E_T[:]).then_inc(eT_ready, 1)

                def divide(b):
                    dve.wait_ge(e_ready, b.count(2 * N, 2 * N))
                    tot = flat(total[:, b.u])
                    nc.vector.reciprocal(tot, tot).then_inc(i_ready, 1)
                    dve.wait_ge(i_ready, b.count(1, 1))
                    nc.vector.tensor_copy(o[:].rearrange("p q h d -> p (q h) d"),
                                          tot.unsqueeze(2).broadcast_to([P, 2 * H, HD])).then_inc(o_ready, 1)

                def add(b):
                    dve.wait_ge(o_turned, b.count(1, 1))
                    dve.wait_ge(pv_done, b.count(N, N))
                    nc.vector.tensor_scalar(out[:], PV[b.u][:, 0:L], gf[:, 0:1], None, ALU.mult).then_inc(out_ready, 1)
                    dve.wait_ge(out_ready, b.count(2, 1))
                    nc.vector.tensor_tensor(out[:], out[:], O_T[:, 0:L], ALU.mult).then_inc(out_ready, 1)
                    dve.wait_ge(out_ready, b.count(2, 2))
                    nc.vector.tensor_tensor(flat(b.of(x)), flat(b.of(x)), out[:], ALU.add).then_inc(added, 1)
                    dve.wait_ge(added, b.count(1, 1))
                    nc.vector.bn_stats(flat(b.of(stats)), flat(b.of(x)))

                def body(prev, b, nxt):
                    if prev is None:
                        norm_tile(xs[:, b.u, :], x, b).then_inc(normed, 1)
                    for n in range(N):
                        extremes(b, n)
                        if n >= 2:
                            copy(b, n - 2)
                        elif prev:
                            copy(prev, N - 2 + n)
                        if prev and n == 3:
                            divide(prev)
                        if prev and n == 7:
                            add(prev)
                        if nxt and n == 5:
                            norm_tile(xs[:, nxt.u, :], x, nxt).then_inc(normed, 1)
                    if nxt is None:
                        copy(b, N - 2)
                        copy(b, N - 1)
                        divide(b)
                        add(b)
                each_batch(dve, body)

    def route(layer):
        m = MOE[layer]
        R = 17 if layer == 1 else 16
        router = small[f"l{layer}_router"]
        with ExitStack() as st:
            sem = lambda n: nc.alloc_semaphore(f"r{layer}_{n}")
            staged, turned, xT_ready, l_ready, own, act_done, to_act, taken = (
                sem(n) for n in ("staged", "turned", "xT", "l", "own", "act", "ta", "taken"))
            carve = carver()
            t = lambda n, s: sb(f"r{layer}_{n}", s, F32, st) if layer == 1 else carve(s)
            lg = t("lg", [P, NB, R])
            prob = t("prob", [P, NB, PAD])
            rep = t("rep", [P, NB, PAD])
            best = t("best", [P, NB, 8])
            row = t("row", [P, 3, NB])
            block = st.enter_context(nc.Block())

            @block.gpsimd
            def _(pool):
                with pool.Fori(0, NB) as i:
                    pool.wait_ge(turned, i + 1)
                    nc.gpsimd.tensor_copy(xs[:, 0:1, :], xn[:, ds(i, 1), :]).then_inc(staged, 1)

            @block.tensor
            def _(pe):
                pe.sem_inc(turned, 1)
                with pe.Fori(0, NB) as i:
                    pe.wait_ge(staged, i + 1)
                    for c in range(C):
                        last = nc.tensor.transpose(bank[0][:, c * P:(c + 1) * P], xs[:, 0, c * P:(c + 1) * P], ident[:])
                    last.then_inc(turned, 1)
                    pe.wait_ge(xT_ready, i + 1)
                    pe.wait_ge(taken, i + 1)
                    for c in range(C):
                        last = nc.tensor.matmul(bank[1][:, 0:R], xT[:, 0, c, :], router[:, c, :], start=(c == 0),
                                                stop=(c == C - 1))
                    last.then_inc(l_ready, 1)

            @block.scalar
            def _(act):
                with act.Fori(0, NB) as i:
                    act.wait_ge(turned, i + 2)
                    nc.scalar.copy(flat(xT[:, 0]), bank[0][:, 0:D]).then_inc(xT_ready, 1)
                act.wait_ge(to_act, 1)
                if layer == 1:
                    nc.scalar.activation(prob[:, :, 0:NE], prob[:, :, 0:NE], ACT.Exp).then_inc(act_done, 1)
                    nc.scalar.activation(row[:, 2, :], lg[:, :, NE], ACT.Sigmoid).then_inc(act_done, 1)
                else:
                    nc.scalar.activation(lg[:], lg[:], ACT.Sigmoid).then_inc(act_done, 1)

            @block.vector
            def _(dve):
                bc = lambda a, n=NE: a.unsqueeze(2).broadcast_to([P, NB, n])
                nc.vector.memset(prob[:], FILL).then_inc(own, 1)
                nc.vector.memset(best[:], FILL).then_inc(own, 1)
                dve.sem_inc(taken, 1)
                with dve.Fori(0, NB) as i:
                    dve.wait_ge(l_ready, i + 1)
                    nc.vector.tensor_copy(flat(lg[:, ds(i, 1), :]), bank[1][:, 0:R]).then_inc(taken, 1)
                dve.wait_ge(taken, NB + 1)
                dve.wait_ge(own, 2)
                step = Chain(dve, own, 2)
                if layer == 1:
                    step(nc.vector.tensor_reduce(row[:, 0, :], lg[:, :, 0:NE], AX.X, ALU.max))
                    nc.vector.tensor_tensor(prob[:, :, 0:NE], lg[:, :, 0:NE], bc(row[:, 0, :]),
                                            ALU.subtract).then_inc(to_act, 1)
                    dve.wait_ge(act_done, 2)
                    step(nc.vector.tensor_reduce(row[:, 0, :], prob[:, :, 0:NE], AX.X, ALU.add))
                    step(nc.vector.reciprocal(row[:, 0, :], row[:, 0, :]))
                    step(nc.vector.tensor_tensor(prob[:, :, 0:NE], prob[:, :, 0:NE], bc(row[:, 0, :]), ALU.mult))
                    score = prob[:, :, 0:NE]
                else:
                    dve.sem_inc(to_act, 1)
                    dve.wait_ge(act_done, 1)
                    score = lg[:]
                    if layer == 2:
                        step(nc.vector.tensor_copy(prob[:, :, 0:NE], score))
                    else:
                        g4 = prob[:, :, 0:NE].rearrange("p t (g i) -> p t g i", g=4)
                        step(nc.vector.tensor_tensor(prob[:, :, 0:NE], score,
                                                     small["l3_ebias"][:].unsqueeze(1).broadcast_to([P, NB, NE]),
                                                     ALU.add))
                        hi = t("hi", [P, NB, 4, 2])
                        lo = t("lo", [P, NB, 4, 2])
                        f = lambda a: a.rearrange("p t g -> p (t g)")
                        for k in range(2):
                            step(nc.vector.tensor_tensor(hi[:, :, :, k], g4[:, :, :, 2 * k], g4[:, :, :, 2 * k + 1],
                                                         ALU.max))
                            step(nc.vector.tensor_tensor(lo[:, :, :, k], g4[:, :, :, 2 * k], g4[:, :, :, 2 * k + 1],
                                                         ALU.min))
                        g1 = t("g1", [P, NB, 4])
                        g2 = t("g2", [P, NB, 4])
                        step(nc.vector.tensor_tensor(g1[:], hi[:, :, :, 0], hi[:, :, :, 1], ALU.max))
                        step(nc.vector.tensor_tensor(g2[:], hi[:, :, :, 0], hi[:, :, :, 1], ALU.min))
                        step(nc.vector.tensor_tensor(lo[:, :, :, 0], lo[:, :, :, 0], lo[:, :, :, 1], ALU.max))
                        step(nc.vector.tensor_tensor(g2[:], g2[:], lo[:, :, :, 0], ALU.max))
                        step(nc.vector.tensor_tensor(g1[:], g1[:], g2[:], ALU.add))
                        rank = t("rank", [P, NB, 4])
                        cmp = t("cmp", [P, NB])
                        step(nc.vector.memset(rank[:], 0.0))
                        for j in range(4):
                            for g in range(j + 1, 4):
                                step(nc.vector.tensor_tensor(cmp[:], g1[:, :, j], g1[:, :, g], ALU.is_ge))
                                step(nc.vector.tensor_tensor(rank[:, :, g], rank[:, :, g], cmp[:], ALU.add))
                                step(nc.vector.tensor_tensor(cmp[:], g1[:, :, g], g1[:, :, j], ALU.is_gt))
                                step(nc.vector.tensor_tensor(rank[:, :, j], rank[:, :, j], cmp[:], ALU.add))
                        step(nc.vector.tensor_scalar(rank[:], rank[:], 1.5, None, ALU.is_lt))
                        r4 = rank[:].unsqueeze(3).broadcast_to([P, NB, 4, 4])
                        step(nc.vector.tensor_scalar(g2[:], rank[:], -1.0, -BARRED, ALU.add, ALU.mult))
                        step(nc.vector.tensor_tensor(g4, g4, r4, ALU.mult))
                        step(nc.vector.tensor_tensor(g4, g4, g2[:].unsqueeze(3).broadcast_to([P, NB, 4, 4]), ALU.add))
                for i in range(NB):
                    nc.vector.max(best[:, i, :], prob[:, i, 0:NE]).then_inc(own, 1)
                step.n += NB
                dve.wait_ge(own, 2 + step.n)
                step(nc.vector.memset(best[:, :, m["k"]:8], FILL))
                for i in range(NB):
                    nc.vector.match_replace(rep[:, i, :], best[:, i, :], prob[:, i, :], TAKEN).then_inc(own, 1)
                step.n += NB
                dve.wait_ge(own, 2 + step.n)
                w = comb[:, :, 0:NE]
                step(nc.vector.tensor_scalar(rep[:, :, 0:NE], rep[:, :, 0:NE], TAKEN, None, ALU.is_equal))
                step(nc.vector.tensor_tensor(w, rep[:, :, 0:NE], score, ALU.mult))
                step(nc.vector.tensor_reduce(row[:, 0, :], w, AX.X, ALU.add))
                if layer == 1:
                    step(nc.vector.tensor_scalar(row[:, 0, :], row[:, 0, :], 1e-9, None, ALU.max))
                if layer == 3:
                    step(nc.vector.tensor_scalar(row[:, 0, :], row[:, 0, :], 1e-20, None, ALU.add))
                step(nc.vector.reciprocal(row[:, 0, :], row[:, 0, :]))
                if layer == 3:
                    step(nc.vector.tensor_scalar(row[:, 0, :], row[:, 0, :], 2.5, None, ALU.mult))
                step(nc.vector.tensor_scalar(row[:, 0, :], row[:, 0, :], tg_f[:, layer:layer + 1], None, ALU.mult))
                step(nc.vector.tensor_tensor(w, w, bc(row[:, 0, :]), ALU.mult))
                n = m["E"] - NE
                if layer == 1:
                    step(nc.vector.tensor_scalar(row[:, 2, :], row[:, 2, :], tg_f[:, 1:2], None, ALU.mult))
                    step(nc.vector.tensor_copy(comb[:, :, NE:NE + n], bc(row[:, 2, :], n)))
                else:
                    step(nc.vector.memset(comb[:, :, NE:NE + n], 1.0))
                    step(nc.vector.tensor_scalar(comb[:, :, NE:NE + n], comb[:, :, NE:NE + n],
                                                 tg_f[:, layer:layer + 1], None, ALU.mult))

    def experts(layer):
        m = MOE[layer]
        E, I, parts = m["E"], m["I"], m["parts"]
        gu_w, dn_w, kp = moe_views(layer)
        func = ACT.Gelu if layer == 2 else ACT.Silu
        with ExitStack() as st:
            sem = lambda n: nc.alloc_semaphore(f"m{layer}_{n}")
            (staged, turned, xT_ready, gu_ready, sg_ready, h_ready, h_turned, hT_ready, y_ready, acc_done, own,
             c_turned, cT_ready, b_ready, ones_ready) = (sem(n) for n in (
                "staged", "turned", "xT", "gu", "sg", "h", "ht", "hT", "y", "acc", "own", "ct", "cT", "b", "one"))
            sg = sb(f"sg{layer}", [P, 2, I], F32, st)
            h = sb(f"h{layer}", [P, 2, I], F32, st)
            hT = sb(f"hT{layer}", [kp, 2, parts, P], F32, st)
            ones3 = sb(f"ones3{layer}", [3, P], BF16, st)
            cs = sb(f"cs{layer}", [P, 20], F32, st)
            cT = sb(f"cT{layer}", [20, P], F32, st)
            block = st.enter_context(nc.Block())
            GU, HT, Y = bank[0:2], bank[2:4], bank[4:6]
            XT = bank[6]
            if layer == 2:
                gb = gbias[:].rearrange("p (e n) -> p e n", e=E)

            @block.gpsimd
            def _(pool):
                with pool.Fori(0, NB) as t:
                    pool.wait_ge(turned, t + 1)
                    if layer == 2:
                        nc.gpsimd.tensor_copy(cs[:, 0:E], flat(comb[:, ds(t, 1), 0:E]))
                    nc.gpsimd.tensor_copy(xs[:, 0:1, :], xn[:, ds(t, 1), :]).then_inc(staged, 1)

            @block.tensor
            def _(pe):
                pe.sem_inc(turned, 1)
                pe.wait_ge(moe_loaded[layer - 1], 32)
                pe.wait_ge(ones_ready, 1)

                def gate_up(b, w, bias):
                    for c in range(C):
                        last = nc.tensor.matmul(GU[b][:, 0:2 * I], xT[:, 0, c, :], w[c], start=(c == 0),
                                                stop=(c == C - 1 and bias is None))
                    if bias is not None:
                        last = nc.tensor.matmul(GU[b][:, 0:2 * I], ones3[:], bias, start=False, stop=True)
                    last.then_inc(gu_ready, 1)

                def turn(b, at_count):
                    pe.wait_ge(h_ready, at_count)
                    for k in range(parts):
                        last = nc.tensor.transpose(HT[b][0:kp, k * P:(k + 1) * P], h[:, b, k * kp:(k + 1) * kp],
                                                   ident[:])
                    last.then_inc(h_turned, 1)

                def down(b, w, at_count):
                    pe.wait_ge(hT_ready, at_count)
                    pe.wait_ge(acc_done, at_count)
                    for k in range(parts):
                        last = nc.tensor.matmul(Y[b][:, 0:D], hT[:, b, k, :], w[k], start=(k == 0),
                                                stop=(k == parts - 1))
                    last.then_inc(y_ready, 1)

                with pe.Fori(0, NB) as t:
                    pe.wait_ge(staged, t + 1)
                    for c in range(C):
                        last = nc.tensor.transpose(XT[:, c * P:(c + 1) * P], xs[:, 0, c * P:(c + 1) * P], ident[:])
                    if layer == 2:
                        last = nc.tensor.transpose(XT[0:E, D:D + P], cs[:, 0:E], ident[:])
                    last.then_inc(turned, 1)
                    pe.wait_ge(xT_ready, t + 1)
                    if layer == 2:
                        nc.tensor.matmul(bank[7][:, 0:D], cT[0:E, :], small["l2_b2"][:], start=True,
                                         stop=True).then_inc(c_turned, 1)
                    st_w = lambda e: [gu_w[:, e, c, :] for c in range(C)]
                    st_d = lambda e: [dn_w[:, e, k, :] for k in range(parts)]
                    gate_up(0, st_w(0), gb[:, 0, :] if layer == 2 else None)
                    gate_up(1, st_w(1), gb[:, 1, :] if layer == 2 else None)
                    turn(0, t * E + 1)

                    n = (E - 2) // 2
                    with pe.Fori(0, n) as j:
                        for u in range(2):
                            gu_e = gu_w[:, 2:2 + 2 * n].rearrange("p (j u) c i -> p j u c i", u=2)
                            dn_e = dn_w[:, 0:2 * n].rearrange("p (j u) k d -> p j u k d", u=2)
                            bias = None
                            if layer == 2:
                                bias = flat(gb[:, 2:2 + 2 * n, :].rearrange("p (j u) n -> p j u n", u=2)[:, ds(j, 1), u, :])
                            gate_up(u, [flat(gu_e[:, ds(j, 1), u, c, :]) for c in range(C)], bias)
                            turn(1 - u, t * E + j * 2 + (u + 2))
                            down(u, [flat(dn_e[:, ds(j, 1), u, k, :]) for k in range(parts)], t * E + j * 2 + (u + 1))
                    if E % 2:
                        gate_up(0, st_w(E - 1), None)
                        turn(1, t * E + (E - 1))
                        down((E - 3) % 2, st_d(E - 3), t * E + (E - 2))
                    turn((E - 1) % 2, t * E + E)
                    down((E - 2) % 2, st_d(E - 2), t * E + (E - 1))
                    down((E - 1) % 2, st_d(E - 1), t * E + E)

            @block.scalar
            def _(act):
                def gate(b, at_count):
                    act.wait_ge(gu_ready, at_count)
                    nc.scalar.activation(sg[:, b, :], GU[b][:, 0:I], func).then_inc(sg_ready, 1)

                def move(b, at_count):
                    act.wait_ge(h_turned, at_count)
                    nc.scalar.copy(hT[:, b].rearrange("p k t -> p (k t)"), HT[b][0:kp, 0:parts * P]).then_inc(hT_ready, 1)

                with act.Fori(0, NB) as t:
                    act.wait_ge(turned, t + 2)
                    if layer == 2:
                        nc.scalar.copy(cT[0:E, :], XT[0:E, D:D + P])
                    nc.scalar.copy(flat(xT[:, 0]), XT[:, 0:D]).then_inc(xT_ready, 1)
                    gate(0, t * E + 1)
                    gate(1, t * E + 2)
                    move(0, t * E + 1)
                    with act.Fori(0, (E - 2) // 2) as j:
                        for u in range(2):
                            gate(u, t * E + j * 2 + (u + 3))
                            move(1 - u, t * E + j * 2 + (u + 2))
                    if E % 2:
                        gate(0, t * E + E)
                        move(1, t * E + (E - 1))
                    move((E - 1) % 2, t * E + E)

            @block.vector
            def _(dve):
                nc.vector.memset(ones3[:], 1.0).then_inc(ones_ready, 1)
                dve.sem_inc(acc_done, 2)

                def hidden(b, at_count):
                    dve.wait_ge(sg_ready, at_count)
                    nc.vector.tensor_tensor(h[:, b, :], sg[:, b, :], GU[b][:, I:2 * I], ALU.mult).then_inc(h_ready, 1)

                with dve.Fori(0, NB) as t:
                    xt = flat(x[:, ds(t, 1), :])

                    def add(b, scalar, at_count):
                        dve.wait_ge(y_ready, at_count)
                        dve.wait_ge(acc_done, at_count + 1)
                        nc.vector.scalar_tensor_tensor(xt, Y[b][:, 0:D], scalar, xt, ALU.mult,
                                                       ALU.add).then_inc(acc_done, 1)

                    if layer == 2:
                        dve.wait_ge(c_turned, t + 1)
                        nc.vector.tensor_tensor(xt, xt, bank[7][:, 0:D], ALU.add).then_inc(own, 1)
                        dve.wait_ge(own, t * 2 + 1)
                        nc.vector.scalar_tensor_tensor(xt, flat(xn[:, ds(t, 1), :]), tg_f[:, 2:3], xt, ALU.mult,
                                                       ALU.add).then_inc(own, 1)
                        dve.wait_ge(own, t * 2 + 2)
                    ct = comb[:, ds(t, 1), :].rearrange("p a e -> p (a e)")
                    hidden(0, t * E + 1)
                    hidden(1, t * E + 2)
                    n = (E - 2) // 2
                    with dve.Fori(0, n) as j:
                        for u in range(2):
                            hidden(u, t * E + j * 2 + (u + 3))
                            cu = comb[:, :, 0:2 * n].rearrange("p t (j u) -> p t j u", u=2)[:, ds(t, 1), ds(j, 1), u]
                            add(u, cu.rearrange("p a b -> p (a b)"), t * E + j * 2 + (u + 1))
                    if E % 2:
                        hidden(0, t * E + E)
                        add((E - 3) % 2, ct[:, E - 3:E - 2], t * E + (E - 2))
                    add((E - 2) % 2, ct[:, E - 2:E - 1], t * E + (E - 1))
                    add((E - 1) % 2, ct[:, E - 1:E], t * E + E)
                    dve.wait_ge(acc_done, t * E + (E + 2))
                    nc.vector.bn_stats(flat(stats[:, ds(t, 1), :]), xt)

    def store():
        with ExitStack() as st:
            block = st.enter_context(nc.Block())

            @block.sync
            def _(sp):
                sp.dma_start(io["out"], x[:]).then_inc(out_stored, 16)
                for k in range(3):
                    if STOP > (0, 4, 6)[k]:
                        sp.wait_ge(moe_loaded[k], 32)
                sp.wait_ge(out_stored, 16)

    def mixture(layer):
        normalize(f"nf{layer}")
        with nc.cleanup_on_exit():
            route(layer)
            experts(layer)

    stages = [decay_attention, linear, masked_attention, lambda: mixture(1), many_heads, lambda: mixture(2),
              channel_heads, lambda: mixture(3)]
    setup()
    for stage in stages[:STOP]:
        stage()
    store()


def kernel(**inputs):
    import numpy as np
    import concourse.bacc as bacc
    from concourse.bass_utils import run_bass_kernel_spmd as run

    i = {k: np.asarray(v) for k, v in inputs.items()}

    def rows(a):
        return np.broadcast_to(a.reshape(1, -1), (P, a.size))

    def chunks(a):
        return a.reshape(C, P, -1).transpose(1, 0, 2)

    def gate_up(gate, up):
        gu = np.concatenate([gate, up], axis=2)
        return gu.reshape(gu.shape[0], C, P, -1).transpose(2, 0, 1, 3)

    def down(d, parts):
        return d.reshape(d.shape[0], parts, -1, D).transpose(2, 0, 1, 3)

    def join(*a):
        return np.concatenate(a, axis=0)

    tr = lambda a: a.transpose(0, 2, 1)
    cut = lambda a: a.reshape(D, 4, 176).transpose(1, 0, 2)
    Wkv = np.concatenate([i["L2_xattn_Wk"], i["L2_xattn_Wv"]], axis=0)
    arrays = {
        "x": i["x"].transpose(1, 0, 2), "ctx": i["ctx_2048"].transpose(1, 0, 2),
        "ctxT": i["ctx_2048"].reshape(NB, P, C, P).transpose(3, 0, 2, 1),
        "mask": np.broadcast_to(i["mask_BxS2_bk0"][None], (P, NB, P)),
        "g_xattn": rows(i["g_xattn"]), "g_ffn": rows(i["g_ffn"]), "decay": rows(i["L0_xattn_decay"]),
        "l0_win": chunks(i["L0_xattn_W_in"].T), "l0_bin": i["L0_xattn_b_in"].reshape(C, P).T,
        "l0_wout": chunks(i["L0_xattn_W_out"].T), "l0_bout": rows(i["L0_xattn_b_out"]),
        "l0_gamma": rows(i["L0_xattn_gamma"]), "l0_beta": rows(i["L0_xattn_beta"]),
        "l0_w": chunks(i["L0_ffn_weight"].T), "l0_scale": rows(i["L0_ffn_scale_weight"]),
        "l0_bias": rows(i["L0_ffn_bias"]),
        "l1_router": chunks(np.concatenate([i["L1_ffn_router_w"].T, i["L1_ffn_sh_gate_w"]], axis=1)),
        "l2_router": chunks(i["L2_ffn_wa"]), "l3_router": chunks(i["L3_ffn_gate_weight"].T),
        "l2_wq": chunks(i["L2_xattn_Wq"].T), "l2_wk": chunks(Wkv[0::2].T), "l2_wv": chunks(Wkv[1::2].T),
        "l2_b2": join(i["L2_ffn_rb2"], i["L2_ffn_sb2"]), "l3_gamma": rows(i["L3_xattn_gamma"]),
        "l3_ebias": rows(i["L3_ffn_expert_bias"]),
        "l2_gub": np.broadcast_to(np.concatenate([join(i["L2_ffn_rgb"], i["L2_ffn_sgb"]),
                                                  join(i["L2_ffn_rb1"], i["L2_ffn_sb1"])], axis=1).reshape(1, -1),
                                  (3, 18 * 256)),
        "l1_gu": gate_up(join(i["L1_ffn_w_gate"], cut(i["L1_ffn_sh_gate"])),
                         join(i["L1_ffn_w_up"], cut(i["L1_ffn_sh_up"]))),
        "l1_dn": down(join(i["L1_ffn_w_down"], i["L1_ffn_sh_down"].reshape(4, 176, D)), 2),
        "l2_gu": gate_up(join(i["L2_ffn_rg"], i["L2_ffn_sg"]), join(i["L2_ffn_rw1"], i["L2_ffn_sw1"])),
        "l2_dn": down(join(i["L2_ffn_rw2"], i["L2_ffn_sw2"]), 1),
        "l3_gu": gate_up(tr(join(i["L3_ffn_gate_proj"], i["L3_ffn_shared_gate"][None])),
                         tr(join(i["L3_ffn_up_proj"], i["L3_ffn_shared_up"][None]))),
        "l3_dn": down(tr(join(i["L3_ffn_down_proj"], i["L3_ffn_shared_down"][None])), 1),
    }
    arrays["pack"] = np.concatenate([arrays.pop(k).reshape(P, -1) for k, _ in PACKED], axis=1)
    nc = bacc.Bacc("TRN2", target_bir_lowering=False, num_devices=1)
    io, sent = {}, {}
    for name, a in arrays.items():
        a = np.ascontiguousarray(a)
        sent[f"in_{name}"] = a
        io[name] = nc.dram_tensor(f"in_{name}", a.shape, mybir.dt.from_np(a.dtype), kind="ExternalInput").ap()
    io["out"] = nc.dram_tensor("out_x", [P, NB, D], F32, kind="ExternalOutput").ap()
    build(nc, io)
    got = run(nc, [sent], core_ids=[0]).results[0]["out_x"]
    return got.transpose(1, 0, 2)
```

```python
from contextlib import ExitStack

import concourse.bass as bass
from concourse import mybir

F32 = mybir.dt.float32
BF16 = mybir.dt.bfloat16
I32 = mybir.dt.int32
U8 = mybir.dt.uint8
ALU = mybir.AluOpType
ACT = mybir.ActivationFunctionType
AX = mybir.AxisListType
ds = bass.ds

P = 128
NB = 16
D = 256
C = D // P
NE = 16
PAD = 24
FILL = -3.0e38
BARRED = -2.9e38
TAKEN = -3.2e38
LN_EPS = 1e-5
ROUTED = -(-((4 * NB * P + NE * (P - 1)) // P) // 8) * 8
TILES = ROUTED + 4 * NB


PACKED = (("g_xattn", 4), ("g_ffn", 4), ("decay", 1), ("l0_bin", C), ("l0_gamma", D), ("l0_beta", D),
          ("l0_bout", D), ("l0_win", C * D), ("l0_wout", C * D), ("l0_scale", D), ("l0_bias", D), ("l0_w", C * D),
          ("l1_router", C * 17), ("l2_router", C * 16), ("l3_router", C * 16), ("l3_gamma", 1), ("l3_ebias", 16),
          ("l2_wq", C * D), ("l2_wk", C * D), ("l2_wv", C * D))
CHUNKED = ("l0_win", "l0_wout", "l0_w", "l1_router", "l2_router", "l3_router", "l2_wq", "l2_wk", "l2_wv")


class Chain:

    def __init__(self, eng, sem, base=0):
        self.eng, self.sem, self.base, self.n = eng, sem, base, 0

    def __call__(self, ins):
        ins.then_inc(self.sem, 1)
        self.n += 1
        self.eng.wait_ge(self.sem, self.base + self.n)
        return ins


def flat(ap):
    return ap.rearrange("p a b -> p (a b)")


class At:

    def __init__(self, k, j=None, steps=NB // 2 - 1):
        self.k, self.j, self.steps = k, j, steps
        self.u = k % 2

    def count(self, each, plus=0):
        if self.j is None:
            return self.k * each + plus
        return self.j * (2 * each) + (self.k * each + plus)

    def of(self, view):
        view = view[:]
        if self.j is None:
            return view[:, self.k:self.k + 1]
        lo = self.k - self.k % 2
        dims = "abcd"[:len(view.shape) - 2]
        pairs = view[:, lo:lo + 2 * self.steps].rearrange(f"p (j u) {' '.join(dims)} -> p j u {' '.join(dims)}", u=2)
        return pairs[:, ds(self.j, 1), self.k % 2]


def each_of_four(eng, body):
    with eng.Fori(0, NB // 4) as j:
        for u in range(4):
            def part(view, u=u):
                names = "abcd"[:len(view.shape) - 2]
                dims = " ".join(names)
                return view[:].rearrange(f"p (j u) {dims} -> p j u {dims}", u=4)[:, ds(j, 1), u]
            body(part)


def each_batch(eng, body):
    body(None, At(0), At(1))
    with eng.Fori(0, NB // 2 - 1) as j:
        body(At(0, j), At(1, j), At(2, j))
        body(At(1, j), At(2, j), At(3, j))
    body(At(NB - 2), At(NB - 1), None)


def each_batch_far(eng, body):
    steps = NB // 2 - 2
    body(None, At(0), At(1), At(2))
    with eng.Fori(0, steps) as j:
        body(*(At(k, j, steps) for k in range(4)))
        body(*(At(k, j, steps) for k in range(1, 5)))
    body(*(At(k) for k in range(NB - 4, NB)))
    body(At(NB - 3), At(NB - 2), At(NB - 1), None)
    body(At(NB - 2), At(NB - 1), None, None)


def build(nc, io):
    with ExitStack() as top:
        _build(nc, io, top)


def _build(nc, io, top):
    def sb(name, shape, dt=F32, at=None):
        return (at or top).enter_context(nc.sbuf_tensor(name, shape, dt))

    WEIGHTS = 20 * (C * 2 * 176 + 2 * D)
    bank = [top.enter_context(nc.psum_tensor(f"bank{i}", [P, 512], F32)) for i in range(8)]
    x = sb("x", [P, NB, D])
    xn = sb("xn", [P, NB, D])
    ctx = sb("ctx", [P, NB, D])
    ctxT = sb("ctxT", [P, NB, C, P])
    weights = sb("weights", [P, WEIGHTS])
    ident = sb("ident", [P, P])
    ones = sb("ones", [P, P])
    neg_half = sb("neg_half", [P, 64])
    stats = sb("stats", [P, NB, 6])
    var = sb("var", [P, 2, NB])
    nmean = sb("nmean", [P, NB])
    rstd = sb("rstd", [P, NB])
    comb = sb("comb", [P, NB, 20])
    xs = sb("xs", [P, 2, D])
    xT = sb("xT", [P, 2, C, P])
    pack = sb("pack", [P, sum(n for _, n in PACKED)])
    small, at = {"mask": sb("mask", [P, NB, P], U8), "l2_b2": sb("l2_b2", [18, D])}, 0
    for k, n in PACKED:
        view = pack[:, at:at + n]
        small[k] = view.rearrange("p (c n) -> p c n", c=C) if k in CHUNKED else view
        at += n
    gbias = sb("gbias", [3, 18 * 256], BF16)
    slot = sb("slot", [P, NB, NE])
    best = sb("best", [P, NB, 8])
    row_in = sb("row_in", [P, NB, 4], I32)
    row_out = sb("row_out", [P, NB, 4], I32)
    weight = sb("weight", [P, NB, 4])
    tile_expert_f = sb("tile_expert_f", [1, TILES])
    tile_expert = sb("tile_expert", [1, TILES], I32)
    numbers = sb("numbers", [P, ROUTED])
    slots_in, slots_out = io["slots_in"], io["slots_out"]
    tg_x = sb("tg_x", [P, 4])
    tg_f = sb("tg_f", [P, 4])

    NCH, CH = 6, 18 * 256 // 6
    x_loaded, ctx_loaded, ctxT_loaded, pack_loaded, rest_loaded = (
        top.enter_context(nc.semaphore(n)) for n in ("x_loaded", "ctx_loaded", "ctxT_loaded", "pack_loaded",
                                                     "rest_loaded"))
    moe_loaded = [top.enter_context(nc.semaphore(f"moe_loaded{i}")) for i in range(3)]
    out_stored = top.enter_context(nc.semaphore("out_stored"))

    MOE = {1: dict(E=20, I=176, parts=2, k=4), 2: dict(E=18, I=128, parts=1, k=2), 3: dict(E=17, I=128, parts=1, k=4)}

    def moe_views(layer):
        m = MOE[layer]
        n = m["E"] * C * 2 * m["I"]
        kp = m["I"] // m["parts"]
        gu = weights[:, 0:n].rearrange("p (e c i) -> p e c i", e=m["E"], c=C)
        dn = weights[0:kp, n:n + m["E"] * m["parts"] * D].rearrange("p (e k d) -> p e k d", e=m["E"], k=m["parts"])
        return gu, dn, kp

    def load_experts(eng, layer):
        gu, dn, _ = moe_views(layer)
        eng.dma_start(gu, io[f"l{layer}_gu"]).then_inc(moe_loaded[layer - 1], 16)
        eng.dma_start(dn, io[f"l{layer}_dn"]).then_inc(moe_loaded[layer - 1], 16)

    def carver(layer=None):
        names = [k for k, _ in PACKED]
        begin, end = (sum(n for _, n in PACKED[:names.index(k)]) for k in ("l0_gamma", "l1_router"))
        space, at, limit = (pack, [begin], end) if layer == 1 else (weights, [18 * (C * 2 * 128 + D)], WEIGHTS)

        def carve(shape):
            n = 1
            for k in shape[1:]:
                n *= k
            view = space[0:shape[0], at[0]:at[0] + n]
            at[0] += n
            assert at[0] <= limit
            if len(shape) > 2:
                names = "abcd"[:len(shape) - 1]
                view = view.rearrange(f"p ({' '.join(names)}) -> p {' '.join(names)}",
                                      **{k: v for k, v in zip(names, shape[1:])})
            return view
        return carve

    def setup():
        with ExitStack() as st:
            sem = lambda n: st.enter_context(nc.semaphore(n))
            cleared = sem("su_cleared")
            numbers_i = sb("numbers_i", [P, ROUTED], I32, st)
            block = st.enter_context(nc.Block())

            @block.sync
            def _(sp):
                sp.dma_start(x[:], io["x"]).then_inc(x_loaded, 16)
                sp.dma_start(ctx[:], io["ctx"]).then_inc(ctx_loaded, 16)
                sp.dma_start(ctxT[:], io["ctxT"]).then_inc(ctxT_loaded, 16)
                load_experts(sp, 1)

            @block.scalar
            def _(act):
                act.dma_start(pack[:], io["pack"]).then_inc(pack_loaded, 16)
                act.dma_start(small["mask"][:], io["mask"]).then_inc(rest_loaded, 16)
                act.dma_start(small["l2_b2"][:], io["l2_b2"]).then_inc(rest_loaded, 16)
                act.wait_ge(pack_loaded, 16)
                nc.scalar.activation(tg_x[:], small["g_xattn"], ACT.Tanh)
                nc.scalar.activation(tg_f[:], small["g_ffn"], ACT.Tanh)

            @block.gpsimd
            def _(pool):
                nc.gpsimd.memset(ident[:], 0.0).then_inc(cleared, 1)
                nc.gpsimd.memset(ones[:], 1.0)
                nc.gpsimd.memset(neg_half[:], -0.5)
                pool.iota(numbers_i[:], pattern=[[1, ROUTED]], base=0, channel_multiplier=0).then_inc(cleared, 1)
                pool.wait_ge(cleared, 2)
                nc.gpsimd.tensor_copy(numbers[:], numbers_i[:])
                nc.gpsimd.affine_select(out=ident[:], in_=ident[:], compare_op=ALU.not_equal, fill=1.0, base=0,
                                        pattern=[[-1, P]], channel_multiplier=1)

            @block.vector
            def _(dve):
                dve.wait_ge(x_loaded, 16)
                each_of_four(dve, lambda part: nc.vector.bn_stats(flat(part(stats)), flat(part(x))))

    def finish_vector(dve, own, var_ready, rstd_ready):
        nc.vector.tensor_tensor(nmean[:], stats[:, :, 1], stats[:, :, 4], ALU.add).then_inc(own, 1)
        nc.vector.tensor_tensor(var[:, 0, :], stats[:, :, 1], stats[:, :, 4], ALU.subtract).then_inc(own, 1)
        nc.vector.tensor_tensor(var[:, 1, :], stats[:, :, 2], stats[:, :, 5], ALU.add).then_inc(own, 1)
        dve.wait_ge(own, 3)
        nc.vector.tensor_tensor(var[:, 0, :], var[:, 0, :], var[:, 0, :], ALU.mult).then_inc(own, 1)
        nc.vector.tensor_scalar(var[:, 1, :], var[:, 1, :], 1.0 / D, LN_EPS, ALU.mult, ALU.add).then_inc(own, 1)
        nc.vector.tensor_scalar(nmean[:], nmean[:], -0.5, None, ALU.mult).then_inc(own, 1)
        dve.wait_ge(own, 6)
        nc.vector.scalar_tensor_tensor(var[:, 1, :], var[:, 0, :], 0.25, var[:, 1, :], ALU.mult,
                                       ALU.add).then_inc(var_ready, 1)
        dve.wait_ge(rstd_ready, 1)

    def finish_pool(pool, var_ready, rstd_ready):
        pool.wait_ge(var_ready, 1)
        nc.gpsimd.tensor_tensor(rstd[:], var[:, 1, :], neg_half[:, 0:NB], ALU.pow).then_inc(rstd_ready, 1)

    def norm_tile(out, src, t):
        return nc.vector.tensor_scalar(out, t.of(src).rearrange("p a d -> p (a d)"),
                                       t.of(nmean[:]), t.of(rstd[:]), ALU.add, ALU.mult)

    def decay_attention():
        with ExitStack() as st:
            sem = lambda n: st.enter_context(nc.semaphore(f"l0a_{n}"))
            own, pe_done, e_ready, summed, cw_ready, sumT_ready, inT_ready = (
                sem(n) for n in ("own", "pe", "e", "summed", "cw", "sumT", "inT"))
            fin = [[sem(f"{n}{i}") for n in ("fin", "var", "rstd")] for i in range(2)]
            based, scaled_ready, x_ready = sem("based"), sem("scaled"), sem("x")
            K = sb("K", [P, 1], F32, st)
            powers = sb("powers", [P, P], F32, st)
            kbc = sb("kbc", [P, P], F32, st)
            cw = sb("cw", [P, 2], F32, st)
            bb = sb("bb", [P, C], F32, st)
            sumT = sb("sumT", [P, C, NB], F32, st)
            inT = sb("inT", [P, C, NB], F32, st)
            gg = sb("l0b_gg", [P, 2, D], F32, st)
            tmp = sb("l0b_tmp", [P, 2, D], F32, st)
            block = st.enter_context(nc.Block())

            @block.scalar
            def _(act):
                act.wait_ge(pack_loaded, 16)
                nc.scalar.activation(K[:], small["decay"], ACT.Exp, scale=-1.0).then_inc(e_ready, 1)

            @block.vector
            def _(dve):
                step = Chain(dve, own)
                dve.wait_ge(e_ready, 1)
                step(nc.vector.tensor_scalar(K[:], K[:], 1.0, None, ALU.add))
                step(nc.vector.reciprocal(K[:], K[:]))
                step(nc.vector.tensor_scalar(kbc[:], ones[:], K[:], None, ALU.mult))
                step(nc.vector.tensor_tensor_scan(powers[:], kbc[:], ident[:], 0.0, ALU.mult, ALU.add))
                step(nc.vector.tensor_reduce(cw[:, 0:1], powers[:], AX.X, ALU.add))
                nc.vector.tensor_scalar(cw[:, 0:1], cw[:, 0:1], 1.0 / P, None, ALU.mult).then_inc(cw_ready, 1)
                finish_vector(dve, *fin[0])
                each_of_four(dve, lambda part: nc.vector.tensor_scalar(
                    part(xn), part(x), part(nmean), part(rstd), ALU.add, ALU.mult).then_inc(based, 1))
                step(nc.vector.tensor_scalar(gg[:, 0, :], small["l0_gamma"], tg_x[:, 0:1], None, ALU.mult))
                nc.vector.tensor_scalar(gg[:, 1, :], small["l0_beta"], tg_x[:, 0:1], None, ALU.mult).then_inc(based, 1)
                dve.wait_ge(pe_done, 1)
                step(nc.vector.tensor_copy(cw[:, 1:2], bank[0][:, 32:33]))
                nc.vector.tensor_copy(sumT[:], bank[0][:, 0:32].rearrange("p (b c) -> p c b", c=C)).then_inc(sumT_ready, 1)
                dve.wait_ge(pe_done, 2)
                step(nc.vector.tensor_scalar(bb[:], small["l0_bin"], cw[:, 1:2], None, ALU.mult))
                for c in range(C):
                    nc.vector.tensor_scalar(inT[:, c, :], bank[1][:, c * NB:(c + 1) * NB], bb[:, c:c + 1], None,
                                            ALU.add).then_inc(inT_ready, 1)
                dve.wait_ge(based, NB)
                for b in range(NB):
                    dve.wait_ge(pe_done, 3 + b)
                    nc.vector.tensor_tensor(xn[:, b, :], xn[:, b, :], bank[2 + b % 4][:, 0:D], ALU.add).then_inc(summed, 1)
                    if b:
                        dve.wait_ge(summed, b)
                        nc.vector.bn_stats(stats[:, b - 1, :], xn[:, b - 1, :])
                dve.wait_ge(summed, NB)
                step(nc.vector.bn_stats(stats[:, NB - 1, :], xn[:, NB - 1, :]))
                finish_vector(dve, *fin[1])
                dve.wait_ge(based, 2 * NB + 1)

                def scaled(b):
                    nc.vector.scalar_tensor_tensor(tmp[:, b.u, :], flat(b.of(xn)), b.of(nmean), gg[:, 0, :], ALU.add,
                                                   ALU.mult).then_inc(scaled_ready, 1)

                def body(prev, b, nxt):
                    if prev is None:
                        scaled(b)
                    if prev:
                        dve.wait_ge(x_ready, b.count(1, 0))
                        nc.vector.bn_stats(flat(prev.of(stats)), flat(prev.of(x)))
                    if nxt:
                        scaled(nxt)
                    dve.wait_ge(scaled_ready, b.count(1, 1))
                    nc.vector.scalar_tensor_tensor(flat(b.of(x)), tmp[:, b.u, :], b.of(rstd), flat(b.of(x)), ALU.mult,
                                                   ALU.add).then_inc(x_ready, 1)
                    if nxt is None:
                        dve.wait_ge(x_ready, b.count(1, 1))
                        nc.vector.bn_stats(flat(b.of(stats)), flat(b.of(x)))
                each_batch(dve, body)

            @block.gpsimd
            def _(pool):
                finish_pool(pool, *fin[0][1:])
                pool.wait_ge(based, NB + 1)
                each_of_four(pool, lambda part: nc.gpsimd.tensor_tensor(
                    flat(part(x)), flat(part(x)), gg[:, 1, :], ALU.add).then_inc(based, 1))
                finish_pool(pool, *fin[1][1:])

            @block.tensor
            def _(pe):
                pe.wait_ge(cw_ready, 1)
                pe.wait_ge(ctx_loaded, 16)
                nc.tensor.matmul(bank[0][:, 32:33], ones[:], cw[:, 0:1], start=True, stop=True)
                for b in range(NB):
                    for c in range(C):
                        last = nc.tensor.matmul(bank[0][:, b * C + c:b * C + c + 1], ctx[:, b, c * P:(c + 1) * P],
                                                cw[:, 0:1], start=True, stop=True)
                last.then_inc(pe_done, 1)
                pe.wait_ge(sumT_ready, 1)
                for e in range(C):
                    for c in range(C):
                        last = nc.tensor.matmul(bank[1][:, e * NB:(e + 1) * NB],
                                                small["l0_win"][:, c, e * P:(e + 1) * P], sumT[:, c, :],
                                                start=(c == 0), stop=(c == C - 1))
                last.then_inc(pe_done, 1)
                pe.wait_ge(inT_ready, 2)
                for b in range(NB):
                    if b >= 4:
                        pe.wait_ge(summed, b - 3)
                    for c in range(C):
                        nc.tensor.matmul(bank[2 + b % 4][:, 0:D], inT[:, c, b:b + 1].broadcast_to([P, P]),
                                         small["l0_wout"][:, c, :], start=(c == 0), stop=False)
                    nc.tensor.matmul(bank[2 + b % 4][:, 0:D], ones[0:1, :], small["l0_bout"][0:1, :], start=False,
                                     stop=True).then_inc(pe_done, 1)

    def linear():
        with ExitStack() as st:
            sem = lambda n: st.enter_context(nc.semaphore(f"l0f_{n}"))
            normed, turned, xT_ready, y_ready, own, added, w_ready, *fin = (
                sem(n) for n in ("normed", "turned", "xT", "y", "own", "added", "w", "fin", "var", "rstd"))
            block = st.enter_context(nc.Block())
            w = small["l0_w"]

            @block.gpsimd
            def _(pool):
                finish_pool(pool, *fin[1:])
                nc.gpsimd.memset(xn[:], 0.0)

            @block.tensor
            def _(pe):
                def turn(t):
                    pe.wait_ge(normed, t.count(1, 1))
                    for c in range(C):
                        last = nc.tensor.transpose(bank[t.u][:, c * P:(c + 1) * P], xs[:, t.u, c * P:(c + 1) * P],
                                                   ident[:])
                    last.then_inc(turned, 1)

                def body(prev, t, nxt, far):
                    if prev is None:
                        turn(t)
                        pe.wait_ge(w_ready, 4)
                    if nxt:
                        turn(nxt)
                    pe.wait_ge(xT_ready, t.count(1, 1))
                    if prev:
                        pe.wait_ge(added, t.count(1, 0))
                    for c in range(C):
                        nc.tensor.matmul(bank[2 + t.u][:, 0:D], xT[:, t.u, c, :], w[:, c, :], start=(c == 0),
                                         stop=False)
                    nc.tensor.matmul(bank[2 + t.u][:, 0:D], ones[0:1, :], small["l0_bias"][0:1, :], start=False,
                                     stop=True).then_inc(y_ready, 1)
                each_batch_far(pe, body)

            @block.scalar
            def _(act):
                def body(prev, t, nxt, far):
                    act.wait_ge(turned, t.count(1, 1))
                    nc.scalar.copy(flat(xT[:, t.u]), bank[t.u][:, 0:D]).then_inc(xT_ready, 1)
                each_batch_far(act, body)

            @block.vector
            def _(dve):
                finish_vector(dve, *fin)
                step = Chain(dve, w_ready)
                for c in range(C):
                    step(nc.vector.tensor_tensor(w[:, c, :], w[:, c, :], small["l0_scale"], ALU.mult))
                step(nc.vector.tensor_scalar(flat(w), flat(w), tg_f[:, 0:1], None, ALU.mult))
                step(nc.vector.tensor_scalar(small["l0_bias"], small["l0_bias"], tg_f[:, 0:1], None, ALU.mult))

                dve.sem_inc(added, 1)

                def body(prev, t, nxt, far):
                    if prev is None:
                        norm_tile(xs[:, 0, :], x, t).then_inc(normed, 1)
                        norm_tile(xs[:, 1, :], x, nxt).then_inc(normed, 1)
                    if far:
                        dve.wait_ge(turned, t.count(1, 1))
                        norm_tile(xs[:, far.u, :], x, far).then_inc(normed, 1)
                    xt = flat(t.of(x))
                    dve.wait_ge(y_ready, t.count(1, 1))
                    nc.vector.tensor_tensor(xt, xt, bank[2 + t.u][:, 0:D], ALU.add).then_inc(added, 1)
                    dve.wait_ge(added, t.count(1, 2))
                    nc.vector.bn_stats(flat(t.of(stats)), xt)
                each_batch_far(dve, body)

    def masked_attention():
        with ExitStack() as st:
            sem = lambda n: st.enter_context(nc.semaphore(f"l1a_{n}"))
            (normed, turned, xT_ready, s_ready, shift_ready, exp_ready, e_turned, eT_ready, y_ready, own,
             added, *fin) = (sem(n) for n in ("normed", "turned", "xT", "s", "shift", "exp", "et", "eT", "y", "own",
                                              "added", "fin", "var", "rstd"))
            score = sb("score", [P, 2, P], F32, st)
            neg = sb("neg", [P, P], F32, st)
            shift = sb("shift", [P, 2], F32, st)
            total = sb("total", [P, 2], F32, st)
            factor = sb("factor", [P, 2], F32, st)
            kept = sb("kept", [P, NB], F32, st)
            e = sb("e", [P, 2, P], F32, st)
            eT = sb("eT", [P, 2, P], F32, st)
            block = st.enter_context(nc.Block())
            mask = small["mask"]
            zeroed = sem("zeroed")

            @block.sync
            def _(sp):
                rows = slots_in.rearrange("(t p) d -> p t d", p=P)
                for t in range(0, ROUTED, NB):
                    sp.dma_start(rows[:, t:t + NB, :], xn[:]).then_inc(zeroed, 16)
                sp.wait_ge(zeroed, 16 * ROUTED // NB)

            @block.gpsimd
            def _(pool):
                finish_pool(pool, *fin[1:])

            @block.tensor
            def _(pe):
                pe.wait_ge(ctxT_loaded, 16)

                def scores(b):
                    pe.wait_ge(normed, b.count(1, 1))
                    for c in range(C):
                        last = nc.tensor.transpose(bank[b.u][:, c * P:(c + 1) * P], xs[:, b.u, c * P:(c + 1) * P],
                                                   ident[:])
                    last.then_inc(turned, 1)
                    pe.wait_ge(xT_ready, b.count(1, 1))
                    for c in range(C):
                        last = nc.tensor.matmul(bank[2 + b.u][:, 0:P], xT[:, b.u, c, :], flat(b.of(ctxT)[:, :, c, :]),
                                                start=(c == 0), stop=(c == C - 1))
                    last.then_inc(s_ready, 1)

                def body(prev, b, nxt, far):
                    if prev is None:
                        scores(b)
                    if nxt:
                        scores(nxt)
                    pe.wait_ge(exp_ready, b.count(1, 1))
                    nc.tensor.transpose(bank[4 + b.u][:, 0:P], e[:, b.u, :], ident[:]).then_inc(e_turned, 1)
                    pe.wait_ge(eT_ready, b.count(1, 1))
                    nc.tensor.matmul(bank[6 + b.u][:, 0:D], eT[:, b.u, :], flat(b.of(ctx)), start=True,
                                     stop=True).then_inc(y_ready, 1)
                each_batch_far(pe, body)

            @block.scalar
            def _(act):
                def copy(b):
                    act.wait_ge(turned, b.count(1, 1))
                    nc.scalar.copy(flat(xT[:, b.u]), bank[b.u][:, 0:D]).then_inc(xT_ready, 1)

                def body(prev, b, nxt, far):
                    if prev is None:
                        copy(b)
                    if nxt:
                        copy(nxt)
                    act.wait_ge(shift_ready, b.count(1, 1))
                    nc.scalar.activation(e[:, b.u, :], score[:, b.u, :], ACT.Exp, bias=shift[:, b.u:b.u + 1],
                                         accum_out=total[:, b.u:b.u + 1]).then_inc(exp_ready, 1)
                each_batch_far(act, body)

            @block.vector
            def _(dve):
                finish_vector(dve, *fin)
                dve.wait_ge(rest_loaded, 32)
                step = Chain(dve, own)
                step(nc.vector.tensor_reduce(kept[:], mask[:], AX.X, ALU.max))
                step(nc.vector.tensor_scalar(kept[:], kept[:], tg_x[:, 1:2], None, ALU.mult))

                def masked(b, base):
                    step = Chain(dve, own, base)
                    mk = flat(b.of(mask))
                    step(nc.vector.tensor_scalar(neg[:], mk, -1.0, 1e30, ALU.add, ALU.mult))
                    dve.wait_ge(s_ready, b.count(1, 1))
                    step(nc.vector.scalar_tensor_tensor(score[:, b.u, :], bank[2 + b.u][:, 0:P], D ** -0.5, mk,
                                                        ALU.mult, ALU.mult))
                    step(nc.vector.tensor_tensor(score[:, b.u, :], score[:, b.u, :], neg[:], ALU.add))
                    step(nc.vector.tensor_reduce(shift[:, b.u:b.u + 1], score[:, b.u, :], AX.X, ALU.max))
                    nc.vector.tensor_scalar(shift[:, b.u:b.u + 1], shift[:, b.u:b.u + 1], -1.0, None,
                                            ALU.mult).then_inc(shift_ready, 1)

                def body(prev, b, nxt, far):
                    if prev is None:
                        norm_tile(xs[:, b.u, :], x, b).then_inc(normed, 1)
                        norm_tile(xs[:, nxt.u, :], x, nxt).then_inc(normed, 1)
                        masked(b, 2)
                    if far:
                        dve.wait_ge(turned, b.count(1, 1))
                        norm_tile(xs[:, far.u, :], x, far).then_inc(normed, 1)
                    dve.wait_ge(e_turned, b.count(1, 1))
                    nc.vector.tensor_copy(eT[:, b.u, :], bank[4 + b.u][:, 0:P]).then_inc(eT_ready, 1)
                    if nxt:
                        masked(nxt, nxt.count(6))
                    at = 10 if nxt else 6
                    nc.vector.reciprocal(factor[:, b.u:b.u + 1], total[:, b.u:b.u + 1]).then_inc(own, 1)
                    dve.wait_ge(own, b.count(6, at + 1))
                    nc.vector.tensor_scalar(factor[:, b.u:b.u + 1], factor[:, b.u:b.u + 1],
                                            b.of(kept), None, ALU.mult).then_inc(own, 1)
                    dve.wait_ge(own, b.count(6, at + 2))
                    dve.wait_ge(y_ready, b.count(1, 1))
                    nc.vector.scalar_tensor_tensor(flat(b.of(x)), bank[6 + b.u][:, 0:D], factor[:, b.u:b.u + 1],
                                                   flat(b.of(x)), ALU.mult, ALU.add).then_inc(added, 1)
                    dve.wait_ge(added, b.count(1, 1))
                    nc.vector.bn_stats(flat(b.of(stats)), flat(b.of(x)))
                each_batch_far(dve, body)

    def many_heads():
        H, HD, W = 32, 8, 8 * 9
        carve = carver()
        with ExitStack() as st:
            sem = lambda n: st.enter_context(nc.semaphore(f"l2a_{n}"))
            (normed, c_staged, turned, xT_ready, p_ready, squared, sum_ready, pow_done, v_ready, qk_ready, qk_turned,
             k_ready, q_spread, s_ready, e_ready, pv_done, pvT_ready, turned_back, o_ready, added, own, mask_ready,
             *fin) = (
                sem(n) for n in ("normed", "cs", "turned", "xT", "p", "sq", "sum", "pow", "v", "qk", "qkt", "k",
                                 "q", "s", "e", "pv", "pvT", "back", "o", "added", "own", "mk", "fin", "var", "rstd"))
            sq = flat(small["l0_win"])
            qk = small["l0_wout"]
            pvT = flat(small["l0_w"])
            cT = carve([P, 2, C, P])
            ss = carve([P, 2 * H])
            rn = carve([P, 2 * H])
            kT = carve([P, 2, C, P])
            qm = [carve([P, C, 4, P]) for _ in range(2)]
            rowmask = carve([P, 4])
            v = [carve([P, H * (W + HD + 1)]) for _ in range(2)]
            e = carve([P, 2, 4, P])
            inv = carve([P, H])
            o = carve([P, H, HD])
            block = st.enter_context(nc.Block())
            PROJ, Q_T, S, PV = (bank[1], bank[5]), bank[2], bank[3:5], bank[6:8]
            own_columns = [v[i][:].rearrange("p (h w) -> p h w", h=H) for i in range(2)]

            @block.sync
            def _(sp):
                load_experts(sp, 2)

            @block.gpsimd
            def _(pool):
                nc.gpsimd.memset(rowmask[:], 1.0).then_inc(mask_ready, 1)
                for i in range(2):
                    nc.gpsimd.memset(v[i][:], 0.0).then_inc(mask_ready, 1)
                pool.wait_ge(mask_ready, 3)
                for i in range(2):
                    nc.gpsimd.memset(own_columns[i][:, :, HD], 1.0).then_inc(mask_ready, 1)
                pool.wait_ge(mask_ready, 5)
                for g in range(4):
                    rm = rowmask[32 * g:32 * g + 32]
                    nc.gpsimd.affine_select(out=rm, in_=rm, compare_op=ALU.is_ge, fill=0.0, base=0,
                                            pattern=[[-HD, 4]], channel_multiplier=1).then_inc(mask_ready, 1)
                pool.wait_ge(mask_ready, 9)
                for g in range(4):
                    rm = rowmask[32 * g:32 * g + 32]
                    nc.gpsimd.affine_select(out=rm, in_=rm, compare_op=ALU.is_ge, fill=0.0, base=HD - 1,
                                            pattern=[[HD, 4]], channel_multiplier=-1).then_inc(mask_ready, 1)
                pool.wait_ge(mask_ready, 13)
                finish_pool(pool, *fin[1:])

                def roots(b, free):
                    if free is not None:
                        pool.wait_ge(qk_turned, free)
                    nc.gpsimd.tensor_copy(cT[:, b.u].rearrange("p c m -> p (c m)"),
                                          b.of(ctxT).rearrange("p a c m -> p (a c m)")).then_inc(c_staged, 1)
                    pool.wait_ge(sum_ready, b.count(1, 1))
                    nc.gpsimd.tensor_tensor(rn[:], ss[:], neg_half[:], ALU.pow).then_inc(pow_done, 1)

                def body(prev, b, nxt, far):
                    if prev is None:
                        roots(b, None)
                        roots(nxt, None)
                    if far:
                        roots(far, b.count(1, 1))
                each_batch_far(pool, body)

            @block.tensor
            def _(pe):
                def turn(b):
                    pe.wait_ge(normed, b.count(1, 1))
                    for c in range(C):
                        last = nc.tensor.transpose(bank[0][:, c * P:(c + 1) * P], xs[:, b.u, c * P:(c + 1) * P],
                                                   ident[:])
                    last.then_inc(turned, 1)

                def product(out, lhs, w):
                    for c in range(C):
                        last = nc.tensor.matmul(out, lhs[:, c, :], small[w][:, c, :], start=(c == 0),
                                                stop=(c == C - 1))
                    return last

                def project(b):
                    pe.wait_ge(c_staged, b.count(1, 1))
                    pe.wait_ge(xT_ready, b.count(1, 1))
                    product(PROJ[b.u][:, 0:D], xT[:, 0], "l2_wq")
                    product(PROJ[b.u][:, D:2 * D], cT[:, b.u], "l2_wk").then_inc(p_ready, 1)

                def turn_qk(b):
                    product(bank[0][:, D:2 * D], cT[:, b.u], "l2_wv")
                    pe.wait_ge(qk_ready, b.count(1, 1))
                    for i, out in enumerate((Q_T, bank[0])):
                        for c in range(C):
                            last = nc.tensor.transpose(out[:, c * P:(c + 1) * P], qk[:, i, c * P:(c + 1) * P], ident[:])
                    last.then_inc(qk_turned, 1)

                def turn_back(b):
                    pe.wait_ge(pvT_ready, b.count(1, 1))
                    for t in range(4):
                        last = nc.tensor.transpose(PV[b.u][:, t * W:(t + 1) * W], pvT[0:W, t * P:(t + 1) * P],
                                                   ident[0:W, 0:W])
                    last.then_inc(turned_back, 1)

                def body(prev, b, nxt, far):
                    if prev is None:
                        turn(b)
                        project(b)
                        turn(nxt)
                        project(nxt)
                        turn_qk(b)
                    for n in range(8 + 1):
                        if n < 8:
                            c, g = divmod(n, 4)
                            rows = slice(32 * g, 32 * g + 32)
                            if n == 0:
                                pe.wait_ge(q_spread, b.count(2, 2))
                                pe.wait_ge(k_ready, b.count(1, 1))
                            nc.tensor.matmul(S[n % 2][:], kT[rows, b.u, c, :],
                                             qm[b.u][rows, c].rearrange("p j q -> p (j q)"), start=True, stop=True,
                                             tile_position=(32 * g, 0)).then_inc(s_ready, 1)
                        if n >= 1:
                            m = n - 1
                            pe.wait_ge(e_ready, b.count(8, m + 1))
                            if m == 0:
                                pe.wait_ge(v_ready, b.count(1, 1))
                            for j in range(4):
                                t, i = divmod(4 * m + j, 8)
                                at = t * 8 * (W + HD + 1) + i * W
                                last = nc.tensor.matmul(PV[b.u][0:W, t * P:(t + 1) * P], v[b.u][:, at:at + W],
                                                        e[:, m % 2, j, :], start=(i == 0), stop=(i == 7))
                            last.then_inc(pv_done, 1)
                        if n == 1 and far:
                            turn(far)
                        if n == 2 and far:
                            project(far)
                        if n == 2 and prev:
                            turn_back(prev)
                        if n == 5 and nxt:
                            turn_qk(nxt)
                    if nxt is None:
                        turn_back(b)
                each_batch_far(pe, body)

            @block.scalar
            def _(act):
                def copy_x(b):
                    act.wait_ge(turned, b.count(1, 1))
                    nc.scalar.copy(flat(xT[:, 0]), bank[0][:, 0:D]).then_inc(xT_ready, 1)

                def square(b):
                    act.wait_ge(p_ready, b.count(1, 1))
                    nc.scalar.activation(sq, PROJ[b.u][:], ACT.Square).then_inc(squared, 1)

                def copy_v_k(b):
                    act.wait_ge(qk_turned, b.count(1, 1))
                    nc.scalar.copy(own_columns[b.u][:, :, 0:HD],
                                   bank[0][:, D:2 * D].rearrange("p (h d) -> p h d", h=H)).then_inc(v_ready, 1)
                    nc.scalar.copy(flat(kT[:, b.u]), bank[0][:, 0:D]).then_inc(k_ready, 1)

                def copy_sums(b):
                    act.wait_ge(pv_done, b.count(8, 8))
                    nc.scalar.copy(pvT[0:W, :], PV[b.u][0:W, :]).then_inc(pvT_ready, 1)

                act.wait_ge(mask_ready, 5)

                def body(prev, b, nxt, far):
                    if prev is None:
                        copy_x(b)
                        square(b)
                        copy_x(nxt)
                        act.wait_ge(sum_ready, 1)
                        square(nxt)
                        copy_v_k(b)
                    for n in range(8):
                        act.wait_ge(s_ready, b.count(8, n + 1))
                        nc.scalar.activation(e[:, n % 2].rearrange("p j q -> p (j q)"), S[n % 2][:], ACT.Exp,
                                             scale=HD ** -0.5).then_inc(e_ready, 1)
                        if n == 0 and prev:
                            copy_sums(prev)
                        if n == 1 and far:
                            copy_x(far)
                        if n == 3 and far:
                            square(far)
                        if n == 5 and nxt:
                            copy_v_k(nxt)
                    if nxt is None:
                        copy_sums(b)
                each_batch_far(act, body)

            @block.vector
            def _(dve):
                finish_vector(dve, *fin)
                dve.wait_ge(mask_ready, 13)

                def norm(b):
                    norm_tile(xs[:, b.u, :], x, b).then_inc(normed, 1)

                def sums(b):
                    dve.wait_ge(squared, b.count(1, 1))
                    nc.vector.tensor_reduce(ss[:], sq.rearrange("p (h d) -> p h d", d=HD), AX.X,
                                            ALU.add).then_inc(own, 1)
                    dve.wait_ge(own, b.count(1, 1))
                    nc.vector.tensor_scalar(ss[:], ss[:], 1.0 / HD, 1e-6, ALU.mult, ALU.add).then_inc(sum_ready, 1)

                def scale(b):
                    dve.wait_ge(pow_done, b.count(1, 1))
                    nc.vector.tensor_tensor(qk.rearrange("p i (h d) -> p (i h) d", h=H),
                                            PROJ[b.u][:].rearrange("p (h d) -> p h d", d=HD),
                                            rn[:].unsqueeze(2).broadcast_to([P, 2 * H, HD]),
                                            ALU.mult).then_inc(qk_ready, 1)

                def spread(b):
                    dve.wait_ge(qk_turned, b.count(1, 1))
                    for c in range(C):
                        nc.vector.tensor_tensor(qm[b.u][:, c],
                                                Q_T[:, c * P:(c + 1) * P].unsqueeze(1).broadcast_to([P, 4, P]),
                                                rowmask[:].unsqueeze(2).broadcast_to([P, 4, P]),
                                                ALU.mult).then_inc(q_spread, 1)

                def finish(b):
                    dve.wait_ge(turned_back, b.count(1, 1))
                    pv = PV[b.u][:, 0:H * (HD + 1)].rearrange("p (h d) -> p h d", h=H)
                    nc.vector.reciprocal(inv[:], pv[:, :, HD]).then_inc(o_ready, 1)
                    dve.wait_ge(o_ready, b.count(2, 1))
                    nc.vector.tensor_tensor(o[:], pv[:, :, 0:HD], inv[:].unsqueeze(2).broadcast_to([P, H, HD]),
                                            ALU.mult).then_inc(o_ready, 1)
                    dve.wait_ge(o_ready, b.count(2, 2))
                    nc.vector.scalar_tensor_tensor(flat(b.of(x)), flat(o[:]), tg_x[:, 2:3], flat(b.of(x)), ALU.mult,
                                                   ALU.add).then_inc(added, 1)
                    dve.wait_ge(added, b.count(1, 1))
                    nc.vector.bn_stats(flat(b.of(stats)), flat(b.of(x)))

                def body(prev, b, nxt, far):
                    if prev is None:
                        norm(b)
                        norm(nxt)
                        sums(b)
                        scale(b)
                        sums(nxt)
                        spread(b)
                    if far:
                        dve.wait_ge(turned, b.count(1, 1))
                        norm(far)
                    if nxt:
                        scale(nxt)
                    if prev:
                        finish(prev)
                    if far:
                        sums(far)
                    if nxt:
                        spread(nxt)
                    if nxt is None:
                        finish(b)
                each_batch_far(dve, body)

    def channel_heads():
        H, HD, L = 8, 16, D
        scale = HD ** -0.5
        G, N = 4, 8
        carve = carver()
        with ExitStack() as st:
            sem = lambda n: st.enter_context(nc.semaphore(f"l3a_{n}"))
            (normed, k_spread, v_ready, s_ready, m_ready, e_ready, e_turned, eT_ready, pv_done, i_ready, o_ready,
             o_turned, out_ready, added, mask_ready, *fin) = (
                sem(n) for n in ("normed", "ks", "v", "s", "m", "e", "et", "eT", "pv", "i", "o", "ot", "out", "added",
                                 "mk", "fin", "var", "rstd"))
            km = [carve([P, 2, L]) for _ in range(2)]
            rowmask = carve([P, 2, L])
            mx = carve([P, 4, 2])
            e = [carve([P, 2, L]) for _ in range(4)]
            eT = carve([P, 2, 4, P])
            v = [carve([P, C, H * (P + HD)]) for _ in range(2)]
            total = carve([P, 2, 2, H])
            o = carve([P, 2, H, HD])
            out = carve([P, L])
            gf = carve([P, 1])
            block = st.enter_context(nc.Block())
            S = (bank[0], bank[1], bank[5], bank[7])
            PV, E_T, O_T = bank[3:5], bank[2], bank[6]

            @block.sync
            def _(sp):
                load_experts(sp, 3)

            @block.gpsimd
            def _(pool):
                nc.gpsimd.memset(rowmask[:], -scale).then_inc(mask_ready, 1)
                for i in range(2):
                    nc.gpsimd.memset(v[i][:], 0.0).then_inc(mask_ready, 1)
                pool.wait_ge(mask_ready, 3)
                for g in range(G):
                    rm = rowmask[32 * g:32 * g + 32]
                    nc.gpsimd.affine_select(out=rm, in_=rm, compare_op=ALU.is_ge, fill=0.0, base=0,
                                            pattern=[[-HD, 2], [0, L]], channel_multiplier=1).then_inc(mask_ready, 1)
                pool.wait_ge(mask_ready, 3 + G)
                for g in range(G):
                    rm = rowmask[32 * g:32 * g + 32]
                    nc.gpsimd.affine_select(out=rm, in_=rm, compare_op=ALU.is_ge, fill=0.0, base=HD - 1,
                                            pattern=[[HD, 2], [0, L]], channel_multiplier=-1).then_inc(mask_ready, 1)
                pool.wait_ge(mask_ready, 3 + 2 * G)
                finish_pool(pool, *fin[1:])

                def prep(b, free):
                    if free is not None:
                        pool.wait_ge(pv_done, free)
                    for j in range(2):
                        nc.gpsimd.tensor_tensor(km[b.u][:, j, :], flat(b.of(ctx)), rowmask[:, j, :],
                                                ALU.mult).then_inc(k_spread, 1)
                    for c in range(C):
                        nc.gpsimd.tensor_copy(v[b.u][:, c, :].rearrange("p (h w) -> p h w", h=H)[:, :, 0:HD],
                                              flat(b.of(ctxT)[:, :, c, :]).rearrange("p (h d) -> p h d", h=H)
                                              ).then_inc(v_ready, 1)

                def body(prev, b, nxt):
                    if prev is None:
                        prep(b, None)
                    if nxt:
                        prep(nxt, prev and prev.count(N, N))
                each_batch(pool, body)

            @block.tensor
            def _(pe):
                def scores(b, n):
                    qh, g = divmod(n, G)
                    rows = slice(32 * g, 32 * g + 32)
                    if n == 0:
                        pe.wait_ge(normed, b.count(1, 1))
                        pe.wait_ge(k_spread, b.count(2, 2))
                        pe.wait_ge(v_ready, b.count(2, 2))
                    nc.tensor.matmul(S[n % 4][:], xs[rows, b.u, qh * P:(qh + 1) * P],
                                     km[b.u][rows].rearrange("p j l -> p (j l)"), start=True, stop=True,
                                     tile_position=(32 * g, 0)).then_inc(s_ready, 1)

                def turn(b, n):
                    pe.wait_ge(e_ready, b.count(2 * N, 2 * n + 2))
                    if not (b.j is None and b.k == 0 and n == 0):
                        pe.wait_ge(eT_ready, b.count(N, n))
                    for j in range(2):
                        for c in range(C):
                            k = j * C + c
                            last = nc.tensor.transpose(E_T[:, k * P:(k + 1) * P],
                                                       e[n % 4][:, j, c * P:(c + 1) * P], ident[:])
                    last.then_inc(e_turned, 1)

                def values(b, n):
                    qh, g = divmod(n, G)
                    pe.wait_ge(eT_ready, b.count(N, n + 1))
                    for j in range(2):
                        h = 2 * g + j
                        for c in range(C):
                            last = nc.tensor.matmul(PV[b.u][:, qh * P:(qh + 1) * P], v[b.u][:, c, h * P:(h + 1) * P],
                                                    eT[:, n % 2, j * C + c, :], start=(h == 0 and c == 0),
                                                    stop=(h == H - 1 and c == C - 1))
                    last.then_inc(pv_done, 1)

                def turn_back(b):
                    pe.wait_ge(o_ready, b.count(1, 1))
                    for qh in range(2):
                        last = nc.tensor.transpose(O_T[:, qh * P:(qh + 1) * P],
                                                   o[:, qh].rearrange("p h d -> p (h d)"), ident[:])
                    last.then_inc(o_turned, 1)

                def body(prev, b, nxt):
                    for n in range(N):
                        scores(b, n)
                        if n >= 2:
                            turn(b, n - 2)
                        elif prev:
                            turn(prev, N - 2 + n)
                        if n >= 3:
                            values(b, n - 3)
                        elif prev:
                            values(prev, N - 3 + n)
                        if n == 5 and prev:
                            turn_back(prev)
                    if nxt is None:
                        turn(b, N - 2)
                        values(b, N - 3)
                        turn(b, N - 1)
                        values(b, N - 2)
                        values(b, N - 1)
                        turn_back(b)
                each_batch(pe, body)

            @block.scalar
            def _(act):
                def body(prev, b, nxt):
                    for n in range(N):
                        qh, g = divmod(n, G)
                        act.wait_ge(m_ready, b.count(N, n + 1))
                        for j in range(2):
                            nc.scalar.activation(e[n % 4][:, j, :], S[n % 4][:, j * L:(j + 1) * L], ACT.Exp,
                                                 bias=mx[:, n % 4, j:j + 1], scale=-1.0,
                                                 accum_out=total[:, b.u, qh, 2 * g + j:2 * g + j + 1]
                                                 ).then_inc(e_ready, 1)
                each_batch(act, body)

            @block.vector
            def _(dve):
                nc.vector.tensor_tensor(gf[:], small["l3_gamma"], tg_x[:, 3:4], ALU.mult)
                finish_vector(dve, *fin)

                def extremes(b, n):
                    dve.wait_ge(s_ready, b.count(N, n + 1))
                    nc.vector.tensor_reduce(mx[:, n % 4, :], S[n % 4][:].rearrange("p (j l) -> p j l", j=2), AX.X,
                                            ALU.min).then_inc(m_ready, 1)

                def copy(b, n):
                    dve.wait_ge(e_turned, b.count(N, n + 1))
                    nc.vector.tensor_copy(eT[:, n % 2].rearrange("p a q -> p (a q)"),
                                          E_T[:]).then_inc(eT_ready, 1)

                def divide(b):
                    dve.wait_ge(e_ready, b.count(2 * N, 2 * N))
                    tot = flat(total[:, b.u])
                    nc.vector.reciprocal(tot, tot).then_inc(i_ready, 1)
                    dve.wait_ge(i_ready, b.count(1, 1))
                    nc.vector.tensor_copy(o[:].rearrange("p q h d -> p (q h) d"),
                                          tot.unsqueeze(2).broadcast_to([P, 2 * H, HD])).then_inc(o_ready, 1)

                def add(b):
                    dve.wait_ge(o_turned, b.count(1, 1))
                    dve.wait_ge(pv_done, b.count(N, N))
                    nc.vector.tensor_scalar(out[:], PV[b.u][:, 0:L], gf[:, 0:1], None, ALU.mult).then_inc(out_ready, 1)
                    dve.wait_ge(out_ready, b.count(2, 1))
                    nc.vector.tensor_tensor(out[:], out[:], O_T[:, 0:L], ALU.mult).then_inc(out_ready, 1)
                    dve.wait_ge(out_ready, b.count(2, 2))
                    nc.vector.tensor_tensor(flat(b.of(x)), flat(b.of(x)), out[:], ALU.add).then_inc(added, 1)
                    dve.wait_ge(added, b.count(1, 1))
                    nc.vector.bn_stats(flat(b.of(stats)), flat(b.of(x)))

                def body(prev, b, nxt):
                    if prev is None:
                        norm_tile(xs[:, b.u, :], x, b).then_inc(normed, 1)
                    for n in range(N):
                        extremes(b, n)
                        if n >= 2:
                            copy(b, n - 2)
                        elif prev:
                            copy(prev, N - 2 + n)
                        if prev and n == 3:
                            divide(prev)
                        if prev and n == 7:
                            add(prev)
                        if nxt and n == 5:
                            norm_tile(xs[:, nxt.u, :], x, nxt).then_inc(normed, 1)
                    if nxt is None:
                        copy(b, N - 2)
                        copy(b, N - 1)
                        divide(b)
                        add(b)
                each_batch(dve, body)

    def route(layer):
        m = MOE[layer]
        R = 17 if layer == 1 else 16
        router = small[f"l{layer}_router"]
        with ExitStack() as st:
            sem = lambda n: nc.alloc_semaphore(f"r{layer}_{n}")
            turned, xT_ready, l_ready, own, act_done, to_act, taken = (
                sem(n) for n in ("turned", "xT", "l", "own", "act", "ta", "taken"))
            carve = carver(layer)
            lg = carve([P, NB, R])
            prob = carve([P, NB, PAD])
            rep = carve([P, NB, PAD])
            row = carve([P, 3, NB])
            sel = carve([P, NB, NE])
            acc = carve([P, NE, NB])
            go_on = carve([P, NE, NB])
            nt = carve([P, 2, NE])
            before = carve([P, P])
            normed, xn_ready, *fin = (sem(n) for n in ("normed", "xn", "fin", "var", "rstd"))
            sel_ready, counted, tri_ready = (sem(n) for n in ("sel", "counted", "tri"))
            block = st.enter_context(nc.Block())

            @block.gpsimd
            def _(pool):
                nc.gpsimd.memset(before[:], 1.0).then_inc(tri_ready, 1)
                pool.wait_ge(tri_ready, 1)
                nc.gpsimd.affine_select(out=before[:], in_=before[:], compare_op=ALU.is_gt, fill=0.0, base=0,
                                        pattern=[[1, P]], channel_multiplier=-1).then_inc(tri_ready, 1)
                pool.wait_ge(tri_ready, 2)
                finish_pool(pool, *fin[1:])

            @block.tensor
            def _(pe):
                def turn(b):
                    pe.wait_ge(normed, b.count(1, 1))
                    for c in range(C):
                        last = nc.tensor.transpose(bank[b.u][:, c * P:(c + 1) * P], xs[:, b.u, c * P:(c + 1) * P],
                                                   ident[:])
                    last.then_inc(turned, 1)

                def body(prev, b, nxt, far):
                    if prev is None:
                        turn(b)
                    if nxt:
                        turn(nxt)
                    pe.wait_ge(xT_ready, b.count(1, 1))
                    pe.wait_ge(taken, b.count(1, 1))
                    for c in range(C):
                        last = nc.tensor.matmul(bank[2 + b.u][:, 0:R], xT[:, b.u, c, :], router[:, c, :],
                                                start=(c == 0), stop=(c == C - 1))
                    last.then_inc(l_ready, 1)
                each_batch_far(pe, body)
                pe.wait_ge(tri_ready, 2)
                pe.wait_ge(sel_ready, 1)
                nc.tensor.matmul(bank[2][:, 0:D], before[:], flat(sel[:]), start=True, stop=True)
                nc.tensor.matmul(bank[3][:, 0:D], ones[:], sel[:].rearrange("p t e -> p e t"), start=True,
                                 stop=True).then_inc(counted, 1)

            @block.scalar
            def _(act):
                def body(prev, b, nxt, far):
                    act.wait_ge(turned, b.count(1, 1))
                    nc.scalar.copy(flat(xT[:, b.u]), bank[b.u][:, 0:D]).then_inc(xT_ready, 1)
                each_batch_far(act, body)
                act.wait_ge(to_act, 1)
                if layer == 1:
                    nc.scalar.activation(prob[:, :, 0:NE], prob[:, :, 0:NE], ACT.Exp).then_inc(act_done, 1)
                    nc.scalar.activation(row[:, 2, :], lg[:, :, NE], ACT.Sigmoid).then_inc(act_done, 1)
                else:
                    nc.scalar.activation(lg[:], lg[:], ACT.Sigmoid).then_inc(act_done, 1)

            @block.vector
            def _(dve):
                bc = lambda a, n=NE: a.unsqueeze(2).broadcast_to([P, NB, n])
                nc.vector.memset(prob[:], FILL).then_inc(own, 1)
                nc.vector.memset(best[:], FILL).then_inc(own, 1)
                finish_vector(dve, *fin)
                dve.sem_inc(taken, 2)

                def body(prev, b, nxt, far):
                    if prev is None:
                        norm_tile(xs[:, 0, :], x, b).then_inc(normed, 1)
                        norm_tile(xs[:, 1, :], x, nxt).then_inc(normed, 1)
                    if far:
                        dve.wait_ge(turned, b.count(1, 1))
                        norm_tile(xs[:, far.u, :], x, far).then_inc(normed, 1)
                    norm_tile(flat(b.of(xn)), x, b).then_inc(xn_ready, 1)
                    dve.wait_ge(l_ready, b.count(1, 1))
                    nc.vector.tensor_copy(flat(b.of(lg)), bank[2 + b.u][:, 0:R]).then_inc(taken, 1)
                each_batch_far(dve, body)
                dve.wait_ge(taken, NB + 2)
                dve.wait_ge(xn_ready, NB)
                dve.wait_ge(own, 2)
                step = Chain(dve, own, 2)
                if layer == 1:
                    step(nc.vector.tensor_reduce(row[:, 0, :], lg[:, :, 0:NE], AX.X, ALU.max))
                    nc.vector.tensor_tensor(prob[:, :, 0:NE], lg[:, :, 0:NE], bc(row[:, 0, :]),
                                            ALU.subtract).then_inc(to_act, 1)
                    dve.wait_ge(act_done, 2)
                    step(nc.vector.tensor_reduce(row[:, 0, :], prob[:, :, 0:NE], AX.X, ALU.add))
                    step(nc.vector.reciprocal(row[:, 0, :], row[:, 0, :]))
                    step(nc.vector.tensor_tensor(prob[:, :, 0:NE], prob[:, :, 0:NE], bc(row[:, 0, :]), ALU.mult))
                    score = prob[:, :, 0:NE]
                else:
                    dve.sem_inc(to_act, 1)
                    dve.wait_ge(act_done, 1)
                    score = lg[:]
                    if layer == 2:
                        step(nc.vector.tensor_copy(prob[:, :, 0:NE], score))
                    else:
                        g4 = prob[:, :, 0:NE].rearrange("p t (g i) -> p t g i", g=4)
                        step(nc.vector.tensor_tensor(prob[:, :, 0:NE], score,
                                                     small["l3_ebias"][:].unsqueeze(1).broadcast_to([P, NB, NE]),
                                                     ALU.add))
                        hi = carve([P, NB, 4, 2])
                        lo = carve([P, NB, 4, 2])
                        f = lambda a: a.rearrange("p t g -> p (t g)")
                        for k in range(2):
                            step(nc.vector.tensor_tensor(hi[:, :, :, k], g4[:, :, :, 2 * k], g4[:, :, :, 2 * k + 1],
                                                         ALU.max))
                            step(nc.vector.tensor_tensor(lo[:, :, :, k], g4[:, :, :, 2 * k], g4[:, :, :, 2 * k + 1],
                                                         ALU.min))
                        g1 = carve([P, NB, 4])
                        g2 = carve([P, NB, 4])
                        step(nc.vector.tensor_tensor(g1[:], hi[:, :, :, 0], hi[:, :, :, 1], ALU.max))
                        step(nc.vector.tensor_tensor(g2[:], hi[:, :, :, 0], hi[:, :, :, 1], ALU.min))
                        step(nc.vector.tensor_tensor(lo[:, :, :, 0], lo[:, :, :, 0], lo[:, :, :, 1], ALU.max))
                        step(nc.vector.tensor_tensor(g2[:], g2[:], lo[:, :, :, 0], ALU.max))
                        step(nc.vector.tensor_tensor(g1[:], g1[:], g2[:], ALU.add))
                        rank = carve([P, NB, 4])
                        cmp = carve([P, NB])
                        step(nc.vector.memset(rank[:], 0.0))
                        for j in range(4):
                            for g in range(j + 1, 4):
                                step(nc.vector.tensor_tensor(cmp[:], g1[:, :, j], g1[:, :, g], ALU.is_ge))
                                step(nc.vector.tensor_tensor(rank[:, :, g], rank[:, :, g], cmp[:], ALU.add))
                                step(nc.vector.tensor_tensor(cmp[:], g1[:, :, g], g1[:, :, j], ALU.is_gt))
                                step(nc.vector.tensor_tensor(rank[:, :, j], rank[:, :, j], cmp[:], ALU.add))
                        step(nc.vector.tensor_scalar(rank[:], rank[:], 1.5, None, ALU.is_lt))
                        r4 = rank[:].unsqueeze(3).broadcast_to([P, NB, 4, 4])
                        step(nc.vector.tensor_scalar(g2[:], rank[:], -1.0, -BARRED, ALU.add, ALU.mult))
                        step(nc.vector.tensor_tensor(g4, g4, r4, ALU.mult))
                        step(nc.vector.tensor_tensor(g4, g4, g2[:].unsqueeze(3).broadcast_to([P, NB, 4, 4]), ALU.add))
                for i in range(NB):
                    nc.vector.max(best[:, i, :], prob[:, i, 0:NE]).then_inc(own, 1)
                step.n += NB
                dve.wait_ge(own, 2 + step.n)
                step(nc.vector.memset(best[:, :, m["k"]:8], FILL))
                for i in range(NB):
                    nc.vector.match_replace(rep[:, i, :], best[:, i, :], prob[:, i, :], TAKEN).then_inc(own, 1)
                step.n += NB
                dve.wait_ge(own, 2 + step.n)
                w = comb[:, :, 0:NE]
                step(nc.vector.tensor_scalar(sel[:], rep[:, :, 0:NE], TAKEN, None, ALU.is_equal))
                dve.sem_inc(sel_ready, 1)
                step(nc.vector.tensor_tensor(w, sel[:], score, ALU.mult))
                step(nc.vector.tensor_reduce(row[:, 0, :], w, AX.X, ALU.add))
                if layer == 1:
                    step(nc.vector.tensor_scalar(row[:, 0, :], row[:, 0, :], 1e-9, None, ALU.max))
                if layer == 3:
                    step(nc.vector.tensor_scalar(row[:, 0, :], row[:, 0, :], 1e-20, None, ALU.add))
                step(nc.vector.reciprocal(row[:, 0, :], row[:, 0, :]))
                if layer == 3:
                    step(nc.vector.tensor_scalar(row[:, 0, :], row[:, 0, :], 2.5, None, ALU.mult))
                step(nc.vector.tensor_scalar(row[:, 0, :], row[:, 0, :], tg_f[:, layer:layer + 1], None, ALU.mult))
                step(nc.vector.tensor_tensor(w, w, bc(row[:, 0, :]), ALU.mult))
                n = m["E"] - NE
                if layer == 1:
                    step(nc.vector.tensor_scalar(row[:, 2, :], row[:, 2, :], tg_f[:, 1:2], None, ALU.mult))
                    step(nc.vector.tensor_copy(comb[:, :, NE:NE + n], bc(row[:, 2, :], n)))
                else:
                    step(nc.vector.memset(comb[:, :, NE:NE + n], 1.0))
                    step(nc.vector.tensor_scalar(comb[:, :, NE:NE + n], comb[:, :, NE:NE + n],
                                                 tg_f[:, layer:layer + 1], None, ALU.mult))
                if layer == 2:
                    for b in range(NB):
                        nc.vector.scalar_tensor_tensor(x[:, b, :], xn[:, b, :], tg_f[:, 2:3], x[:, b, :], ALU.mult,
                                                       ALU.add)
                assign_slots(layer, dve, step, sel, acc, go_on, nt,
                             bank[2][:, 0:D].rearrange("p (t e) -> p t e", t=NB),
                             bank[3][:, 0:D].rearrange("p (e t) -> p e t", t=NB), counted)

    def shape_of(layer):
        m = MOE[layer]
        shared = m["E"] - NE
        routed = (m["k"] * NB * P + NE * (P - 1)) // P
        routed += -routed % 8
        return m["k"], shared, shared * NB, routed

    def assign_slots(layer, dve, step, sel, acc, go_on, nt, PRE, CNT, counted):
        k, shared, first, routed = shape_of(layer)
        step(nc.vector.memset(go_on[:], 1.0))
        step(nc.vector.memset(go_on[:, :, 0:1], 0.0))
        dve.wait_ge(counted, 1)
        step(nc.vector.tensor_tensor_scan(flat(acc[:]), flat(go_on[:]), flat(CNT), 0.0, ALU.mult, ALU.add))
        step(nc.vector.tensor_scalar(nt[:, 1, :], acc[:, :, NB - 1], 1.0 / P, None, ALU.mult))
        step(nc.vector.tensor_tensor(go_on[:], nt[:, 1, :].unsqueeze(2).broadcast_to([P, NE, NB]),
                                     numbers[:, 0:NB].unsqueeze(1).broadcast_to([P, NE, NB]), ALU.is_gt))
        step(nc.vector.tensor_reduce(nt[:, 0, :], go_on[:], AX.X, ALU.add))
        step(nc.vector.tensor_tensor(acc[:], acc[:], CNT, ALU.subtract))
        step(nc.vector.tensor_tensor_scan(nt[:, 1, :], ones[:, 0:NE], nt[:, 0, :], 0.0, ALU.mult, ALU.add))
        step(nc.vector.tensor_tensor(nt[:, 0, :], nt[:, 1, :], nt[:, 0, :], ALU.subtract))
        step(nc.vector.tensor_scalar(nt[:, 0, :], nt[:, 0, :], float(P), 1.0, ALU.mult, ALU.add))
        step(nc.vector.tensor_tensor(slot[:], acc[:].rearrange("p e t -> p t e"),
                                     nt[:, 0:1, :].broadcast_to([P, NB, NE]), ALU.add))
        step(nc.vector.tensor_tensor(slot[:], slot[:], PRE, ALU.add))
        step(nc.vector.tensor_tensor(slot[:], slot[:], sel[:], ALU.mult))
        for t in range(NB):
            nc.vector.max(best[:, t, :], slot[:, t, :]).then_inc(step.sem, 1)
        step.n += NB
        dve.wait_ge(step.sem, step.base + step.n)
        step(nc.vector.tensor_scalar(row_in[:, :, 0:k], best[:, :, 0:k], -1.0, None, ALU.add))
        step(nc.vector.tensor_scalar(row_out[:, :, 0:k], best[:, :, 0:k], first * P - 1.0, None, ALU.add))
        for s in range(shared):
            step(nc.vector.memset(tile_expert_f[:, s * NB:(s + 1) * NB], float(NE + s)))
        mine = tile_expert_f[:, first:first + routed]
        step(nc.vector.memset(mine, 0.0))
        for e in range(NE):
            step(nc.vector.scalar_tensor_tensor(mine, numbers[0:1, 0:routed], nt[0:1, 1, e:e + 1], mine, ALU.is_ge,
                                                ALU.add))
        step(nc.vector.tensor_scalar(mine, mine, NE - 1.0, None, ALU.min))
        step(nc.vector.tensor_copy(tile_expert[:, 0:first + routed], tile_expert_f[:, 0:first + routed]))

    def bias_parts(pool, load, bias_raw, part, b_in, own):
        step = Chain(pool, own)
        for i in range(NCH):
            load(i).then_inc(b_in, 16)
            pool.wait_ge(b_in, 16 * (i + 1))
            cols = slice(i * CH, (i + 1) * CH)
            step(nc.gpsimd.tensor_copy(part[0][:], bias_raw[:]))
            step(nc.gpsimd.tensor_tensor(bias_raw[:], bias_raw[:], part[0][:], ALU.subtract))
            step(nc.gpsimd.tensor_copy(part[1][:], bias_raw[:]))
            step(nc.gpsimd.tensor_tensor(bias_raw[:], bias_raw[:], part[1][:], ALU.subtract))
            step(nc.gpsimd.tensor_copy(gbias[0:3, cols], bias_raw[:]))
            step(nc.gpsimd.tensor_copy(gbias[0:2, cols], part[1][0:2, :]))
            step(nc.gpsimd.tensor_copy(gbias[0:1, cols], part[0][0:1, :]))

    def slot_experts(layer):
        m = MOE[layer]
        I, parts = m["I"], m["parts"]
        k, shared, first, routed = shape_of(layer)
        total = first + routed
        gu_w, dn_w, kp = moe_views(layer)
        func = ACT.Gelu if layer == 2 else ACT.Silu
        U = 4 if layer == 1 else 8
        turns = total // U - 1
        with ExitStack() as st:
            sem = lambda n: nc.alloc_semaphore(f"m{layer}_{n}")
            (turned, xT_ready, gu_ready, sg_ready, h_ready, h_turned, hT_ready, y_ready, y_copied, ones_ready,
             scattered) = (sem(n) for n in ("turned", "xT", "gu", "sg", "h", "ht", "hT", "y", "yc", "one", "sc"))
            loaded = [sem(f"loaded{i}") for i in range(U)]
            stored = [sem(f"stored{i}") for i in range(U)]
            carve = carver(layer)
            h = carve([P, 2, I])
            hT = carve([kp, 2, parts, P])
            ones3 = sb(f"ones3{layer}", [3, P], BF16, st)
            if layer == 1:
                bias_raw = sb("bias_raw", [3, CH], F32, st)
                part = [sb(f"bias_part{i}", [3, CH], BF16, st) for i in range(2)]
                b_in, b_own = sem("bin"), sem("bown")
            xg2 = carve([P, U - 2, D])
            y = carve([P, U, D])
            block = st.enter_context(nc.Block())
            GU, HT, Y, XT = bank[0:2], bank[2:4], bank[4:6], bank[6:8]
            xg = [xs[:, 0:1], xs[:, 1:2]] + [xg2[:, i:i + 1] for i in range(U - 2)]
            if layer == 2:
                gb = gbias[:].rearrange("p (e n) -> p e n", e=m["E"])

            class Tile:

                def __init__(self, c, j=None):
                    self.c, self.j = c, j

                def __sub__(self, d):
                    return Tile(self.c - d, self.j)

                def there(self):
                    return self.j is not None or 0 <= self.c < total

                def count(self, plus=1):
                    return self.c + plus if self.j is None else self.j * U + (self.c + plus)

                def count_dma(self, plus=1):
                    turn = (self.c // U + plus) * 16
                    return turn if self.j is None else self.j * 16 + turn

                def of(self, view):
                    if self.j is None:
                        return view[:, self.c:self.c + 1]
                    lo = self.c - self.c % U
                    names = " ".join("abcd"[:len(view.shape) - 2])
                    v = view[:, lo:lo + U * turns].rearrange(f"p (j u) {names} -> p j u {names}", u=U)
                    return v[:, ds(self.j, 1), self.c % U]

            def each_step(eng, step):
                for c in range(U):
                    step(Tile(c))
                with eng.Fori(0, turns) as j:
                    for c in range(U, 2 * U):
                        step(Tile(c, j))
                for c in range(total, total + 4):
                    step(Tile(c))

            @block.gpsimd
            def _(pool):
                for t in range(NB):
                    for i in range(k):
                        pool.indirect_dma_start(out=slots_in, in_=xn[:, t, :], in_offset=None,
                                                out_offset=bass.IndirectOffsetOnAxis(ap=row_in[:, t, i:i + 1], axis=0)
                                                ).then_inc(scattered, 16)
                if layer == 1:
                    bias_parts(pool, lambda i: pool.dma_start(bias_raw[:], io["l2_gub"][:, i * CH:(i + 1) * CH]),
                               bias_raw, part, b_in, b_own)

            @block.sync
            def _(sp):
                for s in range(shared):
                    with sp.Fori(0, NB // U) as j:
                        for u in range(U):
                            sp.wait_ge(turned, j * U + (s * NB + u + 1))
                            src = xn[:].rearrange("p (j u) d -> p j u d", u=U)[:, ds(j, 1), u]
                            sp.dma_start(xg[u], src).then_inc(loaded[u], 16)
                sp.wait_ge(scattered, 16 * NB * k)
                rows = slots_in[0:routed * P].rearrange("(j u p) d -> p j u d", p=P, u=U)
                with sp.Fori(0, routed // U) as j:
                    for u in range(U):
                        sp.wait_ge(turned, j * U + (first + u + 1))
                        sp.dma_start(xg[u], rows[:, ds(j, 1), u]).then_inc(loaded[u], 16)

            @block.tensor
            def _(pe):
                pe.sem_inc(turned, U)
                pe.wait_ge(moe_loaded[layer - 1], 32)
                pe.wait_ge(ones_ready, 1)

                known = {}

                def expert(n):
                    if n.c not in known:
                        known[n.c] = pe.value_load(n.of(tile_expert), min_val=0, max_val=m["E"] - 1)
                    return known[n.c]

                def turn_x(n):
                    pe.wait_ge(loaded[n.c % U], n.count_dma())
                    for c in range(C):
                        last = nc.tensor.transpose(XT[n.c % 2][:, c * P:(c + 1) * P],
                                                   flat(xg[n.c % U])[:, c * P:(c + 1) * P], ident[:])
                    last.then_inc(turned, 1)

                def gate_up(n, e):
                    out = GU[n.c % 2][:, 0:2 * I]
                    pe.wait_ge(xT_ready, n.count())
                    for c in range(C):
                        last = nc.tensor.matmul(out, xT[:, n.c % 2, c, :], flat(gu_w[:, ds(e, 1), c, :]),
                                                start=(c == 0), stop=(c == C - 1 and layer != 2))
                    if layer == 2:
                        last = nc.tensor.matmul(out, ones3[:], flat(gb[:, ds(e, 1), :]), start=False, stop=True)
                    last.then_inc(gu_ready, 1)

                def turn_h(n):
                    pe.wait_ge(h_ready, n.count())
                    for i in range(parts):
                        last = nc.tensor.transpose(HT[n.c % 2][0:kp, i * P:(i + 1) * P],
                                                   h[:, n.c % 2, i * kp:(i + 1) * kp], ident[:])
                    last.then_inc(h_turned, 1)

                def down(n, e):
                    pe.wait_ge(hT_ready, n.count())
                    pe.wait_ge(y_copied, n.count())
                    for i in range(parts):
                        last = nc.tensor.matmul(Y[n.c % 2][:, 0:D], hT[:, n.c % 2, i, :],
                                                flat(dn_w[:, ds(e, 1), i, :]), start=(i == 0), stop=(i == parts - 1))
                    last.then_inc(y_ready, 1)

                def step(n):
                    if n.c % U == 0:
                        known.clear()
                    e = expert(n - 1) if (n - 1).there() else None
                    if n.there():
                        turn_x(n)
                    if (n - 1).there():
                        gate_up(n - 1, e)
                    if n.there() and n.c % U != U - 1:
                        expert(n)
                    e = expert(n - 3) if (n - 3).there() else None
                    if (n - 2).there():
                        turn_h(n - 2)
                    if (n - 3).there():
                        down(n - 3, e)
                each_step(pe, step)

            @block.scalar
            def _(act):
                out_rows = slots_out[0:total * P].rearrange("(t p) d -> p t d", p=P)

                def copy_x(n):
                    act.wait_ge(turned, n.count(U + 1))
                    nc.scalar.copy(flat(xT[:, n.c % 2]), XT[n.c % 2][:, 0:D]).then_inc(xT_ready, 1)

                def gate(n):
                    act.wait_ge(gu_ready, n.count())
                    nc.scalar.activation(h[:, n.c % 2, :], GU[n.c % 2][:, 0:I], func).then_inc(sg_ready, 1)

                def copy_h(n):
                    act.wait_ge(h_turned, n.count())
                    nc.scalar.copy(hT[:, n.c % 2].rearrange("p k t -> p (k t)"),
                                   HT[n.c % 2][0:kp, 0:parts * P]).then_inc(hT_ready, 1)

                def store_y(n):
                    act.wait_ge(y_copied, n.count(3))
                    act.dma_start(n.of(out_rows), y[:, n.c % U:n.c % U + 1, :]).then_inc(stored[n.c % U], 16)

                def step(n):
                    for part, n in ((copy_x, n), (gate, n - 1), (copy_h, n - 2), (store_y, n - 4)):
                        if n.there():
                            part(n)
                each_step(act, step)

            @block.vector
            def _(dve):
                nc.vector.memset(ones3[:], 1.0).then_inc(ones_ready, 1)
                dve.sem_inc(y_copied, 2)
                for i in range(U):
                    dve.sem_inc(stored[i], 16)

                def hidden(n):
                    dve.wait_ge(sg_ready, n.count())
                    nc.vector.tensor_tensor(h[:, n.c % 2, :], h[:, n.c % 2, :], GU[n.c % 2][:, I:2 * I],
                                            ALU.mult).then_inc(h_ready, 1)

                def copy_y(n):
                    dve.wait_ge(y_ready, n.count())
                    dve.wait_ge(stored[n.c % U], n.count_dma())
                    nc.vector.tensor_copy(y[:, n.c % U, :], Y[n.c % 2][:, 0:D]).then_inc(y_copied, 1)

                def step(n):
                    for part, n in ((hidden, n - 1), (copy_y, n - 3)):
                        if n.there():
                            part(n)
                each_step(dve, step)
                for i in range(U):
                    dve.wait_ge(stored[i], (total // U + 1) * 16)

    def combine(layer):
        k, shared, first, routed = shape_of(layer)
        n = k + shared
        sets = 4 if n <= 4 else 2
        room = NB // sets
        with ExitStack() as st:
            sem = lambda n: nc.alloc_semaphore(f"c{layer}_{n}")
            block = st.enter_context(nc.Block())
            own = sem("own")
            carve = carver(layer)
            hit = carve([P, NB, NE])
            if layer == 2:
                E = MOE[layer]["E"]
                cT = carve([E, 2, P])
                c_turned, cT_ready, b_ready, b_added = (sem(n) for n in ("ct", "cT", "b", "ba"))
                CT, BIAS = bank[4:6], bank[6:8]

                @block.tensor
                def _(pe):
                    def turn(t):
                        nc.tensor.transpose(CT[t % 2][0:E, 0:P], comb[:, t, 0:E], ident[:]).then_inc(c_turned, 1)

                    turn(0)
                    for t in range(NB):
                        if t + 1 < NB:
                            turn(t + 1)
                        pe.wait_ge(cT_ready, t + 1)
                        if t >= 2:
                            pe.wait_ge(b_added, t - 1)
                        nc.tensor.matmul(BIAS[t % 2][:, 0:D], cT[:, t % 2, :], small["l2_b2"][:], start=True,
                                         stop=True).then_inc(b_ready, 1)

                @block.scalar
                def _(act):
                    for t in range(NB):
                        act.wait_ge(c_turned, t + 1)
                        nc.scalar.copy(cT[:, t % 2, :], CT[t % 2][0:E, 0:P]).then_inc(cT_ready, 1)
            ready = [[sem(f"ready{i}_{j}") for j in range(n)] for i in range(sets)]
            added = sem("added")
            rows = slots_out[0:first * P].rearrange("(s j u p) d -> p s j u d", p=P, u=sets, s=shared)
            place = lambda t, i: t // 2 * 2 * n + 2 * i + t % 2 + 1

            if layer == 3:
                @block.scalar
                def _(act):
                    pairs = lambda a: a.rearrange("p (j u) d -> p j (u d)", u=2)
                    with act.Fori(0, NB // 2) as j:
                        act.wait_ge(added, j * (2 * n) + 2 * n)
                        act.dma_start(pairs(io["out"])[:, ds(j, 1)], pairs(x[:])[:, ds(j, 1)]).then_inc(out_stored, 16)
                    act.wait_ge(out_stored, 16 * NB // 2)

            @block.gpsimd
            def _(pool):
                for pair in range(0, NB, 2):
                    for i in range(k):
                        for t in (pair, pair + 1):
                            if t >= sets:
                                pool.wait_ge(added, place(t - sets, i))
                            pool.indirect_dma_start(
                                out=xn[:, t % sets * room + i, :], out_offset=None, in_=slots_out,
                                in_offset=bass.IndirectOffsetOnAxis(ap=row_out[:, t, i:i + 1], axis=0)
                                ).then_inc(ready[t % sets][i], 16)

            @block.sync
            def _(sp):
                for i in range(k, n):
                    for t in range(sets):
                        sp.dma_start(xn[:, t * room + i, :], rows[:, i - k, 0, t]).then_inc(ready[t][i], 16)
                with sp.Fori(0, NB // sets - 1) as j:
                    for pair in range(0, sets, 2):
                        for i in range(k, n):
                            for u in (pair, pair + 1):
                                sp.wait_ge(added, j * (sets * n) + place(u, i))
                                sp.dma_start(xn[:, u * room + i:u * room + i + 1, :],
                                             rows[:, i - k, 1:][:, ds(j, 1), u]).then_inc(ready[u][i], 16)

            @block.vector
            def _(dve):
                step = Chain(dve, own)
                for i in range(k):
                    step(nc.vector.tensor_tensor(hit, slot[:], best[:, :, i:i + 1].broadcast_to([P, NB, NE]),
                                                 ALU.is_equal))
                    step(nc.vector.tensor_tensor(hit, hit, comb[:, :, 0:NE], ALU.mult))
                    step(nc.vector.tensor_reduce(weight[:, :, i], hit, AX.X, ALU.add))
                with dve.Fori(0, NB // sets) as j:
                    tile = lambda a, u: flat(a.rearrange("p (j u) d -> p j u d", u=sets)[:, ds(j, 1), u])
                    for pair in range(0, sets, 2):
                        for u in (pair, pair + 1) if layer == 2 else ():
                            dve.wait_ge(b_ready, j * sets + (u + 1))
                            nc.vector.tensor_tensor(tile(x[:], u), tile(x[:], u), BIAS[u % 2][:, 0:D],
                                                    ALU.add).then_inc(b_added, 1)
                        if layer == 2:
                            dve.wait_ge(b_added, j * sets + (pair + 2))
                        for i in range(n):
                            for u in (pair, pair + 1):
                                w = weight[:, :, i:i + 1] if i < k else comb[:, :, NE + i - k:NE + i - k + 1]
                                dve.wait_ge(ready[u][i], j * 16 + 16)
                                if i:
                                    dve.wait_ge(added, j * (sets * n) + place(u, i - 1))
                                nc.vector.scalar_tensor_tensor(tile(x[:], u), xn[:, u * room + i, :], tile(w, u),
                                                               tile(x[:], u), ALU.mult, ALU.add).then_inc(added, 1)
                        for u in (pair, pair + 1) if layer < 3 else ():
                            dve.wait_ge(added, j * (sets * n) + place(u, n - 1))
                            nc.vector.bn_stats(tile(stats[:], u), tile(x[:], u))

    def mixture(layer):
        with nc.cleanup_on_exit():
            route(layer)
            slot_experts(layer)
            combine(layer)

    stages = [decay_attention, linear, masked_attention, lambda: mixture(1), many_heads, lambda: mixture(2),
              channel_heads, lambda: mixture(3)]
    setup()
    for stage in stages:
        stage()


def kernel(**inputs):
    import numpy as np
    import concourse.bacc as bacc
    from concourse.bass_utils import run_bass_kernel_spmd as run

    i = {k: np.asarray(v) for k, v in inputs.items()}

    def rows(a):
        return np.broadcast_to(a.reshape(1, -1), (P, a.size))

    def chunks(a):
        return a.reshape(C, P, -1).transpose(1, 0, 2)

    def gate_up(gate, up):
        gu = np.concatenate([gate, up], axis=2)
        return gu.reshape(gu.shape[0], C, P, -1).transpose(2, 0, 1, 3)

    def down(d, parts):
        return d.reshape(d.shape[0], parts, -1, D).transpose(2, 0, 1, 3)

    def join(*a):
        return np.concatenate(a, axis=0)

    tr = lambda a: a.transpose(0, 2, 1)
    cut = lambda a: a.reshape(D, 4, 176).transpose(1, 0, 2)
    Wkv = np.concatenate([i["L2_xattn_Wk"], i["L2_xattn_Wv"]], axis=0)
    arrays = {
        "x": i["x"].transpose(1, 0, 2), "ctx": i["ctx_2048"].transpose(1, 0, 2),
        "ctxT": i["ctx_2048"].reshape(NB, P, C, P).transpose(3, 0, 2, 1),
        "mask": np.broadcast_to(i["mask_BxS2_bk0"][None], (P, NB, P)),
        "g_xattn": rows(i["g_xattn"]), "g_ffn": rows(i["g_ffn"]), "decay": rows(i["L0_xattn_decay"]),
        "l0_win": chunks(i["L0_xattn_W_in"].T), "l0_bin": i["L0_xattn_b_in"].reshape(C, P).T,
        "l0_wout": chunks(i["L0_xattn_W_out"].T), "l0_bout": rows(i["L0_xattn_b_out"]),
        "l0_gamma": rows(i["L0_xattn_gamma"]), "l0_beta": rows(i["L0_xattn_beta"]),
        "l0_w": chunks(i["L0_ffn_weight"].T), "l0_scale": rows(i["L0_ffn_scale_weight"]),
        "l0_bias": rows(i["L0_ffn_bias"]),
        "l1_router": chunks(np.concatenate([i["L1_ffn_router_w"].T, i["L1_ffn_sh_gate_w"]], axis=1)),
        "l2_router": chunks(i["L2_ffn_wa"]), "l3_router": chunks(i["L3_ffn_gate_weight"].T),
        "l2_wq": chunks(i["L2_xattn_Wq"].T), "l2_wk": chunks(Wkv[0::2].T), "l2_wv": chunks(Wkv[1::2].T),
        "l2_b2": join(i["L2_ffn_rb2"], i["L2_ffn_sb2"]), "l3_gamma": rows(i["L3_xattn_gamma"]),
        "l3_ebias": rows(i["L3_ffn_expert_bias"]),
        "l2_gub": np.broadcast_to(np.concatenate([join(i["L2_ffn_rgb"], i["L2_ffn_sgb"]),
                                                  join(i["L2_ffn_rb1"], i["L2_ffn_sb1"])], axis=1).reshape(1, -1),
                                  (3, 18 * 256)),
        "l1_gu": gate_up(join(i["L1_ffn_w_gate"], cut(i["L1_ffn_sh_gate"])),
                         join(i["L1_ffn_w_up"], cut(i["L1_ffn_sh_up"]))),
        "l1_dn": down(join(i["L1_ffn_w_down"], i["L1_ffn_sh_down"].reshape(4, 176, D)), 2),
        "l2_gu": gate_up(join(i["L2_ffn_rg"], i["L2_ffn_sg"]), join(i["L2_ffn_rw1"], i["L2_ffn_sw1"])),
        "l2_dn": down(join(i["L2_ffn_rw2"], i["L2_ffn_sw2"]), 1),
        "l3_gu": gate_up(tr(join(i["L3_ffn_gate_proj"], i["L3_ffn_shared_gate"][None])),
                         tr(join(i["L3_ffn_up_proj"], i["L3_ffn_shared_up"][None]))),
        "l3_dn": down(tr(join(i["L3_ffn_down_proj"], i["L3_ffn_shared_down"][None])), 1),
    }
    arrays["pack"] = np.concatenate([arrays.pop(k).reshape(P, -1) for k, _ in PACKED], axis=1)
    nc = bacc.Bacc("TRN2", target_bir_lowering=False, num_devices=1)
    io, sent = {}, {}
    for name, a in arrays.items():
        a = np.ascontiguousarray(a)
        sent[f"in_{name}"] = a
        io[name] = nc.dram_tensor(f"in_{name}", a.shape, mybir.dt.from_np(a.dtype), kind="ExternalInput").ap()
    io["out"] = nc.dram_tensor("out_x", [P, NB, D], F32, kind="ExternalOutput").ap()
    io["slots_in"] = nc.dram_tensor("slots_in", [ROUTED * P, D], F32, kind="Internal").ap()
    io["slots_out"] = nc.dram_tensor("slots_out", [TILES * P, D], F32, kind="Internal").ap()
    build(nc, io)
    got = run(nc, [sent], core_ids=[0]).results[0]["out_x"]
    return got.transpose(1, 0, 2)
```
